# Optimizing a Trainium2 kernel written in Bass

```python
import numpy as np
import jax
import jax.numpy as jnp

def _softmax(x, axis=-1):
    return jax.nn.softmax(x, axis=axis)

def _gelu(x):
    return jax.nn.gelu(x, approximate=True)

def _silu(x):
    return jax.nn.silu(x)

def _sigmoid(x):
    return jax.nn.sigmoid(x)

def _layernorm(x, axis=-1, eps=1e-05):
    m = jnp.mean(x, axis=axis, keepdims=True)
    v = jnp.var(x, axis=axis, keepdims=True)
    return (x - m) / jnp.sqrt(v + eps)

def _scatter_add(tgt, idx, src, axis=0):
    return tgt.at[idx].add(src)

def _segment_sum(src, seg, n):
    return jax.ops.segment_sum(src, seg, n)
kernel_name = 'mk_gnn_resnorm_d4_gnn_r64_5759e9'

def setup_inputs(seed: int=0):
    np.random.seed(seed)
    _w = jnp.asarray

    def _rec_inputs():
        import jax
        import jax.numpy as jnp
        _gk = jax.random.key(seed)
        x = 8.953e-05 + 1 * jax.random.normal(jax.random.fold_in(_gk, 1), (100000, 32), jnp.float32)
        src = jax.random.randint(jax.random.fold_in(_gk, 2), (25000,), 0, 100000, jnp.int32)
        dst = jax.random.randint(jax.random.fold_in(_gk, 3), (25000,), 0, 100000, jnp.int32)
        _o = jnp.argsort(dst, stable=True)
        src = src[_o]
        dst = dst[_o]
        edge_attr3_2x32 = -8.16379e-05 + 0.999858 * jax.random.normal(jax.random.fold_in(_gk, 12), (25000, 2, 32), jnp.float32)
        edge_attr_3 = 0.000844983 + 0.999762 * jax.random.normal(jax.random.fold_in(_gk, 13), (25000, 3), jnp.float32)
        edge_attr_32 = 0.000196303 + 1.00016 * jax.random.normal(jax.random.fold_in(_gk, 14), (25000, 32), jnp.float32)
        edge_weight = jax.random.uniform(jax.random.fold_in(_gk, 16), (25000,), jnp.float32, 0.0, 1)
        return (x, src, dst, edge_attr3_2x32, edge_attr_3, edge_attr_32, edge_weight)
    x, src, dst, edge_attr3_2x32, edge_attr_3, edge_attr_32, edge_weight = _rec_inputs()

    def _L0_gnn_setup():
        import jax, jax.numpy as jnp
        import numpy as np
        from math import factorial, pi, sqrt
        MUL = 8
        RS = [(MUL, 0), (MUL, 1)]
        N_NODES = 20000
        N_EDGES = 10000
        FEAT_DIM = sum((m * (2 * l + 1) for m, l in RS))
        R_DIM = sum((mo * mi * (2 * min(lo, li) + 1) for mo, lo in RS for mi, li in RS))
        HIDDEN = 64

        def _cg(j1, j2, j3, m1, m2, m3):
            if m1 + m2 != m3:
                return 0.0
            f = factorial
            pre = sqrt((2 * j3 + 1) * f(j3 + j1 - j2) * f(j3 - j1 + j2) * f(j1 + j2 - j3) / f(j1 + j2 + j3 + 1))
            pre *= sqrt(f(j3 + m3) * f(j3 - m3) * f(j1 - m1) * f(j1 + m1) * f(j2 - m2) * f(j2 + m2))
            kmin = max(0, j2 - j3 - m1, j1 - j3 + m2)
            kmax = min(j1 + j2 - j3, j1 - m1, j2 + m2)
            s = 0.0
            for k in range(kmin, kmax + 1):
                s += (-1) ** k / (f(k) * f(j1 + j2 - j3 - k) * f(j1 - m1 - k) * f(j2 + m2 - k) * f(j3 - j2 + m1 + k) * f(j3 - j1 - m2 + k))
            return pre * s

        def _w3j_complex(l1, l2, l3):
            w = np.zeros((2 * l1 + 1, 2 * l2 + 1, 2 * l3 + 1))
            for m1 in range(-l1, l1 + 1):
                for m2 in range(-l2, l2 + 1):
                    m3 = -(m1 + m2)
                    if abs(m3) <= l3:
                        w[m1 + l1, m2 + l2, m3 + l3] = (-1) ** (l1 - l2 - m3) / sqrt(2 * l3 + 1) * _cg(l1, l2, l3, m1, m2, -m3)
            return w

        def _A(l):
            A = np.zeros((2 * l + 1, 2 * l + 1), dtype=complex)
            A[l, l] = 1.0
            for m in range(1, l + 1):
                A[l + m, l + m] = (-1) ** m / sqrt(2)
                A[l + m, l - m] = 1.0 / sqrt(2)
                A[l - m, l - m] = 1j / sqrt(2)
                A[l - m, l + m] = -1j * (-1) ** m / sqrt(2)
            return A

        def real_w3j(l1, l2, l3):
            wc = _w3j_complex(l1, l2, l3).astype(complex)
            wr = np.einsum('abc,ma,nb,oc->mno', wc, _A(l1).conj(), _A(l2).conj(), _A(l3).conj())
            i = int(np.argmax(np.abs(wr)))
            ph = wr.flat[i] / abs(wr.flat[i])
            wr = wr / ph
            assert np.abs(wr.imag).max() < 1e-10
            return np.real(wr).astype(np.float32)
        _W3J = {}
        for _mo, _lo in RS:
            for _mi, _li in RS:
                for _lf in range(abs(_lo - _li), _lo + _li + 1):
                    if (_lo, _lf, _li) not in _W3J:
                        _W3J[_lo, _lf, _li] = jnp.asarray(real_w3j(_lo, _lf, _li))
        _NORM = []
        for _mo, _lo in RS:
            _num = sum((mi * (2 * min(_lo, li) + 1) for mi, li in RS))
            _NORM.append(sqrt(4.0 * pi) * sqrt(2.0 * _lo + 1.0) / sqrt(_num))
        _F_OFFS = [0] + list(np.cumsum([mi * (2 * li + 1) for mi, li in RS]))

        def spherical_harmonics(rel_vec):
            r = rel_vec / jnp.linalg.norm(rel_vec, axis=-1, keepdims=True)
            x, y, z = (r[:, 0], r[:, 1], r[:, 2])
            y0 = jnp.full_like(x, 0.5 / sqrt(pi))[:, None]
            c1 = sqrt(3.0 / (4.0 * pi))
            y1 = c1 * jnp.stack([y, z, x], axis=-1)
            c2a = 0.5 * sqrt(15.0 / pi)
            c2b = 0.25 * sqrt(5.0 / pi)
            c2c = 0.25 * sqrt(15.0 / pi)
            y2 = jnp.stack([c2a * x * y, c2a * y * z, c2b * (3.0 * z * z - 1.0), c2a * x * z, c2c * (x * x - y * y)], axis=-1)
            return jnp.concatenate([y0, y1, y2], axis=-1)
        key = jax.random.key(seed)
        ks = jax.random.split(key, 6)
        features = jax.random.normal(ks[0], (N_NODES, FEAT_DIM), dtype=jnp.float32)
        abs_distances = jax.random.uniform(ks[1], (N_EDGES,), dtype=jnp.float32, minval=0.1, maxval=1.0)
        rel_vec = jax.random.normal(ks[2], (N_EDGES, 3), dtype=jnp.float32)
        edge_index = jax.random.randint(ks[3], (2, N_EDGES), 0, N_NODES, dtype=jnp.int32)
        w1 = jax.random.normal(ks[4], (1, HIDDEN), dtype=jnp.float32)
        b1 = jnp.zeros((HIDDEN,), jnp.float32)
        w2 = jax.random.normal(ks[5], (HIDDEN, R_DIM), dtype=jnp.float32) / sqrt(HIDDEN)
        b2 = jnp.zeros((R_DIM,), jnp.float32)
        return {'features': features, 'abs_distances': abs_distances, 'rel_vec': rel_vec, 'edge_index': edge_index, 'w1': w1, 'b1': b1, 'w2': w2, 'b2': b2}
    _L0_gnn_all = _L0_gnn_setup()
    _L0_gnn_in = {k: v for k, v in _L0_gnn_all.items() if k in ('w1', 'b1', 'w2', 'b2')}
    del _L0_gnn_all

    def _L1_gnn_setup():
        import jax, jax.numpy as jnp
        import numpy as np
        N_LAYERS = 3
        N_NODES = 500000
        N_EDGES = 2500000
        EMBED_DIM = 32
        key = jax.random.key(seed)
        k_w, k_e = jax.random.split(key)
        weight = jax.random.normal(k_w, (N_NODES, EMBED_DIM), dtype=jnp.float32) * 0.1
        edge_index = jax.random.randint(k_e, (2, N_EDGES), 0, N_NODES, dtype=jnp.int32)
        return {'weight': weight, 'edge_index': edge_index}
    _L1_gnn_all = _L1_gnn_setup()
    _L1_gnn_in = {k: v for k, v in _L1_gnn_all.items() if k in ()}
    del _L1_gnn_all

    def _L2_gnn_setup():
        import jax, jax.numpy as jnp
        import numpy as np
        N_NODES = 50000
        N_EDGES = 12500
        X_DIM = 32
        E_DIM = 32
        HID = 64
        OUT = 32
        key = jax.random.key(seed)
        ks = jax.random.split(key, 6)
        x = jax.random.normal(ks[0], (N_NODES, X_DIM), dtype=jnp.float32)
        edge_index = jax.random.randint(ks[1], (2, N_EDGES), 0, N_NODES, dtype=jnp.int64)
        edge_attr = jax.random.normal(ks[2], (N_EDGES, E_DIM), dtype=jnp.float32)
        in_dim = 2 * X_DIM + E_DIM
        W1 = jax.random.normal(ks[3], (in_dim, HID), dtype=jnp.float32) * (1.0 / np.sqrt(in_dim))
        b1 = jnp.zeros((HID,), dtype=jnp.float32)
        W2 = jax.random.normal(ks[4], (HID, OUT), dtype=jnp.float32) * (1.0 / np.sqrt(HID))
        b2 = jnp.zeros((OUT,), dtype=jnp.float32)
        return {'x': x, 'edge_index': edge_index, 'edge_attr': edge_attr, 'W1': W1, 'b1': b1, 'W2': W2, 'b2': b2}
    _L2_gnn_all = _L2_gnn_setup()
    _L2_gnn_in = {k: v for k, v in _L2_gnn_all.items() if k in ('W1', 'b1', 'W2', 'b2')}
    del _L2_gnn_all

    def _L3_gnn_setup():
        import jax, jax.numpy as jnp
        import numpy as np
        N = 50000
        E = 25000
        H = 2
        F = 32
        IN = 32
        OUT = 32
        NEG_SLOPE = 0.2
        key = jax.random.key(seed)
        ks = jax.random.split(key, 11)
        s = 0.1
        return {'feat': jax.random.normal(ks[0], (N, IN), jnp.float32), 'r_feat': jax.random.normal(ks[1], (E, H, F), jnp.float32), 'src': jax.random.randint(ks[2], (E,), 0, N), 'dst': jax.random.randint(ks[3], (E,), 0, N), 'W1': jax.random.normal(ks[4], (IN, OUT), jnp.float32) * s, 'b1': jnp.zeros((OUT,), jnp.float32), 'W2s': jax.random.normal(ks[5], (IN, H * F), jnp.float32) * s, 'b2s': jnp.zeros((H * F,), jnp.float32), 'W2d': jax.random.normal(ks[6], (IN, H * F), jnp.float32) * s, 'b2d': jnp.zeros((H * F,), jnp.float32), 'attn': jax.random.normal(ks[7], (1, H, F), jnp.float32) * s}
    _L3_gnn_all = _L3_gnn_setup()
    _L3_gnn_in = {k: v for k, v in _L3_gnn_all.items() if k in ('W1', 'b1', 'W2s', 'b2s', 'W2d', 'b2d', 'attn')}
    del _L3_gnn_all
    return {'x': x, 'src': src, 'dst': dst, 'edge_attr3_2x32': edge_attr3_2x32, 'edge_attr_3': edge_attr_3, 'edge_attr_32': edge_attr_32, 'edge_weight': edge_weight, 'L0_gnn_w1': _L0_gnn_in['w1'], 'L0_gnn_b1': _L0_gnn_in['b1'], 'L0_gnn_w2': _L0_gnn_in['w2'], 'L0_gnn_b2': _L0_gnn_in['b2'], 'L2_gnn_W1': _L2_gnn_in['W1'], 'L2_gnn_b1': _L2_gnn_in['b1'], 'L2_gnn_W2': _L2_gnn_in['W2'], 'L2_gnn_b2': _L2_gnn_in['b2'], 'L3_gnn_W1': _L3_gnn_in['W1'], 'L3_gnn_b1': _L3_gnn_in['b1'], 'L3_gnn_W2s': _L3_gnn_in['W2s'], 'L3_gnn_b2s': _L3_gnn_in['b2s'], 'L3_gnn_W2d': _L3_gnn_in['W2d'], 'L3_gnn_b2d': _L3_gnn_in['b2d'], 'L3_gnn_attn': _L3_gnn_in['attn']}

def reference(x, src, dst, edge_attr3_2x32, edge_attr_3, edge_attr_32, edge_weight, L0_gnn_w1, L0_gnn_b1, L0_gnn_w2, L0_gnn_b2, L2_gnn_W1, L2_gnn_b1, L2_gnn_W2, L2_gnn_b2, L3_gnn_W1, L3_gnn_b1, L3_gnn_W2s, L3_gnn_b2s, L3_gnn_W2d, L3_gnn_b2d, L3_gnn_attn):
    import jax
    import jax.numpy as jnp

    def _L0_gnn_ref(features, abs_distances, rel_vec, edge_index, w1, b1, w2, b2):
        import jax, jax.numpy as jnp
        import numpy as np
        from math import factorial, pi, sqrt
        MUL = 8
        RS = [(MUL, 0), (MUL, 1)]
        N_NODES = 20000
        N_EDGES = 10000
        FEAT_DIM = sum((m * (2 * l + 1) for m, l in RS))
        R_DIM = sum((mo * mi * (2 * min(lo, li) + 1) for mo, lo in RS for mi, li in RS))
        HIDDEN = 64

        def _cg(j1, j2, j3, m1, m2, m3):
            if m1 + m2 != m3:
                return 0.0
            f = factorial
            pre = sqrt((2 * j3 + 1) * f(j3 + j1 - j2) * f(j3 - j1 + j2) * f(j1 + j2 - j3) / f(j1 + j2 + j3 + 1))
            pre *= sqrt(f(j3 + m3) * f(j3 - m3) * f(j1 - m1) * f(j1 + m1) * f(j2 - m2) * f(j2 + m2))
            kmin = max(0, j2 - j3 - m1, j1 - j3 + m2)
            kmax = min(j1 + j2 - j3, j1 - m1, j2 + m2)
            s = 0.0
            for k in range(kmin, kmax + 1):
                s += (-1) ** k / (f(k) * f(j1 + j2 - j3 - k) * f(j1 - m1 - k) * f(j2 + m2 - k) * f(j3 - j2 + m1 + k) * f(j3 - j1 - m2 + k))
            return pre * s

        def _w3j_complex(l1, l2, l3):
            w = np.zeros((2 * l1 + 1, 2 * l2 + 1, 2 * l3 + 1))
            for m1 in range(-l1, l1 + 1):
                for m2 in range(-l2, l2 + 1):
                    m3 = -(m1 + m2)
                    if abs(m3) <= l3:
                        w[m1 + l1, m2 + l2, m3 + l3] = (-1) ** (l1 - l2 - m3) / sqrt(2 * l3 + 1) * _cg(l1, l2, l3, m1, m2, -m3)
            return w

        def _A(l):
            A = np.zeros((2 * l + 1, 2 * l + 1), dtype=complex)
            A[l, l] = 1.0
            for m in range(1, l + 1):
                A[l + m, l + m] = (-1) ** m / sqrt(2)
                A[l + m, l - m] = 1.0 / sqrt(2)
                A[l - m, l - m] = 1j / sqrt(2)
                A[l - m, l + m] = -1j * (-1) ** m / sqrt(2)
            return A

        def real_w3j(l1, l2, l3):
            wc = _w3j_complex(l1, l2, l3).astype(complex)
            wr = np.einsum('abc,ma,nb,oc->mno', wc, _A(l1).conj(), _A(l2).conj(), _A(l3).conj())
            i = int(np.argmax(np.abs(wr)))
            ph = wr.flat[i] / abs(wr.flat[i])
            wr = wr / ph
            assert np.abs(wr.imag).max() < 1e-10
            return np.real(wr).astype(np.float32)
        _W3J = {}
        for _mo, _lo in RS:
            for _mi, _li in RS:
                for _lf in range(abs(_lo - _li), _lo + _li + 1):
                    if (_lo, _lf, _li) not in _W3J:
                        _W3J[_lo, _lf, _li] = jnp.asarray(real_w3j(_lo, _lf, _li))
        _NORM = []
        for _mo, _lo in RS:
            _num = sum((mi * (2 * min(_lo, li) + 1) for mi, li in RS))
            _NORM.append(sqrt(4.0 * pi) * sqrt(2.0 * _lo + 1.0) / sqrt(_num))
        _F_OFFS = [0] + list(np.cumsum([mi * (2 * li + 1) for mi, li in RS]))

        def spherical_harmonics(rel_vec):
            r = rel_vec / jnp.linalg.norm(rel_vec, axis=-1, keepdims=True)
            x, y, z = (r[:, 0], r[:, 1], r[:, 2])
            y0 = jnp.full_like(x, 0.5 / sqrt(pi))[:, None]
            c1 = sqrt(3.0 / (4.0 * pi))
            y1 = c1 * jnp.stack([y, z, x], axis=-1)
            c2a = 0.5 * sqrt(15.0 / pi)
            c2b = 0.25 * sqrt(5.0 / pi)
            c2c = 0.25 * sqrt(15.0 / pi)
            y2 = jnp.stack([c2a * x * y, c2a * y * z, c2b * (3.0 * z * z - 1.0), c2a * x * z, c2c * (x * x - y * y)], axis=-1)
            return jnp.concatenate([y0, y1, y2], axis=-1)
        src, dst = (edge_index[0], edge_index[1])
        R = jax.nn.relu(abs_distances[:, None] @ w1 + b1) @ w2 + b2
        Y = spherical_harmonics(rel_vec)
        Fj = features[src]
        E = Fj.shape[0]
        msg_blocks = []
        r_off = 0
        for i, (mo, lo) in enumerate(RS):
            acc = jnp.zeros((E, mo, 2 * lo + 1), dtype=features.dtype)
            for j, (mi, li) in enumerate(RS):
                n_lf = 2 * min(lo, li) + 1
                sz = mo * mi * n_lf
                Rb = R[:, r_off:r_off + sz].reshape(E, mo, mi, n_lf)
                r_off += sz
                Fb = Fj[:, _F_OFFS[j]:_F_OFFS[j + 1]].reshape(E, mi, 2 * li + 1)
                for k, lf in enumerate(range(abs(lo - li), lo + li + 1)):
                    C = _W3J[lo, lf, li]
                    Yf = Y[:, lf * lf:(lf + 1) * (lf + 1)]
                    acc = acc + _NORM[i] * jnp.einsum('euv,ef,evi,ofi->euo', Rb[..., k], Yf, Fb, C)
            msg_blocks.append(acc.reshape(E, -1))
        msg = jnp.concatenate(msg_blocks, axis=-1)
        out = jnp.zeros((features.shape[0], msg.shape[1]), dtype=features.dtype)
        out = out.at[dst].add(msg)
        return out

    def _L1_gnn_ref(weight, edge_index):
        import jax, jax.numpy as jnp
        import numpy as np
        N_LAYERS = 3
        N_NODES = 500000
        N_EDGES = 2500000
        EMBED_DIM = 32
        src, dst = (edge_index[0], edge_index[1])
        n = weight.shape[0]
        deg = jax.ops.segment_sum(jnp.ones(src.shape, dtype=weight.dtype), dst, num_segments=n)
        deg_inv_sqrt = jnp.where(deg > 0, jax.lax.rsqrt(deg), jnp.zeros((), weight.dtype))
        norm = deg_inv_sqrt[src] * deg_inv_sqrt[dst]
        x = weight
        acc = weight
        for _ in range(N_LAYERS):
            msgs = norm[:, None] * x[src]
            x = jax.ops.segment_sum(msgs, dst, num_segments=n)
            acc = acc + x
        return acc / (N_LAYERS + 1)

    def _L2_gnn_ref(x, edge_index, edge_attr, W1, b1, W2, b2):
        import jax, jax.numpy as jnp
        import numpy as np
        N_NODES = 50000
        N_EDGES = 12500
        X_DIM = 32
        E_DIM = 32
        HID = 64
        OUT = 32
        num_nodes = x.shape[0]
        rol, col = (edge_index[0], edge_index[1])
        e_feat = jnp.concatenate([x[rol], x[col], edge_attr], axis=-1)
        h = jax.nn.relu(e_feat @ W1 + b1)
        v = h @ W2 + b2
        x_cand = jax.ops.segment_max(v, col, num_segments=num_nodes)
        return jnp.maximum(x_cand, x[:, -v.shape[-1]:])

    def _L3_gnn_ref(feat, r_feat, src, dst, W1, b1, W2s, b2s, W2d, b2d, attn):
        import jax, jax.numpy as jnp
        import numpy as np
        N = 50000
        E = 25000
        H = 2
        F = 32
        IN = 32
        OUT = 32
        NEG_SLOPE = 0.2
        n = feat.shape[0]
        feat_src = (feat @ W2s + b2s).reshape(n, H, F)
        feat_dst = (feat @ W2d + b2d).reshape(n, H, F)
        en = feat_src[src]
        ev = feat_dst[dst]
        e = jax.nn.leaky_relu(en + ev, negative_slope=NEG_SLOPE)
        e = jnp.sum(e * attn, axis=-1, keepdims=True)
        m = jax.ops.segment_max(e, dst, num_segments=n)
        m = jnp.where(jnp.isfinite(m), m, 0.0)
        ee = jnp.exp(e - m[dst])
        denom = jax.ops.segment_sum(ee, dst, num_segments=n)
        alpha = ee / jnp.maximum(denom[dst], 1e-09)
        msg = jax.nn.softmax(en * r_feat * alpha, axis=-1)
        g_agg = jax.ops.segment_sum(msg, dst, num_segments=n)
        g_sum = jnp.sum(g_agg, axis=1)
        rst = (feat + g_sum) @ W1 + b1
        return rst
    edge_index = jnp.stack([src, dst])
    x = _layernorm(x + _L0_gnn_ref(x, edge_weight, edge_attr_3, edge_index, L0_gnn_w1, L0_gnn_b1, L0_gnn_w2, L0_gnn_b2), axis=-1)
    x = _layernorm(x + _L1_gnn_ref(x, edge_index), axis=-1)
    x = _layernorm(x + _L2_gnn_ref(x, edge_index, edge_attr_32, L2_gnn_W1, L2_gnn_b1, L2_gnn_W2, L2_gnn_b2), axis=-1)
    x = _layernorm(x + _L3_gnn_ref(x, edge_attr3_2x32, src, dst, L3_gnn_W1, L3_gnn_b1, L3_gnn_W2s, L3_gnn_b2s, L3_gnn_W2d, L3_gnn_b2d, L3_gnn_attn), axis=-1)
    return x

_drawn_inputs = setup_inputs


def setup_inputs(seed=0):
    import zlib

    import numpy as np

    out = dict(_drawn_inputs(seed))
    spreads = {'L0_gnn_b1': (0.0, 0.276),
     'L0_gnn_b2': (0.0, 0.1),
     'L2_gnn_b1': (0.0, 0.635),
     'L2_gnn_b2': (0.0, 0.441),
     'L3_gnn_b1': (0.0, 0.1),
     'L3_gnn_b2s': (0.0, 2.0),
     'L3_gnn_b2d': (0.0, 2.0)}
    factors = {'edge_attr3_2x32': 7.103, 'L3_gnn_W2s': 7.04, 'L3_gnn_W2d': 61.465, 'L3_gnn_attn': 31.638}
    for name, (base, spread) in spreads.items():
        noise = np.random.default_rng([zlib.crc32(name.encode()), seed]).standard_normal(out[name].shape)
        drawn = base * np.exp(spread * noise) if base else spread * noise
        out[name] = jnp.asarray(drawn.astype(out[name].dtype))
    for name, factor in factors.items():
        out[name] = (out[name] * factor).astype(out[name].dtype)
    return out
```

```python
from contextlib import ExitStack
from math import pi, sqrt

import concourse.bass as bass
from concourse import mybir

N_NODES, FEAT = 100000, 32
N_EDGES = 25000
P = 128
T = -(-N_EDGES // P)
E_PAD = P * T
FULL = N_EDGES // T
REST = N_EDGES - FULL * T
LOG_LO = 7
HI = -(-(N_NODES >> LOG_LO) // 16) * 16
PAD_DST, PAD_NEXT = 131071, 131070
SKIP = 1 << 20
HID0, PATHS = 64, 384
HEADS, HF = 2, 64
EPS = 1e-5
BIG = 1e38
NEG_SLOPE = 0.2
SLOTS = 2

Y0, C1 = 0.5 / sqrt(pi), sqrt(3 / (4 * pi))
K1, K2 = C1 / sqrt(6), sqrt(3 / (8 * pi))
NORM0, NORM1 = sqrt(4 * pi) / sqrt(16), sqrt(4 * pi) * sqrt(3) / sqrt(32)

GATHER_CHUNK = 28
CHUNKS = T // GATHER_CHUNK
QUADS = T // 4

D_ROWS = 60
D_CHUNKS = N_NODES // (P * D_ROWS)
D_TAIL = N_NODES - D_CHUNKS * P * D_ROWS
TAIL_P, TAIL_ROWS = D_TAIL // 4, 4
NODE_STEPS = 11
N_WEIGHT_LOADS = 20
UNIT_ROWS = 12
D_UNITS = D_ROWS // UNIT_ROWS


def gnn_kernel(nc, x, src, dst, r_feat, rel, edge_attr, edge_weight, w1, b1, w2, b2,
               m_w1, m_b1, m_w2, m_b2, g_w1, g_b1, g_w2s, g_b2s, g_w2d, g_b2d, attn, out):
    f32, i32, f16 = mybir.dt.float32, mybir.dt.int32, mybir.dt.float16
    ALU, ACT, AX = mybir.AluOpType, mybir.ActivationFunctionType, mybir.AxisListType.X

    with ExitStack() as ctx:
        def sb(name, shape, dt=f32):
            return ctx.enter_context(nc.sbuf_tensor(name, shape, dt))

        def sem(name):
            return ctx.enter_context(nc.semaphore(name))

        def dram(name, shape, dt=f32):
            return nc.dram_tensor(name, shape, dt).ap()

        pos_table = dram("pos_table", (HI * P, 1), i32)
        tables = [dram(f"table_{k}", (E_PAD, FEAT)) for k in range(5)]

        A_dst = sb("A_dst", [P, T, FEAT])
        A_src = sb("A_src", [P, T, FEAT])
        A_msg = sb("A_msg", [P, T, FEAT])
        A_sum = sb("A_sum", [P, T, FEAT])
        A_tmp = sb("A_tmp", [P, T, FEAT])
        work = sb("work", [P, T, HF])
        work_flat = work[:].rearrange("p t f -> p (t f)")

        tmp_flat = A_tmp[:].rearrange("p t f -> p (t f)")

        def carver(of):
            at = [0]

            def carve(parts, *dims, dt=f32):
                n = 1
                for d in dims:
                    n *= d
                words = n if dt in (f32, i32) else n // 2
                view = of[0:parts, at[0]:at[0] + words]
                at[0] += words
                assert at[0] <= of.shape[1]
                if dt is not f32:
                    view = view.bitcast(dt)
                if len(dims) == 2:
                    view = view.rearrange("p (a b) -> p a b", b=dims[1])
                if len(dims) == 3:
                    view = view.rearrange("p (a b c) -> p a b c", b=dims[1], c=dims[2])
                return view
            return carve

        src_i = sb("src_i", [P, T], i32)
        dst_i = sb("dst_i", [P, T], i32)
        nxt_i = sb("nxt_i", [P, T], i32)
        pos_i = sb("pos_i", [P, T], i32)
        out_i = sb("out_i", [P, T], i32)
        ew = sb("ew", [P, T + 2])
        dst_f = sb("dst_f", [P, T])
        is_last = sb("is_last", [P, T])
        not_last = sb("not_last", [P, T])
        same = sb("same", [P, T])
        same_pen = sb("same_pen", [P, T])
        in_first = sb("in_first", [P, T])
        in_first_pen = sb("in_first_pen", [P, T])
        in_final = sb("in_final", [P, T])
        dinv = sb("dinv", [P, T])
        stat = sb("stat", [P, T])
        std = sb("std", [P, T])
        r3 = sb("r3", [P, T])
        small = sb("small", [P, 4, T])
        small2 = sb("small2", [P, 4, T])

        ident = sb("ident", [P, P])
        ones = sb("ones", [P, 32])
        eps_t = sb("eps_t", [P, 1])
        rows = sb("rows", [32, 8, P])
        diag = sb("diag", [P, P])
        seam_state = sb("seam_state", [32, P])
        seam_shift = sb("seam_shift", [32, P])
        ends_row = sb("ends_row", [32, P])
        carry = sb("carry", [P, 32])
        end_col = sb("end_col", [P, 32])

        w2fold = sb("w2fold", [HID0 + 1, PATHS])
        w1rep = sb("w1rep", [P, HID0 + 1])
        b1col = sb("b1col", [HID0 + 1, 1])
        mw1 = sb("mw1", [96, HID0])
        mb1 = sb("mb1", [HID0, 1])
        mw2 = sb("mw2", [HID0 + 1, FEAT])
        gw2 = sb("gw2", [HF + 1, 2 * HF])
        gtmp = sb("gtmp", [HF + 1, HF])
        attn_rep = sb("attn_rep", [P, HF])
        gw1 = sb("gw1", [P, P])
        gb1 = sb("gb1", [P, FEAT])
        gb1c = sb("gb1c", [P, FEAT])
        nodes_w = sb("nodes_w", [P, 2 * P])
        nodes_t = sb("nodes_t", [P, P])
        zero_hot = sb("zero_hot", [P, P], f16)

        banks = [ctx.enter_context(nc.psum_tensor(f"bank_{b}", [P, 512], f32)) for b in range(8)]

        loaded_dst, loaded_src, loaded_edges = sem("loaded_dst"), sem("loaded_src"), sem("loaded_edges")
        loaded_w, pads_ready = sem("loaded_w"), sem("pads_ready")
        pool_seq, consts_ready, dve_seq = sem("pool_seq"), sem("consts_ready"), sem("dve_seq")
        src_rows = [sem(f"src_rows_{c}") for c in range(CHUNKS)]
        dst_rows, pos_rows = sem("dst_rows"), sem("pos_rows")
        var_ready, std_ready = sem("var_ready"), sem("std_ready")
        centered, squared = sem("centered"), sem("squared")
        ends_ready, ends_turned = sem("ends_ready"), sem("ends_turned")
        carry_ready, carry_turned = sem("carry_ready"), sem("carry_turned")
        onehots_ready, onehots_used = sem("onehots_ready"), sem("onehots_used")
        hist_done, pos_f_ready = sem("hist_done"), sem("pos_f_ready")
        pos_turned, pos_int, pos_stored = sem("pos_turned"), sem("pos_int"), sem("pos_stored")
        weights_folded, weights_ready = sem("weights_folded"), sem("weights_ready")
        cw_done, cw_copied = sem("cw_done"), sem("cw_copied")
        pre_ready, pre_turned = sem("pre_ready"), sem("pre_turned")
        hid_ready, radial_ready, radial_used = sem("hid_ready"), sem("radial_ready"), sem("radial_used")
        table_ready, table_stored, rows_in = sem("table_ready"), sem("table_stored"), sem("rows_in")
        gather_ok = sem("gather_ok")
        n_loaded = [sem(f"n_loaded_{s}") for s in range(SLOTS)]
        n_turned, n_xt, n_mm = sem("n_turned"), sem("n_xt"), sem("n_mm")
        n_bank = sem("n_bank")
        n_var, n_std, n_z, n_zsq, n_out = sem("n_var"), sem("n_std"), sem("n_z"), sem("n_zsq"), sem("n_out")
        n_stored = [sem(f"n_stored_{s}") for s in range(SLOTS)]
        ea_in, tmp_free = sem("ea_in"), sem("tmp_free")
        e_cat, e_catd, e_turned, e_catT = sem("e_cat"), sem("e_catd"), sem("e_turned"), sem("e_catT")
        e_h, e_hT, e_v, e_vused = sem("e_h"), sem("e_hT"), sem("e_v"), sem("e_vused")
        a_cat, a_turned, a_catT, a_mm = sem("a_cat"), sem("a_turned"), sem("a_catT"), sem("a_mm")
        a_act, a_used = sem("a_act"), sem("a_used")
        rf_in = [sem(f"rf_in_{s}") for s in range(SLOTS)]
        exp_req, exp_done = sem("exp_req"), sem("exp_done")
        z_ready, z_turned, z_T, z_mm, z_used = sem("z_ready"), sem("z_turned"), sem("z_T"), sem("z_mm"), sem("z_used")
        prod_used, node_seq, a_weighed = sem("prod_used"), sem("node_seq"), sem("a_weighed")
        a_leaky = sem("a_leaky")
        final_ready, scattered = sem("final_ready"), sem("scattered")

        cv = carver(work_flat)
        hi_hot = cv(P, SLOTS, HI, dt=f16)
        lo_hot = cv(P, SLOTS * 2, P, dt=f16)
        iota16 = cv(P, HI, dt=f16)
        pos_f = cv(P, HI)
        pos_zero = cv(P, HI)
        pos_int_t = cv(P, 7, P, dt=i32)
        pre = cv(P, SLOTS, 2, HID0 + 1)
        hidT = cv(HID0 + 1, SLOTS, 2 * P)
        prod = cv(P, 2, 640)
        path_sums = cv(P, GATHER_CHUNK, 64)
        ff = cv(P, GATHER_CHUNK, 16)
        g5 = cv(P, GATHER_CHUNK, 8, 5)
        vec_a = cv(P, GATHER_CHUNK, 24)
        cv = carver(work_flat)
        n_x = cv(P, SLOTS, D_ROWS, FEAT)
        n_o = cv(P, SLOTS, D_ROWS, FEAT)
        n_q = cv(P, D_ROWS, FEAT)
        n_xT = cv(P, SLOTS, 3 * P)
        n_s = cv(P, 4, D_ROWS)
        cv = carver(tmp_flat)
        unit = cv(P, T, 5)
        w2raw = cv(HID0 + 1, PATHS)
        cv = carver(work_flat)
        cat = cv(P, SLOTS, 4, 96)
        catT = cv(96, SLOTS, 4 * P)
        hidT2 = cv(HID0 + 1, SLOTS, 4 * P)
        cv = carver(tmp_flat)
        cat3 = cv(P, SLOTS, 4, HF + 1)
        catT3 = cv(HF + 1, SLOTS, 4 * P)
        rf = cv(P, SLOTS, 4, HF)
        leaky = cv(P, SLOTS, 4, HF)
        z_in = cv(P, SLOTS, P)
        zT = cv(P, SLOTS, P)

        edge_no = small2[:, 0, :].bitcast(i32)

        def triple(ap):
            return ap.rearrange("p a t -> p (a t)").rearrange("p (t a) -> p t a", a=3)

        rel_t, rel_sq = triple(small[:, 0:3, :]), triple(small2[:, 1:4, :])

        def pair(ap):
            return ap.rearrange("p a t -> p (a t)").rearrange("p (t h) -> p t h", h=HEADS)

        pair_a, pair_b = pair(small[:, 0:2, :]), pair(small[:, 2:4, :])
        pair_c, pair_d = pair(small2[:, 0:2, :]), pair(small2[:, 2:4, :])

        def flat(ap):
            return ap.rearrange("p a b -> p (a b)")

        def bcast(ap, n):
            return ap.unsqueeze(len(ap.shape)).to_broadcast(list(ap.shape) + [n])

        def mid(ap, n):
            return ap.unsqueeze(1).to_broadcast([ap.shape[0], n, ap.shape[1]])

        main = "(p t) -> p t"
        main3 = "(p t) f -> p t f"

        def pipeline(eng, *steps):
            lag = len(steps) - 1

            def turn(i, parity):
                for k, step in enumerate(steps):
                    if step is None or isinstance(i, int) and not 0 <= i - k < QUADS:
                        continue
                    step(i - k, (parity - k) % SLOTS)

            start = lag + lag % 2
            pairs = (QUADS - start) // 2
            for i in range(start):
                turn(i, i % 2)
            with eng.Fori(0, pairs) as pair:
                turn(pair * 2 + start, 0)
                turn(pair * 2 + (start + 1), 1)
            for i in range(start + 2 * pairs, QUADS + lag):
                turn(i, i % 2)

        NODE_PAIRS = [(0, 2, False), (2, 4, False), (4, D_CHUNKS // 2, True)]
        assert D_CHUNKS % 2 == 1 and D_UNITS % 2 == 1

        def node_chunks(eng, body, first, last, tail):
            if first == 0:
                body(0, 0, 0, P, D_ROWS)
                body(1, 0, 1, P, D_ROWS)
                first = 1
            with eng.Fori(first, last) as i:
                body(i * 2, i, 0, P, D_ROWS)
                body(i * 2 + 1, i, 1, P, D_ROWS)
            if tail:
                body(D_CHUNKS - 1, D_CHUNKS // 2, 0, P, D_ROWS)
                body(D_CHUNKS, D_CHUNKS // 2, 1, TAIL_P, TAIL_ROWS)

        def node_rows(ap, c, parts):
            if parts == P:
                return ap[bass.ds(c * (P * D_ROWS), P * D_ROWS), :].rearrange("(p r) f -> p r f", p=P)
            return ap[D_CHUNKS * P * D_ROWS:N_NODES, :].rearrange("(p r) f -> p r f", p=parts)

        def node_units(slot, n_rows):
            if n_rows == TAIL_ROWS:
                return [(0, slot, TAIL_ROWS)]
            return [(j, (slot + j) % SLOTS, UNIT_ROWS) for j in range(D_UNITS)]

        block = ctx.enter_context(nc.Block())

        @block.sync
        def _(sp):
            sp.wait_ge(pads_ready, 1)
            for tile, ap, off, done in ((src_i, src, 0, loaded_src), (dst_i, dst, 0, loaded_dst),
                                        (nxt_i, dst, 1, loaded_dst)):
                n = REST - off
                sp.dma_start(tile[0:FULL, :], ap[off:off + FULL * T].rearrange(main, t=T)).then_inc(done, 16)
                sp.dma_start(tile[FULL:FULL + 1, 0:n],
                             ap[off + FULL * T:off + FULL * T + n].rearrange("(p t) -> p t", p=1)).then_inc(done, 16)
            sp.dma_start(ew[0:FULL, 0:T], edge_weight[0:FULL * T].rearrange(main, t=T)).then_inc(loaded_edges, 16)
            sp.dma_start(ew[FULL:FULL + 1, 0:REST],
                         edge_weight[FULL * T:N_EDGES].rearrange("(p t) -> p t", p=1)).then_inc(loaded_edges, 16)
            sp.dma_start(rel_t[0:FULL], rel[0:FULL * T, :].rearrange(main3, t=T)).then_inc(loaded_edges, 16)
            sp.dma_start(rel_t[FULL:FULL + 1, 0:REST],
                         rel[FULL * T:N_EDGES, :].rearrange("(p t) f -> p t f", p=1)).then_inc(loaded_edges, 16)
            row, col = "(a b) -> a b", "(a b) -> a b"
            for to, of in (
                (w2raw[0:HID0, :], w2), (w2raw[HID0:HID0 + 1, :], b2.rearrange(row, a=1)),
                (w1rep[:, 0:HID0], w1[0, :].partition_broadcast(P)), (b1col[0:HID0, :], b1.rearrange(col, b=1)),
                (mw1[:], m_w1), (mb1[:], m_b1.rearrange(col, b=1)),
                (mw2[0:HID0, :], m_w2), (mw2[HID0:HID0 + 1, :], m_b2.rearrange(row, a=1)),
                (gw2[0:32, 0:HF], g_w2s), (gw2[0:32, HF:2 * HF], g_w2s), (gw2[32:64, HF:2 * HF], g_w2d),
                (gw2[HF:HF + 1, 0:HF], g_b2s.rearrange(row, a=1)),
                (gw2[HF:HF + 1, HF:2 * HF], g_b2s.rearrange(row, a=1)),
                (gtmp[HF:HF + 1, :], g_b2d.rearrange(row, a=1)),
                (attn_rep[:], attn[0].rearrange("h f -> (h f)").partition_broadcast(P)),
                (gb1[:], g_b1.partition_broadcast(P)),
                *((gw1[32 * k:32 * k + 32, 32 * k:32 * k + 32], g_w1) for k in range(4)),
            ):
                sp.dma_start(to, of).then_inc(loaded_w, 16)

            sp.wait_ge(pos_int, 1)
            table = pos_table.rearrange("(h l) a -> h (l a)", l=P)
            whole = HI // P
            sp.dma_start(table[0:whole * P, :].rearrange("(k p) l -> p k l", p=P),
                         pos_int_t[:, 0:whole, :]).then_inc(pos_stored, 16)
            sp.dma_start(table[whole * P:HI, :], pos_int_t[0:HI - whole * P, whole, :]).then_inc(pos_stored, 16)

            def exchange(k, of):
                sp.wait_ge(table_ready, k + 1)
                sp.dma_start(tables[k].rearrange(main3, t=T), of[:]).then_inc(table_stored, 16)

            def load_nodes(c, half, slot, parts, n_rows):
                sp.wait_ge(n_turned, c * D_UNITS + D_UNITS)
                sp.dma_start(n_x[0:parts, slot, 0:n_rows, :], node_rows(x, c, parts)).then_inc(n_loaded[slot], 16)

            sp.wait_ge(pos_stored, 32)
            for k, (first, last, tail) in enumerate(NODE_PAIRS):
                exchange(k, A_tmp)
                node_chunks(sp, load_nodes, first, last, tail)
            exchange(3, A_dst)

            sp.wait_ge(tmp_free, 1)
            sp.dma_start(A_tmp[0:FULL], edge_attr[0:FULL * T, :].rearrange(main3, t=T)).then_inc(ea_in, 16)
            sp.dma_start(A_tmp[FULL:FULL + 1, 0:REST, :],
                         edge_attr[FULL * T:N_EDGES, :].rearrange("(p t) f -> p t f", p=1)).then_inc(ea_in, 16)
            exchange(4, A_dst)

            edges = r_feat.rearrange("e h f -> e (h f)")

            def load_rf(q, slot, rest_row):
                sp.wait_ge(a_used, q + 1)
                sp.dma_start(rf[0:FULL, slot], edges[0:FULL * T, :].rearrange("(p t) f -> p t f", t=T)
                             [:, bass.ds(q * 4, 4), :]).then_inc(rf_in[slot], 16)
                sp.dma_start(rf[FULL:P, slot], edges[bass.ds(rest_row, 4), :].rearrange("(p t) f -> p t f", p=1)
                             ).then_inc(rf_in[slot], 16)

            true_quads = REST // 4
            assert REST % 4 == 0 and true_quads % 2 == 1 and QUADS % 2 == 1
            with sp.Fori(0, true_quads // 2) as i:
                for slot in range(SLOTS):
                    load_rf(i * 2 + slot, slot, i * 8 + (FULL * T + 4 * slot))
            load_rf(true_quads - 1, 0, N_EDGES - 4)
            load_rf(true_quads, 1, 0)
            with sp.Fori((true_quads + 1) // 2, QUADS // 2) as i:
                for slot in range(SLOTS):
                    load_rf(i * 2 + slot, slot, 0)
            load_rf(QUADS - 1, 0, 0)
            sp.wait_ge(scattered, 16 * T)

        @block.gpsimd
        def _(pool):
            pool.memset(src_i[:], SKIP)
            pool.memset(dst_i[:], PAD_DST)
            pool.memset(nxt_i[:], PAD_NEXT)
            pool.memset(ew[:], 0.0)
            pool.memset(small[:], 1.0)
            pool.memset(w1rep[:], 0.0)
            pool.memset(b1col[:], 1.0)
            pool.memset(gw2[:], 0.0)
            pool.memset(gw1[:], 0.0)
            pool.memset(A_src[:], 0.0).then_inc(pads_ready, 1)
            pool.memset(pos_i[:], SKIP)
            pool.memset(ones[:], 1.0)
            pool.memset(eps_t[:], EPS)
            pool.memset(zero_hot[:], 0.0)
            pool.memset(ident[:], 0.0).then_inc(pool_seq, 1)
            pool.wait_ge(pool_seq, 1)
            pool.affine_select(out=ident[:], in_=ident[:], compare_op=ALU.not_equal, fill=1.0, base=0,
                               pattern=[[-1, P]], channel_multiplier=1)
            pool.iota(edge_no, pattern=[[1, T]], base=1, channel_multiplier=T)
            pool.iota(iota16, pattern=[[1, HI]], base=0, channel_multiplier=0,
                      allow_small_or_imprecise_dtypes=True).then_inc(consts_ready, 1)

            def gather(column, of, idx, limit, done):
                for t in range(T):
                    pool.indirect_dma_start(
                        out=column(t), out_offset=None, in_=of,
                        in_offset=bass.IndirectOffsetOnAxis(ap=idx[:, t:t + 1], axis=0),
                        bounds_check=limit, oob_is_err=False).then_inc(done(t), 16)

            pool.wait_ge(loaded_src, 32)
            pool.wait_ge(pads_ready, 1)
            gather(lambda t: A_src[:, t, :], x, src_i, N_NODES - 1, lambda t: src_rows[t // GATHER_CHUNK])
            pool.wait_ge(loaded_dst, 64)
            pool.wait_ge(gather_ok, 1)
            gather(lambda t: A_dst[:, t, :], x, dst_i, N_NODES - 1, lambda t: dst_rows)
            pool.wait_ge(pos_stored, 32)
            gather(lambda t: pos_i[:, t:t + 1], pos_table, src_i, N_NODES - 1, lambda t: pos_rows)
            pool.wait_ge(pos_rows, 16 * T)
            for k in range(5):
                pool.wait_ge(table_stored, 16 * (k + 1))
                pool.wait_ge(gather_ok, k + 2)
                to = A_msg if k < 3 else A_src
                gather(lambda t: to[:, t, :], tables[k], pos_i, E_PAD - 1, lambda t: rows_in)
                pool.wait_ge(rows_in, 16 * T * (k + 1))
            pool.wait_ge(final_ready, 1)
            for slot in range(SLOTS):
                pool.wait_ge(n_stored[slot], 16 * (D_CHUNKS // 2 + 1))
            for t in range(T):
                pool.indirect_dma_start(
                    out=out, out_offset=bass.IndirectOffsetOnAxis(ap=out_i[:, t:t + 1], axis=0),
                    in_=A_tmp[:, t, :], in_offset=None, bounds_check=N_NODES - 1,
                    oob_is_err=False).then_inc(scattered, 16)

        @block.scalar
        def _(act):
            done = {"root": 0, "square": 0}

            def next_root(scale, bias=True):
                done["root"] += 1
                act.wait_ge(var_ready, done["root"])
                nc.scalar.activation(std[:], stat[:], ACT.Sqrt, scale=scale,
                                     bias=eps_t[:] if bias else 0.0).then_inc(std_ready, 1)

            def next_square(of):
                done["square"] += 1
                act.wait_ge(centered, done["square"])
                nc.scalar.activation(A_sum[:], of[:], ACT.Square).then_inc(squared, 1)

            act.wait_ge(consts_ready, 1)
            next_root(1.0, bias=False)

            act.wait_ge(loaded_w, 16 * N_WEIGHT_LOADS)
            act.sem_inc(hid_ready, SLOTS)
            with act.Fori(0, T // 4) as i:
                for slot in range(SLOTS):
                    u = i * 2 + slot
                    act.wait_ge(pre_turned, u + (1 + SLOTS))
                    act.wait_ge(radial_ready, u + 1)
                    nc.scalar.activation(hidT[:, slot, :], banks[slot][0:HID0 + 1, 0:2 * P], ACT.Relu,
                                         bias=b1col[:]).then_inc(hid_ready, 1)

            next_square(A_src)
            next_root(1.0 / FEAT)
            next_root(1.5625)
            next_root(4.0)
            next_square(A_dst)
            next_root(1.0 / FEAT)
            next_root(1.0, bias=False)

            act.sem_inc(n_xt, SLOTS)
            act.sem_inc(n_bank, SLOTS)

            def nodes(c, half, slot, parts, n_rows):
                if not isinstance(half, int) or half:
                    act.wait_ge(n_stored[slot], half * 16)
                for j, s, nr in node_units(slot, n_rows):
                    u, n, width = c * D_UNITS + j, nr * FEAT, (nr // 4) * parts
                    act.wait_ge(n_turned, u + (1 + SLOTS * D_UNITS))
                    act.wait_ge(n_mm, u + 1)
                    nc.scalar.copy(n_xT[:, s, 0:width], banks[s][:, 0:width]).then_inc(n_xt, 1)
                    act.wait_ge(n_mm, u + (1 + SLOTS))
                    r = j * UNIT_ROWS
                    nc.scalar.activation(n_q[0:parts, r:r + nr, :].rearrange("p r f -> p (r f)"),
                                         banks[2 + s][0:parts, 0:n], ACT.Square)
                    nc.scalar.copy(n_o[0:parts, slot, r:r + nr, :].rearrange("p r f -> p (r f)"),
                                   banks[4 + s][0:parts, 0:n]).then_inc(n_bank, 1)
                var, dev = n_s[0:parts, 0, 0:n_rows], n_s[0:parts, 1, 0:n_rows]
                for k, scale in enumerate((1.0 / FEAT, 1.5625, 4.0)):
                    act.wait_ge(n_var, c * 4 + (k + 1))
                    nc.scalar.activation(dev, var, ACT.Sqrt, scale=scale, bias=eps_t[0:parts]).then_inc(n_std, 1)
                act.wait_ge(n_z, c + 1)
                nc.scalar.activation(n_q[0:parts, 0:n_rows, :], n_o[0:parts, slot, 0:n_rows, :],
                                     ACT.Square).then_inc(n_zsq, 1)
                act.wait_ge(n_var, c * 4 + 4)
                nc.scalar.activation(dev, var, ACT.Sqrt, scale=1.0 / FEAT, bias=eps_t[0:parts]).then_inc(n_std, 1)
                act.wait_ge(n_out, c + 1)
                act.dma_start(node_rows(out, c, parts), n_o[0:parts, slot, 0:n_rows, :]).then_inc(n_stored[slot], 16)

            for first, last, tail in NODE_PAIRS:
                node_chunks(act, nodes, first, last, tail)
            next_square(A_dst)
            next_root(1.0 / FEAT)

            for slot in range(SLOTS):
                act.wait_ge(n_stored[slot], 16 * (D_CHUNKS // 2 + 1))
            act.sem_inc(e_catT, SLOTS)
            act.sem_inc(e_hT, SLOTS)
            act.wait_ge(rows_in, 16 * T * 4)

            def bring_src(q, slot):
                act.wait_ge(e_turned, q + 1)
                nc.scalar.copy(cat[:, slot, :, 0:32], A_src[:, bass.ds(q * 4, 4), :]).then_inc(e_cat, 1)

            def copy_turned(q, slot):
                act.wait_ge(e_turned, q + (1 + SLOTS))
                act.wait_ge(e_h, q + 1)
                nc.scalar.copy(catT[:, slot, :], banks[slot][0:96, :]).then_inc(e_catT, 1)

            def hidden(q, slot):
                act.wait_ge(e_h, q + (1 + SLOTS))
                act.wait_ge(e_v, q + 1)
                nc.scalar.activation(hidT2[0:HID0, slot, :], banks[2 + slot][0:HID0, :], ACT.Relu,
                                     bias=mb1[:]).then_inc(e_hT, 1)

            pipeline(act, bring_src, copy_turned, hidden)
            next_square(A_dst)
            next_root(1.0 / FEAT)

            act.sem_inc(a_catT, SLOTS)
            act.sem_inc(a_act, SLOTS)

            def copy_turned3(q, slot):
                act.wait_ge(a_turned, q + (1 + SLOTS))
                act.wait_ge(a_mm, q + 1)
                nc.scalar.copy(catT3[:, slot, :], banks[slot][0:HF + 1, :]).then_inc(a_catT, 1)

            def slope(q, slot):
                act.wait_ge(a_mm, q + (1 + SLOTS))
                act.wait_ge(a_used, q + 1)
                nc.scalar.activation(leaky[:, slot], banks[2 + slot][:].rearrange("p (t g) -> p t g", t=4)
                                     [:, :, HF:2 * HF], ACT.Copy, scale=NEG_SLOPE).then_inc(a_act, 1)

            pipeline(act, None, copy_turned3, slope)
            act.wait_ge(exp_req, 1)
            nc.scalar.activation(small2[:, 0:2, :], small2[:, 0:2, :], ACT.Exp).then_inc(exp_done, 1)
            act.wait_ge(exp_req, 2)
            nc.scalar.activation(work[:], work[:], ACT.Exp).then_inc(exp_done, 1)

            act.sem_inc(z_T, SLOTS)

            def copy_sums(q, slot):
                act.wait_ge(z_turned, q + (1 + SLOTS))
                act.wait_ge(z_mm, q + 1)
                nc.scalar.copy(zT[:, slot, :], banks[slot][:, 0:P]).then_inc(z_T, 1)

            pipeline(act, copy_sums)
            next_square(A_tmp)
            next_root(1.0 / FEAT)

        @block.tensor
        def _(pe):
            def turn(out_ap, in_ap, n):
                return nc.tensor.transpose(out_ap, in_ap, ident[0:n, 0:n])

            seams = {"n": 0}

            def seam(width):
                seams["n"] += 1
                pe.wait_ge(ends_ready, 2 + seams["n"])
                turn(banks[6][0:width, 0:P], end_col[:, 0:width], P).then_inc(ends_turned, 1)
                pe.wait_ge(carry_ready, seams["n"])
                turn(banks[7][:, 0:width], seam_shift[0:width, :], width).then_inc(carry_turned, 1)

            pe.wait_ge(consts_ready, 1)
            for k in range(2):
                pe.wait_ge(ends_ready, k + 1)
                nc.tensor.matmul(banks[6 + k][0:32, 0:P], ones[:], diag[:], start=True, stop=True).then_inc(ends_turned, 1)

            for k in range(2):
                pe.wait_ge(weights_folded, k + 1)
                nc.tensor.matmul(banks[4 + k][:, 0:P], nodes_t[:], nodes_w[:, 0:P], start=True, stop=True).then_inc(cw_done, 1)

            half = HI // 2
            for h in range(2):
                nc.tensor.matmul(banks[2 + h][:, 0:half], zero_hot[:], iota16[:, 0:half], start=True, stop=False)
            pe.sem_inc(onehots_used, SLOTS)
            with pe.Fori(0, T // 2) as i:
                for slot in range(SLOTS):
                    pe.wait_ge(onehots_ready, i * 2 + (slot + 1))
                    for part in range(2):
                        for h in range(2):
                            last = nc.tensor.matmul(banks[2 + h][:, 0:half], lo_hot[:, slot * 2 + part, :],
                                                    hi_hot[:, slot, h * half:(h + 1) * half], start=False, stop=False)
                    last.then_inc(onehots_used, 1)
            for h in range(2):
                last = nc.tensor.matmul(banks[2 + h][:, 0:half], zero_hot[:], iota16[:, 0:half], start=False, stop=True)
            last.then_inc(hist_done, 1)
            pe.wait_ge(pos_f_ready, 1)
            for k in range(7):
                n = min(P, HI - k * P)
                last = turn(banks[4 + k // 4][0:n, (k % 4) * P:(k % 4 + 1) * P], pos_f[:, k * P:k * P + n], P)
            last.then_inc(pos_turned, 1)

            pe.sem_inc(pre_turned, SLOTS)
            pe.sem_inc(radial_ready, SLOTS)
            pe.wait_ge(pos_int, 1)
            with pe.Fori(0, T // 4) as i:
                for slot in range(SLOTS):
                    u = i * 2 + slot
                    pe.wait_ge(pre_ready, u + 1)
                    pe.wait_ge(hid_ready, u + 1)
                    for j in range(2):
                        last = turn(banks[slot][0:HID0 + 1, j * P:(j + 1) * P], pre[:, slot, j, :], P)
                    last.then_inc(pre_turned, 1)
                    pe.wait_ge(hid_ready, u + (1 + SLOTS))
                    pe.wait_ge(radial_used, u + 1)
                    for j in range(2):
                        last = nc.tensor.matmul(banks[2 + 2 * slot + j][:, 0:PATHS], hidT[:, slot, j * P:(j + 1) * P],
                                                w2fold[:], start=True, stop=True)
                    last.then_inc(radial_ready, 1)
            seam(32)
            seam(1)

            pe.sem_inc(n_mm, SLOTS)
            pe.sem_inc(n_turned, SLOTS * D_UNITS)

            def nodes(c, half, slot, parts, n_rows):
                pe.wait_ge(n_loaded[slot], half * 16 + 16)
                for j, s, nr in node_units(slot, n_rows):
                    u = c * D_UNITS + j
                    pe.wait_ge(n_xt, u + 1)
                    for k in range(nr // 4):
                        r = j * UNIT_ROWS + 4 * k
                        last = turn(banks[s][:, k * parts:(k + 1) * parts],
                                    n_x[0:parts, slot, r:r + 4, :].rearrange("p r f -> p (r f)"), parts)
                    last.then_inc(n_turned, 1)
                    pe.wait_ge(n_xt, u + (1 + SLOTS))
                    pe.wait_ge(n_bank, u + 1)
                    for k in range(nr // 4):
                        for w in range(2):
                            last = nc.tensor.matmul(banks[2 + 2 * w + s][0:parts, k * P:(k + 1) * P],
                                                    n_xT[:, s, k * parts:(k + 1) * parts],
                                                    nodes_w[:, w * P:(w + 1) * P], start=True, stop=True)
                    last.then_inc(n_mm, 1)

            for first, last_pair, tail in NODE_PAIRS:
                node_chunks(pe, nodes, first, last_pair, tail)
                seam(32)
            seam(32)

            pe.sem_inc(e_turned, SLOTS)
            pe.sem_inc(e_h, SLOTS)
            pe.sem_inc(e_v, SLOTS)

            def turn_cat(q, slot):
                pe.wait_ge(e_cat, q + 1)
                pe.wait_ge(e_catd, q + 1)
                pe.wait_ge(e_catT, q + 1)
                for j in range(4):
                    last = turn(banks[slot][0:96, j * P:(j + 1) * P], cat[:, slot, j, :], P)
                last.then_inc(e_turned, 1)

            def first_product(q, slot):
                pe.wait_ge(e_catT, q + (1 + SLOTS))
                pe.wait_ge(e_hT, q + 1)
                nc.tensor.matmul(banks[2 + slot][0:HID0, :], mw1[:], catT[:, slot, :],
                                 start=True, stop=True).then_inc(e_h, 1)

            def second_product(q, slot):
                pe.wait_ge(e_hT, q + (1 + SLOTS))
                pe.wait_ge(e_vused, q + 1)
                for j in range(4):
                    last = nc.tensor.matmul(banks[4 + slot][:, j * FEAT:(j + 1) * FEAT],
                                            hidT2[:, slot, j * P:(j + 1) * P], mw2[:], start=True, stop=True)
                last.then_inc(e_v, 1)

            pipeline(pe, turn_cat, first_product, second_product)
            seam(32)
            seam(32)

            pe.sem_inc(a_turned, SLOTS)
            pe.sem_inc(a_mm, SLOTS)

            def turn_cat3(q, slot):
                pe.wait_ge(a_cat, q + 1)
                pe.wait_ge(a_catT, q + 1)
                for j in range(4):
                    last = turn(banks[slot][0:HF + 1, j * P:(j + 1) * P], cat3[:, slot, j, :], P)
                last.then_inc(a_turned, 1)

            def project(q, slot):
                pe.wait_ge(a_catT, q + (1 + SLOTS))
                pe.wait_ge(a_act, q + 1)
                pe.wait_ge(a_used, q + 1)
                for j in range(4):
                    last = nc.tensor.matmul(banks[2 + slot][:, j * P:(j + 1) * P],
                                            catT3[:, slot, j * P:(j + 1) * P], gw2[:], start=True, stop=True)
                last.then_inc(a_mm, 1)

            pipeline(pe, turn_cat3, project)
            for _ in range(4):
                seam(2)
            seam(32)

            pe.sem_inc(z_turned, SLOTS)
            pe.sem_inc(z_mm, SLOTS)

            def turn_sums(q, slot):
                pe.wait_ge(z_ready, q + 1)
                pe.wait_ge(z_T, q + 1)
                turn(banks[slot][:, 0:P], z_in[:, slot, :], P).then_inc(z_turned, 1)

            def last_product(q, slot):
                pe.wait_ge(z_T, q + (1 + SLOTS))
                pe.wait_ge(z_used, q + 1)
                nc.tensor.matmul(banks[2 + slot][:, 0:P], zT[:, slot, :], gw1[:], start=True, stop=True).then_inc(z_mm, 1)

            pipeline(pe, turn_sums, last_product)

        @block.vector
        def _(v):
            count = {"seq": 0, "root": 0, "square": 0, "ends": 0, "turned": 0, "carry": 0}

            def step(ins):
                count["seq"] += 1
                ins.then_inc(dve_seq, 1)
                v.wait_ge(dve_seq, count["seq"])

            def done(ins, s, n):
                ins.then_inc(s, 1)
                v.wait_ge(s, n)

            def tt(o, a, b, op):
                return v.tensor_tensor(out=o, in0=a, in1=b, op=op)

            def ts(o, a, s1, op0, s2=None, op1=None):
                if op1 is None:
                    return v.tensor_scalar(o, a, s1, None, op0)
                return v.tensor_scalar(o, a, s1, s2, op0, op1)

            def stt(o, a, s, b, op0, op1):
                return v.scalar_tensor_tensor(out=o, in0=a, scalar=s, in1=b, op0=op0, op1=op1)

            def total(o, a, op=ALU.add):
                return v.tensor_reduce(out=o, in_=a, axis=AX, op=op)

            def root(ins):
                count["root"] += 1
                done(ins, var_ready, count["root"])
                v.wait_ge(std_ready, count["root"])
                step(v.reciprocal(std[:], std[:]))

            def norm(a):
                step(total(stat[:], a[:]))
                step(ts(stat[:], stat[:], -1.0 / FEAT, ALU.mult))
                count["square"] += 1
                done(tt(a[:], a[:], bcast(stat[:], FEAT), ALU.add), centered, count["square"])
                v.wait_ge(squared, count["square"])
                root(total(stat[:], A_sum[:]))
                return tt(a[:], a[:], bcast(std[:], FEAT), ALU.mult)

            def seam(to, width, state_row, carry_row, mask, op0, op1, first, back=False):
                e = 0 if back else T - 1
                count["ends"] += 1
                done(v.tensor_copy(end_col[:, 0:width], to[:, e, :]), ends_ready, count["ends"])
                v.wait_ge(ends_turned, count["ends"])
                w = slice(0, width)
                flip = slice(None, None, -1) if back else slice(None)
                step(v.tensor_tensor_scan(out=seam_state[w, flip], data0=rows[w, state_row, flip],
                                          data1=banks[6][w, 0:P][:, flip], initial=first, op0=op0, op1=op1))
                edge = P - 1 if back else 0
                step(v.memset(seam_shift[w, edge:edge + 1], first))
                count["carry"] += 1
                if back:
                    ins = tt(seam_shift[w, 0:P - 1], seam_state[w, 1:P], rows[w, carry_row, 0:P - 1], op0)
                else:
                    ins = tt(seam_shift[w, 1:P], seam_state[w, 0:P - 1], rows[w, carry_row, 1:P], op0)
                done(ins, carry_ready, count["carry"])
                v.wait_ge(carry_turned, count["carry"])
                step(v.tensor_copy(carry[:, w], banks[7][:, w]))
                for f in range(width):
                    last = stt(to[:, :, f], mask[:], carry[:, f:f + 1], to[:, :, f], op0, op1)
                return last

            def scan(to, of, mask, op0, op1, first, back=False):
                flip = slice(None, None, -1) if back else slice(None)
                for f in range(of.shape[2]):
                    last = v.tensor_tensor_scan(out=to[:, flip, f], data0=mask[:, flip], data1=of[:, flip, f],
                                                initial=first, op0=op0, op1=op1)
                return last

            def sums(to, of):
                step(scan(to, of, same, ALU.mult, ALU.add, 0.0))
                step(seam(to, of.shape[2], 0, 1, in_first, ALU.mult, ALU.add, 0.0))

            def maxima(to, of):
                step(scan(to, of, same_pen, ALU.add, ALU.max, -BIG))
                step(seam(to, of.shape[2], 2, 3, in_first_pen, ALU.add, ALU.max, -BIG))

            def spread(to, of, tmp):
                step(tt(tmp[:], of[:], bcast(is_last[:], of.shape[2]), ALU.mult))
                step(scan(to, tmp, not_last, ALU.mult, ALU.add, 0.0, back=True))
                step(seam(to, of.shape[2], 4, 5, in_final, ALU.mult, ALU.add, 0.0, back=True))

            v.memset(A_dst[:], 0.0).then_inc(gather_ok, 1)
            v.wait_ge(pads_ready, 1)
            v.wait_ge(consts_ready, 1)
            v.wait_ge(loaded_dst, 64)
            step(v.tensor_copy(dst_f[:], dst_i[:]))
            step(v.tensor_copy(stat[:], nxt_i[:]))
            step(tt(is_last[:], dst_f[:], stat[:], ALU.not_equal))
            step(ts(not_last[:], is_last[:], -1.0, ALU.mult, 1.0, ALU.add))
            step(v.memset(same[:, 0:1], 0.0))
            step(tt(same[:, 1:T], dst_f[:, 1:T], dst_f[:, 0:T - 1], ALU.is_equal))
            step(ts(same_pen[:], same[:], -1.0, ALU.add, BIG, ALU.mult))
            step(ts(in_first[:], dst_f[:], dst_f[:, 0:1], ALU.is_equal))
            step(ts(in_first_pen[:], in_first[:], -1.0, ALU.add, BIG, ALU.mult))
            step(ts(in_final[:], dst_f[:], dst_f[:, T - 1:T], ALU.is_equal))
            step(ts(stat[:], dst_f[:], float(-SKIP), ALU.add))
            step(tt(stat[:], stat[:], is_last[:], ALU.mult))
            step(ts(out_i[:], stat[:], float(SKIP), ALU.add))

            for k, e in enumerate((T - 1, 0)):
                count["ends"] += 1
                done(ts(diag[:], ident[:], dst_f[:, e:e + 1], ALU.mult), ends_ready, count["ends"])
                v.wait_ge(ends_turned, count["ends"])
                step(v.tensor_copy(rows[:, 6 + k, :], banks[6 + k][0:32, 0:P]))
            last_row, first_row = rows[:, 6, :], rows[:, 7, :]
            step(v.memset(rows[:, 0:6, :], 0.0))
            step(tt(rows[:, 0, 1:P], last_row[:, 0:P - 1], last_row[:, 1:P], ALU.is_equal))
            step(tt(rows[:, 1, 1:P], last_row[:, 0:P - 1], first_row[:, 1:P], ALU.is_equal))
            step(ts(rows[:, 2:4, :], rows[:, 0:2, :], -1.0, ALU.add, BIG, ALU.mult))
            step(tt(rows[:, 5, 0:P - 1], last_row[:, 0:P - 1], first_row[:, 1:P], ALU.is_equal))
            step(tt(rows[:, 4, :], last_row, first_row, ALU.is_equal))
            step(tt(rows[:, 4, :], rows[:, 4, :], rows[:, 5, :], ALU.mult))

            v.wait_ge(loaded_edges, 64)
            step(tt(rel_sq, rel_t, rel_t, ALU.mult))
            root(total(stat[:], rel_sq))
            for to, of in ((0, 1), (1, 2), (2, 0), (3, 1), (4, 2)):
                ins = tt(unit[:, :, to], rel_t[:, :, of], std[:], ALU.mult)
            step(ins)

            v.wait_ge(loaded_w, 16 * N_WEIGHT_LOADS)
            three = w2raw[:, 192:PATHS].rearrange("p (m k) -> p m k", k=3)
            fold = w2fold[:, 0:256].rearrange("p (j u t v) -> p j u t v", j=2, u=8, t=2)

            def uv(ap):
                return ap.rearrange("p (u v) -> p u v", u=8)

            ts(fold[:, 0, :, 0, :], uv(w2raw[:, 0:64]), NORM0 * Y0, ALU.mult)
            ts(fold[:, 0, :, 1, :], uv(w2raw[:, 64:128]), NORM0 * C1 / sqrt(3), ALU.mult)
            ts(fold[:, 1, :, 0, :], uv(w2raw[:, 128:192]), NORM1 * C1 / sqrt(3), ALU.mult)
            ts(fold[:, 1, :, 1, :], uv(three[:, :, 2]), NORM1 * K2, ALU.mult)
            ts(w2fold[:, 320:384], three[:, :, 1], NORM1 * K1, ALU.mult)
            step(ts(w2fold[:, 256:320], three[:, :, 2], -NORM1 * K2 / 3, ALU.mult))
            step(stt(w2fold[:, 256:320], three[:, :, 0], NORM1 * Y0 / sqrt(3), w2fold[:, 256:320], ALU.mult, ALU.add))
            step(tt(gw2[HF:HF + 1, HF:2 * HF], gw2[HF:HF + 1, HF:2 * HF], gtmp[HF:HF + 1, :], ALU.add))
            step(v.memset(nodes_t[:], 0.0))
            for k in range(4):
                q = slice(32 * k, 32 * k + 32)
                ins = v.memset(nodes_t[q, q], 1.0 / FEAT)
            step(ins)
            step(tt(nodes_w[:, 0:P], ident[:], nodes_t[:], ALU.subtract))
            done(tt(nodes_t[:], ident[:], gw1[:], ALU.add), weights_folded, 1)
            v.wait_ge(cw_done, 1)
            done(v.tensor_copy(nodes_t[:], banks[4][:, 0:P]), weights_folded, 2)
            v.wait_ge(cw_done, 2)
            step(v.tensor_copy(nodes_w[:, P:2 * P], banks[5][:, 0:P]))
            step(total(end_col[:, 0:1], gb1[:]))
            step(ts(end_col[:, 0:1], end_col[:, 0:1], -1.0 / FEAT, ALU.mult))
            step(ts(gb1c[:], gb1[:], end_col[:, 0:1], ALU.add))

            hi, lo, val_hi, val_lo = stat, std, r3, dinv
            step(ts(nxt_i[:], dst_i[:], LOG_LO, ALU.arith_shift_right))
            step(v.tensor_copy(hi[:], nxt_i[:]))
            step(ts(hi[:], hi[:], 1.0, ALU.add))
            step(tt(hi[:], hi[:], is_last[:], ALU.mult))
            step(ts(hi[:], hi[:], -1.0, ALU.add))
            step(ts(nxt_i[:], dst_i[:], P - 1, ALU.bitwise_and))
            step(v.tensor_copy(lo[:], nxt_i[:]))
            step(ts(nxt_i[:], edge_no, P - 1, ALU.bitwise_and))
            step(v.tensor_copy(val_lo[:], nxt_i[:]))
            step(ts(nxt_i[:], edge_no, LOG_LO, ALU.arith_shift_right))
            step(v.tensor_copy(val_hi[:], nxt_i[:]))
            step(ts(val_hi[:], val_hi[:], float(P), ALU.mult))
            with v.Fori(0, T // 2) as i:
                for slot in range(SLOTS):
                    t = i * 2 + slot
                    v.wait_ge(onehots_used, i * 2 + (slot + 1))
                    ts(hi_hot[:, slot, :], iota16, hi[:, bass.ds(t, 1)], ALU.is_equal)
                    ts(lo_hot[:, 2 * slot, :], iota16[:, 0:P], lo[:, bass.ds(t, 1)], ALU.is_equal,
                       val_hi[:, bass.ds(t, 1)], ALU.mult)
                    ts(lo_hot[:, 2 * slot + 1, :], iota16[:, 0:P], lo[:, bass.ds(t, 1)], ALU.is_equal,
                       val_lo[:, bass.ds(t, 1)], ALU.mult).then_inc(onehots_ready, 1)
            v.wait_ge(hist_done, 1)
            hist = [banks[2 + h][:, 0:HI // 2] for h in range(2)]
            for h in range(2):
                at = slice(h * HI // 2, (h + 1) * HI // 2)
                step(ts(pos_zero[:, at], hist[h], 0.0, ALU.is_equal, float(SKIP), ALU.mult))
                ins = stt(pos_f[:, at], hist[h], -1.0, pos_zero[:, at], ALU.add, ALU.add)
            done(ins, pos_f_ready, 1)
            v.wait_ge(pos_turned, 1)
            v.tensor_copy(pos_int_t[:, 0:4, :].rearrange("p k l -> p (k l)"), banks[4][:, :])
            v.tensor_copy(pos_int_t[:, 4:6, :].rearrange("p k l -> p (k l)"), banks[5][:, 0:2 * P])
            done(v.tensor_copy(pos_int_t[0:HI - 6 * P, 6, :], banks[5][0:HI - 6 * P, 2 * P:3 * P]), pos_int, 1)

            def pre_activation(u_next, slot, t):
                v.wait_ge(pre_turned, u_next + 1)
                tt(pre[:, slot], mid(w1rep[:], 2), bcast(ew[:, bass.ds(t, 2)], HID0 + 1), ALU.mult).then_inc(pre_ready, 1)

            pre_activation(0, 0, 0)
            v.sem_inc(radial_used, SLOTS)
            for c in range(CHUNKS):
                v.wait_ge(src_rows[c], 16 * GATHER_CHUNK)
                cols = slice(c * GATHER_CHUNK, (c + 1) * GATHER_CHUNK)
                vec_in = A_src[:, cols, 8:32].rearrange("p t (v i) -> p t v i", i=3)
                n3 = unit[:, cols, 0:3].unsqueeze(2).to_broadcast([P, GATHER_CHUNK, 8, 3])
                a4 = vec_a.rearrange("p t (v i) -> p t v i", i=3)
                step(tt(a4, vec_in, n3, ALU.mult))
                v.tensor_copy(ff[:, :, 0:8], A_src[:, cols, 0:8])
                step(total(ff[:, :, 8:16], a4))
                with v.Fori(0, GATHER_CHUNK // 4) as i:
                    for slot in range(SLOTS):
                        u = i * 2 + (c * GATHER_CHUNK // 2 + slot)
                        t_in, t = i * 4 + 2 * slot, i * 4 + (c * GATHER_CHUNK + 2 * slot)
                        pre_activation(u + 1, 1 - slot, t + 2)
                        v.wait_ge(radial_ready, u + (1 + SLOTS))
                        for j in range(2):
                            bank = banks[2 + 2 * slot + j]
                            tt(prod[:, j, 0:256].rearrange("p (a b) -> p a b", b=16),
                               bank[:, 0:256].rearrange("p (a b) -> p a b", b=16),
                               ff[:, bass.ds(t_in + j, 1), :].to_broadcast([P, 16, 16]), ALU.mult)
                            vec = A_src[:, bass.ds(t + j, 1), 8:32].rearrange("p a (v i) -> p (a i) v", i=3)
                            last = tt(prod[:, j, 256:640].rearrange("p (a i v) -> p a i v", i=3, v=8),
                                      bank[:, 256:384].rearrange("p (a v) -> p a v", v=8).unsqueeze(2)
                                      .to_broadcast([P, 16, 3, 8]),
                                      vec.unsqueeze(1).to_broadcast([P, 16, 3, 8]), ALU.mult)
                        done(last, radial_used, u + (1 + SLOTS))
                        total(path_sums[:, bass.ds(t_in, 2), 0:16],
                              prod[:, :, 0:256].rearrange("p j (a b) -> p j a b", b=16))
                        total(path_sums[:, bass.ds(t_in, 2), 16:64],
                              prod[:, :, 256:640].rearrange("p j (a b) -> p j a b", b=8)).then_inc(prod_used, 1)
                        v.wait_ge(prod_used, u + 1)
                beta = path_sums[:, :, 16:40].rearrange("p t (u i) -> p t u i", i=3)
                gamma = path_sums[:, :, 40:64].rearrange("p t (u i) -> p t u i", i=3)

                def n_at(k):
                    return unit[:, cols, k:k + 3].unsqueeze(2).to_broadcast([P, GATHER_CHUNK, 8, 3])

                vec_out = A_msg[:, cols, 8:32].rearrange("p t (u i) -> p t u i", i=3)
                v.tensor_copy(A_msg[:, cols, 0:8], path_sums[:, :, 0:8])
                v.tensor_copy(g5[:, :, :, 0:3], gamma)
                step(v.tensor_copy(g5[:, :, :, 3:5], gamma[:, :, :, 0:2]))
                step(tt(a4, n_at(1), g5[:, :, :, 2:5], ALU.mult))
                step(tt(vec_out, beta, a4, ALU.add))
                step(tt(a4, n_at(2), g5[:, :, :, 1:4], ALU.mult))
                step(tt(vec_out, vec_out, a4, ALU.subtract))
                step(tt(a4, n_at(0), bcast(path_sums[:, :, 8:16], 3), ALU.mult))
                step(tt(vec_out, vec_out, a4, ALU.add))

            step(total(stat[:], A_src[:]))
            step(ts(stat[:], stat[:], -1.0 / FEAT, ALU.mult))
            count["square"] += 1
            done(tt(A_src[:], A_src[:], bcast(stat[:], FEAT), ALU.add), centered, count["square"])
            v.wait_ge(squared, count["square"])
            root(total(stat[:], A_sum[:]))
            r1 = small[:, 0, :]
            step(v.tensor_copy(r1, std[:]))
            step(tt(stat[:], stat[:], std[:], ALU.mult))
            root(stt(stat[:], stat[:], 1.0 / FEAT, std[:], ALU.mult, ALU.mult))
            step(ts(std[:], std[:], 1.25, ALU.mult))
            step(tt(r1, r1, std[:], ALU.mult))
            step(tt(stat[:], stat[:], std[:], ALU.mult))
            root(tt(stat[:], stat[:], std[:], ALU.mult))
            step(ts(r3[:], std[:], 2.0, ALU.mult))
            step(tt(A_src[:], A_src[:], bcast(r1, FEAT), ALU.mult))

            sums(A_sum, A_msg)
            v.memset(A_msg[:], 0.0).then_inc(gather_ok, 1)
            v.wait_ge(dst_rows, 16 * T)
            step(tt(A_dst[:], A_dst[:], A_sum[:], ALU.add))
            step(norm(A_dst))

            deg = stat[:].unsqueeze(2)
            step(v.memset(small[:, 0, :], 1.0))
            step(scan(deg, small[:, 0, :].unsqueeze(2), same, ALU.mult, ALU.add, 0.0))
            root(seam(deg, 1, 0, 1, in_first, ALU.mult, ALU.add, 0.0))
            step(v.tensor_copy(dinv[:], std[:]))
            done(tt(A_tmp[:], A_dst[:], bcast(dinv[:], FEAT), ALU.mult), table_ready, 1)
            step(ts(A_dst[:], A_dst[:], 1.25, ALU.mult))

            def nodes(c, half, slot, parts, n_rows):
                n_unit = len(node_units(slot, n_rows))

                def s(k):
                    return n_s[0:parts, k, 0:n_rows]

                o, q = n_o[0:parts, slot, 0:n_rows, :], n_q[0:parts, 0:n_rows, :]
                var, dev, r, tmp = s(0), s(1), s(2), s(3)

                def nroot(k, ins):
                    done(ins, n_var, c * 4 + k)
                    v.wait_ge(n_std, c * 4 + k)
                    nstep(v.reciprocal(tmp, dev))

                n_in = [0]

                def nstep(ins):
                    n_in[0] += 1
                    ins.then_inc(node_seq, 1)
                    v.wait_ge(node_seq, c * NODE_STEPS + n_in[0])

                v.wait_ge(n_bank, c * D_UNITS + (n_unit + SLOTS))
                nroot(1, total(var, q))
                nstep(v.tensor_copy(r, tmp))
                nstep(tt(var, var, tmp, ALU.mult))
                nroot(2, stt(var, var, 1.0 / FEAT, tmp, ALU.mult, ALU.mult))
                nstep(ts(tmp, tmp, 1.25, ALU.mult))
                nstep(tt(r, r, tmp, ALU.mult))
                nstep(tt(var, var, tmp, ALU.mult))
                nroot(3, tt(var, var, tmp, ALU.mult))
                nstep(stt(r, tmp, 2.0, r, ALU.mult, ALU.mult))
                nstep(tt(o, o, bcast(r, FEAT), ALU.mult))
                done(tt(o, o, mid(gb1c[0:parts], n_rows), ALU.add), n_z, c + 1)
                v.wait_ge(n_zsq, c + 1)
                nroot(4, total(var, q))
                assert n_in[0] == NODE_STEPS
                done(tt(o, o, bcast(tmp, FEAT), ALU.mult), n_out, c + 1)

            for k, (first, last_pair, tail) in enumerate(NODE_PAIRS):
                node_chunks(v, nodes, first, last_pair, tail)
                v.wait_ge(rows_in, 16 * T * (k + 1))
                done(scan(A_sum, A_msg, same, ALU.mult, ALU.add, 0.0), gather_ok, k + 3)
                step(seam(A_sum, FEAT, 0, 1, in_first, ALU.mult, ALU.add, 0.0))
                step(tt(A_sum[:], A_sum[:], bcast(dinv[:], FEAT), ALU.mult))
                if k < 2:
                    done(tt(A_tmp[:], A_sum[:], bcast(dinv[:], FEAT), ALU.mult), table_ready, k + 2)
                step(stt(A_dst[:], A_sum[:], 0.25, A_dst[:], ALU.mult, ALU.add))
            v.sem_inc(tmp_free, 1)
            done(norm(A_dst), table_ready, 4)


            spread(A_sum, A_dst, A_msg)
            v.wait_ge(ea_in, 32)
            for slot in range(SLOTS):
                v.wait_ge(n_stored[slot], 16 * (D_CHUNKS // 2 + 1))
            step(v.memset(hidT2[HID0:HID0 + 1], 1.0))
            v.sem_inc(e_vused, SLOTS)

            def quad(a, q):
                return a[:, bass.ds(q * 4, 4), :]

            def bring_dst(q, slot):
                v.wait_ge(e_turned, q + 1)
                v.tensor_copy(cat[:, slot, :, 32:64], quad(A_sum, q))
                v.tensor_copy(cat[:, slot, :, 64:96], quad(A_tmp, q)).then_inc(e_catd, 1)

            def take(q, slot):
                v.wait_ge(e_v, q + (1 + SLOTS))
                v.tensor_copy(quad(A_msg, q), banks[4 + slot][:, 0:P].rearrange("p (t f) -> p t f", f=FEAT)
                              ).then_inc(e_vused, 1)

            pipeline(v, bring_dst, None, None, take)
            v.wait_ge(e_vused, QUADS + SLOTS)
            maxima(A_sum, A_msg)
            step(tt(A_msg[:], A_sum[:], A_dst[:], ALU.max))
            v.wait_ge(table_stored, 16 * 4)
            step(tt(A_dst[:], A_dst[:], A_msg[:], ALU.add))
            done(norm(A_dst), table_ready, 5)
            done(tt(A_src[:], A_src[:], bcast(r3[:], FEAT), ALU.mult), gather_ok, 6)

            spread(A_sum, A_dst, A_msg)
            step(v.memset(cat3[:, :, :, HF:HF + 1], 1.0))
            v.wait_ge(rows_in, 16 * T * 5)
            v.sem_inc(a_used, SLOTS)

            def bring_both(q, slot):
                v.wait_ge(a_turned, q + 1)
                v.tensor_copy(cat3[:, slot, :, 0:32], quad(A_src, q))
                v.tensor_copy(cat3[:, slot, :, 32:64], quad(A_sum, q)).then_inc(a_cat, 1)

            def score(q, slot):
                v.wait_ge(a_act, q + (1 + SLOTS))
                v.wait_ge(rf_in[slot], q * 16 + (32 - 16 * slot))
                tt(quad(work, q), banks[2 + slot][:].rearrange("p (t g) -> p t g", t=4)[:, :, 0:HF],
                   rf[:, slot], ALU.mult)
                done(tt(leaky[:, slot], banks[2 + slot][:].rearrange("p (t g) -> p t g", t=4)[:, :, HF:2 * HF],
                        leaky[:, slot], ALU.max), a_leaky, q + 1)
                done(tt(leaky[:, slot], leaky[:, slot], mid(attn_rep[:], 4), ALU.mult), a_weighed, q + 1)
                total(quad(pair_a, q), leaky[:, slot].rearrange("p t (h f) -> p t h f", h=HEADS)).then_inc(a_used, 1)

            pipeline(v, bring_both, None, score)
            v.wait_ge(a_used, QUADS + SLOTS)

            maxima(pair_b, pair_a)
            spread(pair_c, pair_b, pair_d)
            done(tt(pair_c, pair_a, pair_c, ALU.subtract), exp_req, 1)
            v.wait_ge(exp_done, 1)
            sums(pair_b, pair_c)
            spread(pair_a, pair_b, pair_d)
            step(ts(pair_a, pair_a, 1e-9, ALU.max))
            step(v.reciprocal(pair_a, pair_a))
            step(tt(pair_c, pair_c, pair_a, ALU.mult))

            w3 = work_flat.rearrange("p (r f) -> p r f", f=FEAT)
            step(tt(w3, w3, bcast(flat(pair_c), FEAT), ALU.mult))
            step(total(flat(pair_b), w3, ALU.max))
            done(tt(w3, w3, bcast(flat(pair_b), FEAT), ALU.subtract), exp_req, 2)
            v.wait_ge(exp_done, 2)
            step(total(flat(pair_b), w3))
            step(v.reciprocal(pair_b, pair_b))
            step(tt(w3, w3, bcast(flat(pair_b), FEAT), ALU.mult))
            step(tt(A_msg[:], work[:, :, 0:FEAT], work[:, :, FEAT:HF], ALU.add))
            sums(A_sum, A_msg)
            step(tt(A_sum[:], A_sum[:], A_dst[:], ALU.add))

            v.sem_inc(z_used, SLOTS)

            def bring_sum(q, slot):
                v.wait_ge(z_turned, q + 1)
                v.tensor_copy(z_in[:, slot, :], quad(A_sum, q).rearrange("p t f -> p (t f)")).then_inc(z_ready, 1)

            def finish(q, slot):
                v.wait_ge(z_mm, q + (1 + SLOTS))
                tt(quad(A_msg, q), banks[2 + slot][:, 0:P].rearrange("p (t f) -> p t f", f=FEAT),
                   mid(gb1[:], 4), ALU.add).then_inc(z_used, 1)

            pipeline(v, bring_sum, None, finish)
            v.wait_ge(z_used, QUADS + SLOTS)
            step(tt(A_tmp[:], A_msg[:], A_dst[:], ALU.add))
            norm(A_tmp).then_inc(final_ready, 1)


_INPUTS = ["x", "src", "dst", "edge_attr3_2x32", "edge_attr_3", "edge_attr_32", "edge_weight",
           "L0_gnn_w1", "L0_gnn_b1", "L0_gnn_w2", "L0_gnn_b2", "L2_gnn_W1", "L2_gnn_b1", "L2_gnn_W2", "L2_gnn_b2",
           "L3_gnn_W1", "L3_gnn_b1", "L3_gnn_W2s", "L3_gnn_b2s", "L3_gnn_W2d", "L3_gnn_b2d", "L3_gnn_attn"]


def kernel(**inputs):
    import numpy as np
    import concourse.bacc as bacc
    from concourse.bass_utils import run_bass_kernel_spmd

    nc = bacc.Bacc("TRN2", target_bir_lowering=False, num_devices=1)
    arrays, args = {}, []
    for name in _INPUTS:
        a = np.ascontiguousarray(inputs[name])
        arrays[f"in_{name}"] = a
        args.append(nc.dram_tensor(f"in_{name}", a.shape, mybir.dt.from_np(a.dtype), kind="ExternalInput").ap())
    out = nc.dram_tensor("out_0", (N_NODES, FEAT), mybir.dt.float32, kind="ExternalOutput").ap()
    gnn_kernel(nc, *args, out)
    return run_bass_kernel_spmd(nc, [arrays], core_ids=[0]).results[0]["out_0"]
```

```python
from contextlib import ExitStack
from math import pi, sqrt

import concourse.bass as bass
from concourse import mybir

N_NODES, FEAT = 100000, 32
N_EDGES = 25000
P = 128
T = -(-N_EDGES // P)
E_PAD = P * T
FULL = N_EDGES // T
REST = N_EDGES - FULL * T
LOG_LO = 7
HI = -(-(N_NODES >> LOG_LO) // 16) * 16
PAD_DST, PAD_NEXT = 131071, 131070
SKIP = 1 << 20
HID0, PATHS = 64, 384
HEADS, HF = 2, 64
EPS = 1e-5
BIG = 1e38
NEG_SLOPE = 0.2
SLOTS = 2

Y0, C1 = 0.5 / sqrt(pi), sqrt(3 / (4 * pi))
K1, K2 = C1 / sqrt(6), sqrt(3 / (8 * pi))
NORM0, NORM1 = sqrt(4 * pi) / sqrt(16), sqrt(4 * pi) * sqrt(3) / sqrt(32)

GATHER_CHUNK = 28
CHUNKS = T // GATHER_CHUNK
HIST_UNITS = GATHER_CHUNK // 2
HIST_SLOTS = HIST_UNITS // 2
QUADS = T // 4
MSG = GATHER_CHUNK * FEAT

D_ROWS = 60
D_CHUNKS = N_NODES // (P * D_ROWS)
D_TAIL = N_NODES - D_CHUNKS * P * D_ROWS
TAIL_P, TAIL_ROWS = D_TAIL // 4, 4
NODE_STEPS = 11
N_WEIGHT_LOADS = 20
UNIT_ROWS = 12
D_UNITS = D_ROWS // UNIT_ROWS


def gnn_kernel(nc, x, src, dst, r_feat, rel, edge_attr, edge_weight, w1, b1, w2, b2,
               m_w1, m_b1, m_w2, m_b2, g_w1, g_b1, g_w2s, g_b2s, g_w2d, g_b2d, attn, out):
    f32, i32, f16 = mybir.dt.float32, mybir.dt.int32, mybir.dt.float16
    ALU, ACT, AX = mybir.AluOpType, mybir.ActivationFunctionType, mybir.AxisListType.X

    with ExitStack() as ctx:
        def sb(name, shape, dt=f32):
            return ctx.enter_context(nc.sbuf_tensor(name, shape, dt))

        def sem(name):
            return ctx.enter_context(nc.semaphore(name))

        def dram(name, shape, dt=f32):
            return nc.dram_tensor(name, shape, dt).ap()

        pos_table = dram("pos_table", (HI * P, 1), i32)
        tables = [dram(f"table_{k}", (E_PAD, FEAT)) for k in range(5)]

        A_dst = sb("A_dst", [P, T, FEAT])
        A_src = sb("A_src", [P, T, FEAT])
        A_msg = sb("A_msg", [P, T, FEAT])
        A_sum = sb("A_sum", [P, T, FEAT])
        A_tmp = sb("A_tmp", [P, T, FEAT])
        work = sb("work", [P, T, HF])
        work_flat = work[:].rearrange("p t f -> p (t f)")

        tmp_flat = A_tmp[:].rearrange("p t f -> p (t f)")

        def carver(of):
            at = [0]

            def carve(parts, *dims, dt=f32):
                n = 1
                for d in dims:
                    n *= d
                words = n if dt in (f32, i32) else n // 2
                view = of[0:parts, at[0]:at[0] + words]
                at[0] += words
                assert at[0] <= of.shape[1]
                if dt is not f32:
                    view = view.bitcast(dt)
                if len(dims) == 2:
                    view = view.rearrange("p (a b) -> p a b", b=dims[1])
                if len(dims) == 3:
                    view = view.rearrange("p (a b c) -> p a b c", b=dims[1], c=dims[2])
                return view
            return carve

        src_i = sb("src_i", [P, T], i32)
        dst_i = sb("dst_i", [P, T], i32)
        nxt_i = sb("nxt_i", [P, T], i32)
        pos_i = sb("pos_i", [P, T], i32)
        out_i = sb("out_i", [P, T], i32)
        ew = sb("ew", [P, T + 4])
        dst_f = sb("dst_f", [P, T])
        is_last = sb("is_last", [P, T])
        not_last = sb("not_last", [P, T])
        same = sb("same", [P, T])
        same_pen = sb("same_pen", [P, T])
        in_first = sb("in_first", [P, T])
        in_first_pen = sb("in_first_pen", [P, T])
        in_final = sb("in_final", [P, T])
        dinv = sb("dinv", [P, T])
        stat = sb("stat", [P, T])
        std = sb("std", [P, T])
        r3 = sb("r3", [P, T])
        small = sb("small", [P, 4, T])
        small2 = sb("small2", [P, 4, T])

        ident = sb("ident", [P, P])
        ones = sb("ones", [P, 32])
        eps_t = sb("eps_t", [P, 1])
        rows = sb("rows", [32, 8, P])
        diag = sb("diag", [P, P])
        seam_state = sb("seam_state", [32, P])
        seam_shift = sb("seam_shift", [32, P])
        ends_row = sb("ends_row", [32, P])
        carry = sb("carry", [P, 32])
        end_col = sb("end_col", [P, 32])

        w2fold = sb("w2fold", [HID0 + 1, PATHS])
        w1rep = sb("w1rep", [P, HID0 + 1])
        b1col = sb("b1col", [HID0 + 1, 1])
        mw1 = sb("mw1", [96, HID0])
        mb1 = sb("mb1", [HID0, 1])
        mw2 = sb("mw2", [HID0 + 1, FEAT])
        gw2 = sb("gw2", [HF + 1, 2 * HF])
        gtmp = sb("gtmp", [HF + 1, HF])
        attn_rep = sb("attn_rep", [P, HF])
        gw1 = sb("gw1", [P, P])
        gw3 = sb("gw3", [HF + 1, FEAT])
        gb1 = sb("gb1", [P, FEAT])
        gb1c = sb("gb1c", [P, FEAT])
        nodes_w = sb("nodes_w", [P, 2 * P])
        nodes_t = sb("nodes_t", [P, P])
        zero_hot = sb("zero_hot", [P, P], f16)

        banks = [ctx.enter_context(nc.psum_tensor(f"bank_{b}", [P, 512], f32)) for b in range(8)]

        loaded_dst, loaded_src, loaded_edges = sem("loaded_dst"), sem("loaded_src"), sem("loaded_edges")
        loaded_w, pads_ready = sem("loaded_w"), sem("pads_ready")
        pool_seq, consts_ready, dve_seq = sem("pool_seq"), sem("consts_ready"), sem("dve_seq")
        src_rows = [sem(f"src_rows_{c}") for c in range(CHUNKS)]
        dst_rows, pos_rows = sem("dst_rows"), sem("pos_rows")
        var_ready, std_ready = sem("var_ready"), sem("std_ready")
        centered, squared = sem("centered"), sem("squared")
        ends_ready, ends_turned = sem("ends_ready"), sem("ends_turned")
        carry_ready, carry_turned = sem("carry_ready"), sem("carry_turned")
        onehots_ready, onehots_used = sem("onehots_ready"), sem("onehots_used")
        digits_ready, lo_seq, lo_ready = sem("digits_ready"), sem("lo_seq"), sem("lo_ready")
        hist_done, pos_f_ready = sem("hist_done"), sem("pos_f_ready")
        pos_turned, pos_int, pos_stored = sem("pos_turned"), sem("pos_int"), sem("pos_stored")
        weights_folded, weights_ready = sem("weights_folded"), sem("weights_ready")
        cw_done, cw_copied = sem("cw_done"), sem("cw_copied")
        pre_ready, pre_turned = sem("pre_ready"), sem("pre_turned")
        hid_ready, radial_ready, radial_used = sem("hid_ready"), sem("radial_ready"), sem("radial_used")
        table_ready, table_stored, rows_in = sem("table_ready"), sem("table_stored"), sem("rows_in")
        gather_ok = sem("gather_ok")
        n_loaded = [sem(f"n_loaded_{s}") for s in range(SLOTS)]
        n_turned, n_xt, n_mm = sem("n_turned"), sem("n_xt"), sem("n_mm")
        n_bank = sem("n_bank")
        n_var, n_std, n_z, n_zsq, n_out = sem("n_var"), sem("n_std"), sem("n_z"), sem("n_zsq"), sem("n_out")
        n_stored = [sem(f"n_stored_{s}") for s in range(SLOTS)]
        ea_in, tmp_free = sem("ea_in"), sem("tmp_free")
        e_cat, e_catd, e_turned, e_catT = sem("e_cat"), sem("e_catd"), sem("e_turned"), sem("e_catT")
        e_h, e_hT, e_v, e_vused = sem("e_h"), sem("e_hT"), sem("e_v"), sem("e_vused")
        a_cat, a_turned, a_catT, a_mm = sem("a_cat"), sem("a_turned"), sem("a_catT"), sem("a_mm")
        a_act, a_used = sem("a_act"), sem("a_used")
        quad_rows = [[sem(f"quad_rows_{k}_{s}") for s in range(SLOTS)] for k in (3, 4)]
        rf_in = [sem(f"rf_in_{s}") for s in range(SLOTS)]
        exp_req, exp_done = sem("exp_req"), sem("exp_done")
        res_mm, res_used = sem("res_mm"), sem("res_used")
        w_ready, w_exp = sem("w_ready"), sem("w_exp")
        msg_ready, msg_turned, msg_T = sem("msg_ready"), sem("msg_turned"), sem("msg_T")
        msg_mm, msg_out = sem("msg_mm"), sem("msg_out")
        f_centered, f_squared, f_var, f_std = sem("f_centered"), sem("f_squared"), sem("f_var"), sem("f_std")
        prod_used, node_seq, a_weighed = sem("prod_used"), sem("node_seq"), sem("a_weighed")
        a_leaky = sem("a_leaky")
        final_ready, scattered = sem("final_ready"), sem("scattered")

        cv = carver(A_msg[:].rearrange("p t f -> p (t f)"))
        hi_hot = cv(P, HIST_SLOTS * 2, HI, dt=f16)
        cv = carver(A_sum[:].rearrange("p t f -> p (t f)"))
        lo_hot = cv(P, HIST_SLOTS * 4, P, dt=f16)
        lo_far = cv(P, HIST_SLOTS, P, dt=f16)
        cv = carver(work_flat)
        iota16 = cv(P, HI, dt=f16)
        pre = cv(P, SLOTS, 2, HID0 + 1)
        hidT = cv(HID0 + 1, SLOTS, 2 * P)
        prod = cv(P, 4, 640)
        path_sums = cv(P, GATHER_CHUNK, 64)
        ff = cv(P, GATHER_CHUNK, 16)
        g5 = cv(P, GATHER_CHUNK, 8, 5)
        vec_a = cv(P, GATHER_CHUNK, 24)
        cv = carver(work_flat)
        n_x = cv(P, SLOTS, D_ROWS, FEAT)
        n_o = cv(P, SLOTS, D_ROWS, FEAT)
        n_q = cv(P, D_ROWS, FEAT)
        n_xT = cv(P, SLOTS, 3 * P)
        n_s = cv(P, 4, D_ROWS)
        cv = carver(tmp_flat)
        unit = cv(P, T, 5)
        w2raw = cv(HID0 + 1, PATHS)
        pos_f = cv(P, HI)
        pos_zero = cv(P, HI)
        pos_int_t = cv(P, 7, P, dt=i32)
        hi_digit = cv(P, T)
        lo_digit, minus_lo = cv(P, T), cv(P, T)
        val_hi, minus_val_hi = cv(P, T), cv(P, T)
        val_lo, minus_val_lo = cv(P, T), cv(P, T)
        cv = carver(work_flat)
        cat = cv(P, SLOTS, 4, 96)
        catT = cv(96, SLOTS, 4 * P)
        hidT2 = cv(HID0 + 1, SLOTS, 4 * P)
        cv = carver(tmp_flat)
        cat3 = cv(P, SLOTS, 4, HF + 1)
        catT3 = cv(HF + 1, SLOTS, 4 * P)
        rf = cv(P, SLOTS, 4, HF)
        leaky = cv(P, SLOTS, 4, HF)
        cv = carver(tmp_flat)
        msgT = cv(P, SLOTS, GATHER_CHUNK * FEAT)

        edge_no = small2[:, 0, :].bitcast(i32)

        def triple(ap):
            return ap.rearrange("p a t -> p (a t)").rearrange("p (t a) -> p t a", a=3)

        rel_t, rel_sq = triple(small[:, 0:3, :]), triple(small2[:, 1:4, :])

        def pair(ap):
            return ap.rearrange("p a t -> p (a t)").rearrange("p (t h) -> p t h", h=HEADS)

        pair_a, pair_b = pair(small[:, 0:2, :]), pair(small[:, 2:4, :])
        pair_c, pair_d = pair(small2[:, 0:2, :]), pair(small2[:, 2:4, :])

        def flat(ap):
            return ap.rearrange("p a b -> p (a b)")

        def bcast(ap, n):
            return ap.unsqueeze(len(ap.shape)).to_broadcast(list(ap.shape) + [n])

        def mid(ap, n):
            return ap.unsqueeze(1).to_broadcast([ap.shape[0], n, ap.shape[1]])

        main = "(p t) -> p t"
        main3 = "(p t) f -> p t f"

        def pipeline(eng, *steps):
            lag = len(steps) - 1

            def turn(i, parity):
                for k, step in enumerate(steps):
                    if step is None or isinstance(i, int) and not 0 <= i - k < QUADS:
                        continue
                    step(i - k, (parity - k) % SLOTS)

            start = lag + lag % 2
            pairs = (QUADS - start) // 2
            for i in range(start):
                turn(i, i % 2)
            with eng.Fori(0, pairs) as pair:
                turn(pair * 2 + start, 0)
                turn(pair * 2 + (start + 1), 1)
            for i in range(start + 2 * pairs, QUADS + lag):
                turn(i, i % 2)

        def in_turn(*steps):
            for i in range(CHUNKS + len(steps) - 1):
                for k, step in enumerate(steps):
                    if 0 <= i - k < CHUNKS:
                        step(i - k)

        NODE_PAIRS = [(0, 2, False), (2, 4, False), (4, D_CHUNKS // 2, True)]
        assert D_CHUNKS % 2 == 1 and D_UNITS % 2 == 1

        def node_chunks(eng, body, first, last, tail):
            if first == 0:
                body(0, 0, 0, P, D_ROWS)
                body(1, 0, 1, P, D_ROWS)
                first = 1
            with eng.Fori(first, last) as i:
                body(i * 2, i, 0, P, D_ROWS)
                body(i * 2 + 1, i, 1, P, D_ROWS)
            if tail:
                body(D_CHUNKS - 1, D_CHUNKS // 2, 0, P, D_ROWS)
                body(D_CHUNKS, D_CHUNKS // 2, 1, TAIL_P, TAIL_ROWS)

        def node_rows(ap, c, parts):
            if parts == P:
                return ap[bass.ds(c * (P * D_ROWS), P * D_ROWS), :].rearrange("(p r) f -> p r f", p=P)
            return ap[D_CHUNKS * P * D_ROWS:N_NODES, :].rearrange("(p r) f -> p r f", p=parts)

        def node_units(slot, n_rows):
            if n_rows == TAIL_ROWS:
                return [(0, slot, TAIL_ROWS)]
            return [(j, (slot + j) % SLOTS, UNIT_ROWS) for j in range(D_UNITS)]

        block = ctx.enter_context(nc.Block())

        @block.sync
        def _(sp):
            sp.wait_ge(pads_ready, 1)
            for tile, ap, off, done in ((src_i, src, 0, loaded_src), (dst_i, dst, 0, loaded_dst),
                                        (nxt_i, dst, 1, loaded_dst)):
                n = REST - off
                sp.dma_start(tile[0:FULL, :], ap[off:off + FULL * T].rearrange(main, t=T)).then_inc(done, 16)
                sp.dma_start(tile[FULL:FULL + 1, 0:n],
                             ap[off + FULL * T:off + FULL * T + n].rearrange("(p t) -> p t", p=1)).then_inc(done, 16)
            sp.dma_start(ew[0:FULL, 0:T], edge_weight[0:FULL * T].rearrange(main, t=T)).then_inc(loaded_edges, 16)
            sp.dma_start(ew[FULL:FULL + 1, 0:REST],
                         edge_weight[FULL * T:N_EDGES].rearrange("(p t) -> p t", p=1)).then_inc(loaded_edges, 16)
            sp.dma_start(rel_t[0:FULL], rel[0:FULL * T, :].rearrange(main3, t=T)).then_inc(loaded_edges, 16)
            sp.dma_start(rel_t[FULL:FULL + 1, 0:REST],
                         rel[FULL * T:N_EDGES, :].rearrange("(p t) f -> p t f", p=1)).then_inc(loaded_edges, 16)
            row, col = "(a b) -> a b", "(a b) -> a b"
            for to, of in (
                (w2raw[0:HID0, :], w2), (w2raw[HID0:HID0 + 1, :], b2.rearrange(row, a=1)),
                (w1rep[:, 0:HID0], w1[0, :].partition_broadcast(P)), (b1col[0:HID0, :], b1.rearrange(col, b=1)),
                (mw1[:], m_w1), (mb1[:], m_b1.rearrange(col, b=1)),
                (mw2[0:HID0, :], m_w2), (mw2[HID0:HID0 + 1, :], m_b2.rearrange(row, a=1)),
                (gw2[0:32, 0:HF], g_w2s), (gw2[0:32, HF:2 * HF], g_w2s), (gw2[32:64, HF:2 * HF], g_w2d),
                (gw2[HF:HF + 1, 0:HF], g_b2s.rearrange(row, a=1)),
                (gw2[HF:HF + 1, HF:2 * HF], g_b2s.rearrange(row, a=1)),
                (gtmp[HF:HF + 1, :], g_b2d.rearrange(row, a=1)),
                (attn_rep[:], attn[0].rearrange("h f -> (h f)").partition_broadcast(P)),
                (gb1[:], g_b1.partition_broadcast(P)),
                *((gw1[32 * k:32 * k + 32, 32 * k:32 * k + 32], g_w1) for k in range(4)),
            ):
                sp.dma_start(to, of).then_inc(loaded_w, 16)

            sp.wait_ge(pos_int, 1)
            table = pos_table.rearrange("(h l) a -> h (l a)", l=P)
            whole = HI // P
            sp.dma_start(table[0:whole * P, :].rearrange("(k p) l -> p k l", p=P),
                         pos_int_t[:, 0:whole, :]).then_inc(pos_stored, 16)
            sp.dma_start(table[whole * P:HI, :], pos_int_t[0:HI - whole * P, whole, :]).then_inc(pos_stored, 16)

            def exchange(k, of):
                sp.wait_ge(table_ready, k + 1)
                sp.dma_start(tables[k].rearrange(main3, t=T), of[:]).then_inc(table_stored, 16)

            def load_nodes(c, half, slot, parts, n_rows):
                sp.wait_ge(n_turned, c * D_UNITS + D_UNITS)
                sp.dma_start(n_x[0:parts, slot, 0:n_rows, :], node_rows(x, c, parts)).then_inc(n_loaded[slot], 16)

            for k, (first, last, tail) in enumerate(NODE_PAIRS):
                exchange(k, A_tmp)
                node_chunks(sp, load_nodes, first, last, tail)
            exchange(3, A_dst)

            sp.wait_ge(tmp_free, 1)
            sp.dma_start(A_tmp[0:FULL], edge_attr[0:FULL * T, :].rearrange(main3, t=T)).then_inc(ea_in, 16)
            sp.dma_start(A_tmp[FULL:FULL + 1, 0:REST, :],
                         edge_attr[FULL * T:N_EDGES, :].rearrange("(p t) f -> p t f", p=1)).then_inc(ea_in, 16)
            exchange(4, A_dst)

            edges = r_feat.rearrange("e h f -> e (h f)")

            def load_rf(q, slot, rest_row):
                sp.wait_ge(a_used, q + 1)
                sp.dma_start(rf[0:FULL, slot], edges[0:FULL * T, :].rearrange("(p t) f -> p t f", t=T)
                             [:, bass.ds(q * 4, 4), :]).then_inc(rf_in[slot], 16)
                sp.dma_start(rf[FULL:P, slot], edges[bass.ds(rest_row, 4), :].rearrange("(p t) f -> p t f", p=1)
                             ).then_inc(rf_in[slot], 16)

            true_quads = REST // 4
            assert REST % 4 == 0 and true_quads % 2 == 1 and QUADS % 2 == 1
            with sp.Fori(0, true_quads // 2) as i:
                for slot in range(SLOTS):
                    load_rf(i * 2 + slot, slot, i * 8 + (FULL * T + 4 * slot))
            load_rf(true_quads - 1, 0, N_EDGES - 4)
            load_rf(true_quads, 1, 0)
            with sp.Fori((true_quads + 1) // 2, QUADS // 2) as i:
                for slot in range(SLOTS):
                    load_rf(i * 2 + slot, slot, 0)
            load_rf(QUADS - 1, 0, 0)
            sp.wait_ge(scattered, 16 * T)

        @block.gpsimd
        def _(pool):
            pool.memset(src_i[:], SKIP)
            pool.memset(dst_i[:], PAD_DST)
            pool.memset(nxt_i[:], PAD_NEXT)
            pool.memset(ew[:], 0.0)
            pool.memset(small[:], 1.0)
            pool.memset(w1rep[:], 0.0)
            pool.memset(b1col[:], 1.0)
            pool.memset(gw2[:], 0.0)
            pool.memset(gw1[:], 0.0)
            pool.memset(A_src[:], 0.0).then_inc(pads_ready, 1)
            pool.memset(pos_i[:], SKIP)
            pool.memset(ones[:], 1.0)
            pool.memset(eps_t[:], EPS)
            pool.memset(zero_hot[:], 0.0)
            pool.memset(ident[:], 0.0).then_inc(pool_seq, 1)
            pool.wait_ge(pool_seq, 1)
            pool.affine_select(out=ident[:], in_=ident[:], compare_op=ALU.not_equal, fill=1.0, base=0,
                               pattern=[[-1, P]], channel_multiplier=1)
            pool.iota(edge_no, pattern=[[1, T]], base=1, channel_multiplier=T)
            pool.iota(iota16, pattern=[[1, HI]], base=0, channel_multiplier=0,
                      allow_small_or_imprecise_dtypes=True).then_inc(consts_ready, 1)

            def gather(column, of, idx, limit, done, columns=range(T)):
                for t in columns:
                    pool.indirect_dma_start(
                        out=column(t), out_offset=None, in_=of,
                        in_offset=bass.IndirectOffsetOnAxis(ap=idx[:, t:t + 1], axis=0),
                        bounds_check=limit, oob_is_err=False).then_inc(done(t), 16)

            pool.wait_ge(loaded_src, 32)
            pool.wait_ge(pads_ready, 1)
            gather(lambda t: A_src[:, t, :], x, src_i, N_NODES - 1, lambda t: src_rows[t // GATHER_CHUNK])
            pool.wait_ge(loaded_dst, 64)
            pool.wait_ge(gather_ok, 1)
            gather(lambda t: A_dst[:, t, :], x, dst_i, N_NODES - 1, lambda t: dst_rows)
            pool.wait_ge(pos_stored, 32)
            gather(lambda t: pos_i[:, t:t + 1], pos_table, src_i, N_NODES - 1, lambda t: pos_rows)
            pool.wait_ge(pos_rows, 16 * T)
            for k in range(5):
                pool.wait_ge(table_stored, 16 * (k + 1))
                pool.wait_ge(gather_ok, k + 2)
                if k < 3:
                    gather(lambda t: A_msg[:, t, :], tables[k], pos_i, E_PAD - 1, lambda t: rows_in)
                    pool.wait_ge(rows_in, 16 * T * (k + 1))
                    continue
                for q in range(QUADS):
                    here = quad_rows[k - 3][q % SLOTS]
                    if q >= SLOTS:
                        pool.wait_ge(here, 64 * (q // SLOTS))
                    gather(lambda t: A_src[:, t, :], tables[k], pos_i, E_PAD - 1, lambda t: here,
                           range(4 * q, 4 * q + 4))
            for slot in range(SLOTS):
                pool.wait_ge(n_stored[slot], 16 * (D_CHUNKS // 2 + 1))
            for t in range(T):
                if t % GATHER_CHUNK == 0:
                    pool.wait_ge(final_ready, t // GATHER_CHUNK + 1)
                pool.indirect_dma_start(
                    out=out, out_offset=bass.IndirectOffsetOnAxis(ap=out_i[:, t:t + 1], axis=0),
                    in_=A_tmp[:, t, :], in_offset=None, bounds_check=N_NODES - 1,
                    oob_is_err=False).then_inc(scattered, 16)

        @block.scalar
        def _(act):
            done = {"root": 0, "square": 0}

            def next_root(scale, bias=True):
                done["root"] += 1
                act.wait_ge(var_ready, done["root"])
                nc.scalar.activation(std[:], stat[:], ACT.Sqrt, scale=scale,
                                     bias=eps_t[:] if bias else 0.0).then_inc(std_ready, 1)

            def next_square(of):
                done["square"] += 1
                act.wait_ge(centered, done["square"])
                nc.scalar.activation(A_sum[:], of[:], ACT.Square).then_inc(squared, 1)

            act.wait_ge(consts_ready, 1)
            next_root(1.0, bias=False)

            act.wait_ge(digits_ready, 1)
            with act.Fori(0, T // GATHER_CHUNK) as i:
                for k in range(HIST_UNITS):
                    slot = k % HIST_SLOTS
                    act.wait_ge(onehots_used, i * HIST_UNITS + (k + 1))
                    t = bass.ds(i * GATHER_CHUNK + (2 * k + 1), 1)
                    far = lo_far[:, slot, :]
                    nc.scalar.activation(far, iota16[:, 0:P], ACT.Abs, bias=minus_lo[:, t]).then_inc(lo_seq, 1)
                    act.wait_ge(lo_seq, i * HIST_UNITS + (k + 1))
                    nc.scalar.activation(lo_hot[:, 4 * slot + 2, :], far, ACT.Relu,
                                         scale=minus_val_hi[:, t], bias=val_hi[:, t])
                    nc.scalar.activation(lo_hot[:, 4 * slot + 3, :], far, ACT.Relu,
                                         scale=minus_val_lo[:, t], bias=val_lo[:, t]).then_inc(lo_ready, 1)

            act.wait_ge(loaded_w, 16 * N_WEIGHT_LOADS)
            act.sem_inc(hid_ready, SLOTS)
            with act.Fori(0, T // 4) as i:
                for slot in range(SLOTS):
                    u = i * 2 + slot
                    act.wait_ge(pre_turned, u + (1 + SLOTS))
                    act.wait_ge(radial_ready, u + 1)
                    nc.scalar.activation(hidT[:, slot, :], banks[slot][0:HID0 + 1, 0:2 * P], ACT.Relu,
                                         bias=b1col[:]).then_inc(hid_ready, 1)

            next_square(A_dst)
            next_root(1.0 / FEAT)
            next_root(1.0, bias=False)
            next_square(A_src)
            next_root(1.0 / FEAT)
            next_root(1.5625)
            next_root(4.0)

            act.sem_inc(n_xt, SLOTS)
            act.sem_inc(n_bank, SLOTS)

            def nodes(c, half, slot, parts, n_rows):
                if not isinstance(half, int) or half:
                    act.wait_ge(n_stored[slot], half * 16)
                for j, s, nr in node_units(slot, n_rows):
                    u, n, width = c * D_UNITS + j, nr * FEAT, (nr // 4) * parts
                    act.wait_ge(n_turned, u + (1 + SLOTS * D_UNITS))
                    act.wait_ge(n_mm, u + 1)
                    nc.scalar.copy(n_xT[:, s, 0:width], banks[s][:, 0:width]).then_inc(n_xt, 1)
                    act.wait_ge(n_mm, u + (1 + SLOTS))
                    r = j * UNIT_ROWS
                    nc.scalar.activation(n_q[0:parts, r:r + nr, :].rearrange("p r f -> p (r f)"),
                                         banks[2 + s][0:parts, 0:n], ACT.Square)
                    nc.scalar.copy(n_o[0:parts, slot, r:r + nr, :].rearrange("p r f -> p (r f)"),
                                   banks[4 + s][0:parts, 0:n]).then_inc(n_bank, 1)
                var, dev = n_s[0:parts, 0, 0:n_rows], n_s[0:parts, 1, 0:n_rows]
                for k, scale in enumerate((1.0 / FEAT, 1.5625, 4.0)):
                    act.wait_ge(n_var, c * 4 + (k + 1))
                    nc.scalar.activation(dev, var, ACT.Sqrt, scale=scale, bias=eps_t[0:parts]).then_inc(n_std, 1)
                act.wait_ge(n_z, c + 1)
                nc.scalar.activation(n_q[0:parts, 0:n_rows, :], n_o[0:parts, slot, 0:n_rows, :],
                                     ACT.Square).then_inc(n_zsq, 1)
                act.wait_ge(n_var, c * 4 + 4)
                nc.scalar.activation(dev, var, ACT.Sqrt, scale=1.0 / FEAT, bias=eps_t[0:parts]).then_inc(n_std, 1)
                act.wait_ge(n_out, c + 1)
                act.dma_start(node_rows(out, c, parts), n_o[0:parts, slot, 0:n_rows, :]).then_inc(n_stored[slot], 16)

            for first, last, tail in NODE_PAIRS:
                node_chunks(act, nodes, first, last, tail)
            next_square(A_dst)
            next_root(1.0 / FEAT)

            for slot in range(SLOTS):
                act.wait_ge(n_stored[slot], 16 * (D_CHUNKS // 2 + 1))
            act.sem_inc(e_catT, SLOTS)
            act.sem_inc(e_hT, SLOTS)

            def bring_src(q, slot):
                act.wait_ge(quad_rows[0][slot], q * 32 + (64 - 32 * slot))
                act.wait_ge(e_turned, q + 1)
                nc.scalar.copy(cat[:, slot, :, 0:32], A_src[:, bass.ds(q * 4, 4), :]).then_inc(e_cat, 1)

            def copy_turned(q, slot):
                act.wait_ge(e_turned, q + (1 + SLOTS))
                act.wait_ge(e_h, q + 1)
                nc.scalar.copy(catT[:, slot, :], banks[slot][0:96, :]).then_inc(e_catT, 1)

            def hidden(q, slot):
                act.wait_ge(e_h, q + (1 + SLOTS))
                act.wait_ge(e_v, q + 1)
                nc.scalar.activation(hidT2[0:HID0, slot, :], banks[2 + slot][0:HID0, :], ACT.Relu,
                                     bias=mb1[:]).then_inc(e_hT, 1)

            pipeline(act, bring_src, copy_turned, hidden)
            next_square(A_dst)
            next_root(1.0 / FEAT)

            act.sem_inc(a_catT, SLOTS)
            act.sem_inc(a_act, SLOTS)
            act.sem_inc(res_used, SLOTS)
            act.wait_ge(table_stored, 16 * 5)

            def copy_turned3(q, slot):
                act.wait_ge(a_turned, q + (1 + SLOTS))
                act.wait_ge(a_mm, q + 1)
                nc.scalar.copy(catT3[:, slot, :], banks[slot][0:HF + 1, :]).then_inc(a_catT, 1)

            def slope(q, slot):
                act.wait_ge(a_mm, q + (1 + SLOTS))
                act.wait_ge(a_used, q + 1)
                nc.scalar.activation(leaky[:, slot], banks[2 + slot][:].rearrange("p (t g) -> p t g", t=4)
                                     [:, :, HF:2 * HF], ACT.Copy, scale=NEG_SLOPE).then_inc(a_act, 1)
                act.wait_ge(res_mm, q + (1 + SLOTS))
                nc.scalar.copy(A_dst[:, bass.ds(q * 4, 4), :], banks[4 + slot][:, 0:P].rearrange("p (t f) -> p t f", f=FEAT)
                               ).then_inc(res_used, 1)

            pipeline(act, None, copy_turned3, slope)
            act.wait_ge(exp_req, 1)
            nc.scalar.activation(small2[:, 0:2, :], small2[:, 0:2, :], ACT.Exp).then_inc(exp_done, 1)

            def chunk(a, c):
                return a[:, c * GATHER_CHUNK:(c + 1) * GATHER_CHUNK, :]

            def exp_chunk(c):
                act.wait_ge(w_ready, c + 1)
                nc.scalar.activation(chunk(work, c), chunk(work, c), ACT.Exp).then_inc(w_exp, 1)

            def copy_messages(c):
                act.wait_ge(msg_turned, c + 1)
                if c >= SLOTS:
                    act.wait_ge(msg_mm, c - 1)
                b = 2 * (c % SLOTS)
                nc.scalar.copy(msgT[:, c % SLOTS, 0:512], banks[b][:, :])
                nc.scalar.copy(msgT[:, c % SLOTS, 512:MSG], banks[b + 1][:, 0:MSG - 512]).then_inc(msg_T, 1)

            def take_product(c):
                act.wait_ge(msg_mm, c + 1)
                b, to = 4 + 2 * (c % SLOTS), chunk(A_msg, c).rearrange("p t f -> p (t f)")
                nc.scalar.copy(to[:, 0:512], banks[b][:, :])
                nc.scalar.copy(to[:, 512:MSG], banks[b + 1][:, 0:MSG - 512]).then_inc(msg_out, 1)

            in_turn(exp_chunk, copy_messages, take_product)

            def final_square(c):
                act.wait_ge(f_centered, c + 1)
                nc.scalar.activation(chunk(A_sum, c), chunk(A_tmp, c), ACT.Square).then_inc(f_squared, 1)

            def final_root(c):
                act.wait_ge(f_var, c + 1)
                at = slice(c * GATHER_CHUNK, (c + 1) * GATHER_CHUNK)
                nc.scalar.activation(std[:, at], stat[:, at], ACT.Sqrt, scale=1.0 / FEAT, bias=eps_t[:]).then_inc(f_std, 1)

            in_turn(final_square, final_root)

        @block.tensor
        def _(pe):
            def turn(out_ap, in_ap, n):
                return nc.tensor.transpose(out_ap, in_ap, ident[0:n, 0:n])

            seams = {"n": 0}

            def seam(width):
                seams["n"] += 1
                pe.wait_ge(ends_ready, 2 + seams["n"])
                turn(banks[6][0:width, 0:P], end_col[:, 0:width], P).then_inc(ends_turned, 1)
                pe.wait_ge(carry_ready, seams["n"])
                turn(banks[7][:, 0:width], seam_shift[0:width, :], width).then_inc(carry_turned, 1)

            pe.wait_ge(consts_ready, 1)
            for k in range(2):
                pe.wait_ge(ends_ready, k + 1)
                nc.tensor.matmul(banks[6 + k][0:32, 0:P], ones[:], diag[:], start=True, stop=True).then_inc(ends_turned, 1)

            for k in range(2):
                pe.wait_ge(weights_folded, k + 1)
                nc.tensor.matmul(banks[4 + k][:, 0:P], nodes_t[:], nodes_w[:, 0:P], start=True, stop=True).then_inc(cw_done, 1)

            half = HI // 2
            pe.wait_ge(digits_ready, 1)
            for h in range(2):
                nc.tensor.matmul(banks[6 + h][:, 0:half], zero_hot[:], iota16[:, 0:half], start=True, stop=False)
            pe.sem_inc(onehots_used, HIST_SLOTS)
            with pe.Fori(0, T // GATHER_CHUNK) as i:
                for k in range(HIST_UNITS):
                    slot = k % HIST_SLOTS
                    pe.wait_ge(onehots_ready, i * HIST_UNITS + (k + 1))
                    pe.wait_ge(lo_ready, i * HIST_UNITS + (k + 1))
                    for j in range(2):
                        for part in range(2):
                            for h in range(2):
                                last = nc.tensor.matmul(banks[6 + h][:, 0:half], lo_hot[:, 4 * slot + 2 * j + part, :],
                                                        hi_hot[:, 2 * slot + j, h * half:(h + 1) * half],
                                                        start=False, stop=False)
                    last.then_inc(onehots_used, 1)
            for h in range(2):
                last = nc.tensor.matmul(banks[6 + h][:, 0:half], zero_hot[:], iota16[:, 0:half], start=False, stop=True)
            last.then_inc(hist_done, 1)
            pe.wait_ge(pos_f_ready, 1)
            for k in range(7):
                n = min(P, HI - k * P)
                last = turn(banks[4 + k // 4][0:n, (k % 4) * P:(k % 4 + 1) * P], pos_f[:, k * P:k * P + n], P)
            last.then_inc(pos_turned, 1)

            pe.sem_inc(pre_turned, SLOTS)
            pe.sem_inc(radial_ready, SLOTS)
            pe.wait_ge(pos_int, 1)

            def turn_pre(u, slot):
                pe.wait_ge(pre_ready, u + 1)
                pe.wait_ge(hid_ready, u + 1)
                for j in range(2):
                    last = turn(banks[slot][0:HID0 + 1, j * P:(j + 1) * P], pre[:, slot, j, :], P)
                last.then_inc(pre_turned, 1)

            turn_pre(0, 0)
            turn_pre(1, 1)
            with pe.Fori(0, T // 4) as i:
                for slot in range(SLOTS):
                    u = i * 2 + slot
                    pe.wait_ge(hid_ready, u + (1 + SLOTS))
                    pe.wait_ge(radial_used, u + 1)
                    for j in range(2):
                        last = nc.tensor.matmul(banks[2 + 2 * slot + j][:, 0:PATHS], hidT[:, slot, j * P:(j + 1) * P],
                                                w2fold[:], start=True, stop=True)
                    last.then_inc(radial_ready, 1)
                for slot in range(SLOTS):
                    turn_pre(i * 2 + (2 + slot), slot)
            seam(32)
            seam(1)

            pe.sem_inc(n_mm, SLOTS)
            pe.sem_inc(n_turned, SLOTS * D_UNITS)

            def nodes(c, half, slot, parts, n_rows):
                pe.wait_ge(n_loaded[slot], half * 16 + 16)
                for j, s, nr in node_units(slot, n_rows):
                    u = c * D_UNITS + j
                    pe.wait_ge(n_xt, u + 1)
                    for k in range(nr // 4):
                        r = j * UNIT_ROWS + 4 * k
                        last = turn(banks[s][:, k * parts:(k + 1) * parts],
                                    n_x[0:parts, slot, r:r + 4, :].rearrange("p r f -> p (r f)"), parts)
                    last.then_inc(n_turned, 1)
                    pe.wait_ge(n_xt, u + (1 + SLOTS))
                    pe.wait_ge(n_bank, u + 1)
                    for k in range(nr // 4):
                        for w in range(2):
                            last = nc.tensor.matmul(banks[2 + 2 * w + s][0:parts, k * P:(k + 1) * P],
                                                    n_xT[:, s, k * parts:(k + 1) * parts],
                                                    nodes_w[:, w * P:(w + 1) * P], start=True, stop=True)
                    last.then_inc(n_mm, 1)

            for first, last_pair, tail in NODE_PAIRS:
                node_chunks(pe, nodes, first, last_pair, tail)
                seam(32)
            seam(32)

            pe.sem_inc(e_turned, SLOTS)
            pe.sem_inc(e_h, SLOTS)
            pe.sem_inc(e_v, SLOTS)

            def turn_cat(q, slot):
                pe.wait_ge(e_cat, q + 1)
                pe.wait_ge(e_catd, q + 1)
                pe.wait_ge(e_catT, q + 1)
                for j in range(4):
                    last = turn(banks[slot][0:96, j * P:(j + 1) * P], cat[:, slot, j, :], P)
                last.then_inc(e_turned, 1)

            def first_product(q, slot):
                pe.wait_ge(e_catT, q + (1 + SLOTS))
                pe.wait_ge(e_hT, q + 1)
                nc.tensor.matmul(banks[2 + slot][0:HID0, :], mw1[:], catT[:, slot, :],
                                 start=True, stop=True).then_inc(e_h, 1)

            def second_product(q, slot):
                pe.wait_ge(e_hT, q + (1 + SLOTS))
                pe.wait_ge(e_vused, q + 1)
                for j in range(4):
                    last = nc.tensor.matmul(banks[4 + slot][:, j * FEAT:(j + 1) * FEAT],
                                            hidT2[:, slot, j * P:(j + 1) * P], mw2[:], start=True, stop=True)
                last.then_inc(e_v, 1)

            pipeline(pe, turn_cat, first_product, second_product)
            seam(32)
            seam(32)

            pe.sem_inc(a_turned, SLOTS)
            pe.sem_inc(a_mm, SLOTS)
            pe.sem_inc(res_mm, SLOTS)

            def turn_cat3(q, slot):
                pe.wait_ge(a_cat, q + 1)
                pe.wait_ge(a_catT, q + 1)
                for j in range(4):
                    last = turn(banks[slot][0:HF + 1, j * P:(j + 1) * P], cat3[:, slot, j, :], P)
                last.then_inc(a_turned, 1)

            def project(q, slot):
                pe.wait_ge(a_catT, q + (1 + SLOTS))
                pe.wait_ge(a_act, q + 1)
                pe.wait_ge(a_used, q + 1)
                for j in range(4):
                    last = nc.tensor.matmul(banks[2 + slot][:, j * P:(j + 1) * P],
                                            catT3[:, slot, j * P:(j + 1) * P], gw2[:], start=True, stop=True)
                last.then_inc(a_mm, 1)
                pe.wait_ge(res_used, q + 1)
                for j in range(4):
                    last = nc.tensor.matmul(banks[4 + slot][:, j * FEAT:(j + 1) * FEAT],
                                            catT3[:, slot, j * P:(j + 1) * P], gw3[:], start=True, stop=True)
                last.then_inc(res_mm, 1)

            pipeline(pe, turn_cat3, project)
            for _ in range(4):
                seam(2)

            def quads_of(c, first_bank):
                for k in range(GATHER_CHUNK // 4):
                    yield k, banks[first_bank + k // 4][:, (k % 4) * P:(k % 4 + 1) * P]

            def turn_messages(c):
                pe.wait_ge(msg_ready, c + 1)
                for k, to in quads_of(c, 2 * (c % SLOTS)):
                    t = c * GATHER_CHUNK + 4 * k
                    last = turn(to, A_msg[:, t:t + 4, :].rearrange("p t f -> p (t f)"), P)
                last.then_inc(msg_turned, 1)

            def message_product(c):
                pe.wait_ge(msg_T, c + 1)
                if c >= SLOTS:
                    pe.wait_ge(msg_out, c - 1)
                for k, to in quads_of(c, 4 + 2 * (c % SLOTS)):
                    last = nc.tensor.matmul(to, msgT[:, c % SLOTS, k * P:(k + 1) * P], gw1[:], start=True, stop=True)
                last.then_inc(msg_mm, 1)

            in_turn(turn_messages, message_product)
            seam(32)

        @block.vector
        def _(v):
            count = {"seq": 0, "root": 0, "square": 0, "ends": 0, "turned": 0, "carry": 0}

            def step(ins):
                count["seq"] += 1
                ins.then_inc(dve_seq, 1)
                v.wait_ge(dve_seq, count["seq"])

            def done(ins, s, n):
                ins.then_inc(s, 1)
                v.wait_ge(s, n)

            def tt(o, a, b, op):
                return v.tensor_tensor(out=o, in0=a, in1=b, op=op)

            def ts(o, a, s1, op0, s2=None, op1=None):
                if op1 is None:
                    return v.tensor_scalar(o, a, s1, None, op0)
                return v.tensor_scalar(o, a, s1, s2, op0, op1)

            def stt(o, a, s, b, op0, op1):
                return v.scalar_tensor_tensor(out=o, in0=a, scalar=s, in1=b, op0=op0, op1=op1)

            def total(o, a, op=ALU.add):
                return v.tensor_reduce(out=o, in_=a, axis=AX, op=op)

            def root(ins):
                count["root"] += 1
                done(ins, var_ready, count["root"])
                v.wait_ge(std_ready, count["root"])
                step(v.reciprocal(std[:], std[:]))

            def norm(a):
                step(total(stat[:], a[:]))
                step(ts(stat[:], stat[:], -1.0 / FEAT, ALU.mult))
                count["square"] += 1
                done(tt(a[:], a[:], bcast(stat[:], FEAT), ALU.add), centered, count["square"])
                v.wait_ge(squared, count["square"])
                root(total(stat[:], A_sum[:]))
                return tt(a[:], a[:], bcast(std[:], FEAT), ALU.mult)

            def seam(to, width, state_row, carry_row, mask, op0, op1, first, back=False):
                e = 0 if back else T - 1
                count["ends"] += 1
                done(v.tensor_copy(end_col[:, 0:width], to[:, e, :]), ends_ready, count["ends"])
                v.wait_ge(ends_turned, count["ends"])
                w = slice(0, width)
                flip = slice(None, None, -1) if back else slice(None)
                step(v.tensor_tensor_scan(out=seam_state[w, flip], data0=rows[w, state_row, flip],
                                          data1=banks[6][w, 0:P][:, flip], initial=first, op0=op0, op1=op1))
                edge = P - 1 if back else 0
                step(v.memset(seam_shift[w, edge:edge + 1], first))
                count["carry"] += 1
                if back:
                    ins = tt(seam_shift[w, 0:P - 1], seam_state[w, 1:P], rows[w, carry_row, 0:P - 1], op0)
                else:
                    ins = tt(seam_shift[w, 1:P], seam_state[w, 0:P - 1], rows[w, carry_row, 1:P], op0)
                done(ins, carry_ready, count["carry"])
                v.wait_ge(carry_turned, count["carry"])
                step(v.tensor_copy(carry[:, w], banks[7][:, w]))
                for f in range(width):
                    last = stt(to[:, :, f], mask[:], carry[:, f:f + 1], to[:, :, f], op0, op1)
                return last

            def scan(to, of, mask, op0, op1, first, back=False):
                flip = slice(None, None, -1) if back else slice(None)
                for f in range(of.shape[2]):
                    last = v.tensor_tensor_scan(out=to[:, flip, f], data0=mask[:, flip], data1=of[:, flip, f],
                                                initial=first, op0=op0, op1=op1)
                return last

            def sums(to, of):
                step(scan(to, of, same, ALU.mult, ALU.add, 0.0))
                step(seam(to, of.shape[2], 0, 1, in_first, ALU.mult, ALU.add, 0.0))

            def maxima(to, of):
                step(scan(to, of, same_pen, ALU.add, ALU.max, -BIG))
                step(seam(to, of.shape[2], 2, 3, in_first_pen, ALU.add, ALU.max, -BIG))

            def spread(to, of, tmp):
                step(tt(tmp[:], of[:], bcast(is_last[:], of.shape[2]), ALU.mult))
                step(scan(to, tmp, not_last, ALU.mult, ALU.add, 0.0, back=True))
                step(seam(to, of.shape[2], 4, 5, in_final, ALU.mult, ALU.add, 0.0, back=True))

            v.memset(A_dst[:], 0.0).then_inc(gather_ok, 1)
            v.wait_ge(pads_ready, 1)
            v.wait_ge(consts_ready, 1)
            v.wait_ge(loaded_dst, 64)
            step(v.tensor_copy(dst_f[:], dst_i[:]))
            step(v.tensor_copy(stat[:], nxt_i[:]))
            step(tt(is_last[:], dst_f[:], stat[:], ALU.not_equal))
            step(ts(not_last[:], is_last[:], -1.0, ALU.mult, 1.0, ALU.add))
            step(v.memset(same[:, 0:1], 0.0))
            step(tt(same[:, 1:T], dst_f[:, 1:T], dst_f[:, 0:T - 1], ALU.is_equal))
            step(ts(same_pen[:], same[:], -1.0, ALU.add, BIG, ALU.mult))
            step(ts(in_first[:], dst_f[:], dst_f[:, 0:1], ALU.is_equal))
            step(ts(in_first_pen[:], in_first[:], -1.0, ALU.add, BIG, ALU.mult))
            step(ts(in_final[:], dst_f[:], dst_f[:, T - 1:T], ALU.is_equal))
            step(ts(stat[:], dst_f[:], float(-SKIP), ALU.add))
            step(tt(stat[:], stat[:], is_last[:], ALU.mult))
            step(ts(out_i[:], stat[:], float(SKIP), ALU.add))

            for k, e in enumerate((T - 1, 0)):
                count["ends"] += 1
                done(ts(diag[:], ident[:], dst_f[:, e:e + 1], ALU.mult), ends_ready, count["ends"])
                v.wait_ge(ends_turned, count["ends"])
                step(v.tensor_copy(rows[:, 6 + k, :], banks[6 + k][0:32, 0:P]))
            last_row, first_row = rows[:, 6, :], rows[:, 7, :]
            step(v.memset(rows[:, 0:6, :], 0.0))
            step(tt(rows[:, 0, 1:P], last_row[:, 0:P - 1], last_row[:, 1:P], ALU.is_equal))
            step(tt(rows[:, 1, 1:P], last_row[:, 0:P - 1], first_row[:, 1:P], ALU.is_equal))
            step(ts(rows[:, 2:4, :], rows[:, 0:2, :], -1.0, ALU.add, BIG, ALU.mult))
            step(tt(rows[:, 5, 0:P - 1], last_row[:, 0:P - 1], first_row[:, 1:P], ALU.is_equal))
            step(tt(rows[:, 4, :], last_row, first_row, ALU.is_equal))
            step(tt(rows[:, 4, :], rows[:, 4, :], rows[:, 5, :], ALU.mult))

            v.wait_ge(loaded_edges, 64)
            step(tt(rel_sq, rel_t, rel_t, ALU.mult))
            root(total(stat[:], rel_sq))
            for to, of in ((0, 1), (1, 2), (2, 0), (3, 1), (4, 2)):
                ins = tt(unit[:, :, to], rel_t[:, :, of], std[:], ALU.mult)
            step(ins)

            v.wait_ge(loaded_w, 16 * N_WEIGHT_LOADS)
            three = w2raw[:, 192:PATHS].rearrange("p (m k) -> p m k", k=3)
            fold = w2fold[:, 0:256].rearrange("p (j u t v) -> p j u t v", j=2, u=8, t=2)

            def uv(ap):
                return ap.rearrange("p (u v) -> p u v", u=8)

            ts(fold[:, 0, :, 0, :], uv(w2raw[:, 0:64]), NORM0 * Y0, ALU.mult)
            ts(fold[:, 0, :, 1, :], uv(w2raw[:, 64:128]), NORM0 * C1 / sqrt(3), ALU.mult)
            ts(fold[:, 1, :, 0, :], uv(w2raw[:, 128:192]), NORM1 * C1 / sqrt(3), ALU.mult)
            ts(fold[:, 1, :, 1, :], uv(three[:, :, 2]), NORM1 * K2, ALU.mult)
            ts(w2fold[:, 320:384], three[:, :, 1], NORM1 * K1, ALU.mult)
            step(ts(w2fold[:, 256:320], three[:, :, 2], -NORM1 * K2 / 3, ALU.mult))
            step(stt(w2fold[:, 256:320], three[:, :, 0], NORM1 * Y0 / sqrt(3), w2fold[:, 256:320], ALU.mult, ALU.add))
            step(tt(gw2[HF:HF + 1, HF:2 * HF], gw2[HF:HF + 1, HF:2 * HF], gtmp[HF:HF + 1, :], ALU.add))
            d = slice(32, 64)
            step(v.memset(gw3[:], 0.0))
            tt(gw3[d, :], gw1[d, d], ident[d, d], ALU.add)
            v.tensor_copy(gw3[HF:HF + 1, :], gb1[HF:HF + 1, :])
            step(v.memset(nodes_t[:], 0.0))
            for k in range(4):
                q = slice(32 * k, 32 * k + 32)
                ins = v.memset(nodes_t[q, q], 1.0 / FEAT)
            step(ins)
            step(tt(nodes_w[:, 0:P], ident[:], nodes_t[:], ALU.subtract))
            done(tt(nodes_t[:], ident[:], gw1[:], ALU.add), weights_folded, 1)
            v.wait_ge(cw_done, 1)
            done(v.tensor_copy(nodes_t[:], banks[4][:, 0:P]), weights_folded, 2)
            v.wait_ge(cw_done, 2)
            step(v.tensor_copy(nodes_w[:, P:2 * P], banks[5][:, 0:P]))
            step(total(end_col[:, 0:1], gb1[:]))
            step(ts(end_col[:, 0:1], end_col[:, 0:1], -1.0 / FEAT, ALU.mult))
            step(ts(gb1c[:], gb1[:], end_col[:, 0:1], ALU.add))

            step(ts(nxt_i[:], dst_i[:], LOG_LO, ALU.arith_shift_right))
            step(ts(hi_digit, nxt_i[:], 1.0, ALU.add))
            step(tt(hi_digit, hi_digit, is_last[:], ALU.mult))
            step(ts(hi_digit, hi_digit, -1.0, ALU.add))
            step(ts(nxt_i[:], dst_i[:], P - 1, ALU.bitwise_and))
            v.tensor_copy(lo_digit, nxt_i[:])
            step(ts(minus_lo, nxt_i[:], -1.0, ALU.mult))
            step(ts(nxt_i[:], edge_no, P - 1, ALU.bitwise_and))
            v.tensor_copy(val_lo, nxt_i[:])
            step(ts(minus_val_lo, nxt_i[:], -1.0, ALU.mult))
            step(ts(nxt_i[:], edge_no, LOG_LO, ALU.arith_shift_right))
            ts(val_hi, nxt_i[:], float(P), ALU.mult)
            done(ts(minus_val_hi, nxt_i[:], float(-P), ALU.mult), digits_ready, 1)

            with v.Fori(0, T // GATHER_CHUNK) as i:
                for k in range(HIST_UNITS):
                    slot = k % HIST_SLOTS
                    v.wait_ge(onehots_used, i * HIST_UNITS + (k + 1))
                    for j in range(2):
                        t = bass.ds(i * GATHER_CHUNK + (2 * k + j), 1)
                        last = ts(hi_hot[:, 2 * slot + j, :], iota16, hi_digit[:, t], ALU.is_equal)
                        for part, value in enumerate((val_hi, val_lo) if j == 0 else ()):
                            ts(lo_hot[:, 4 * slot + part, :], iota16[:, 0:P], lo_digit[:, t],
                               ALU.is_equal, value[:, t], ALU.mult)
                    last.then_inc(onehots_ready, 1)

            v.wait_ge(hist_done, 1)
            for h in range(2):
                at, sum_h = slice(h * HI // 2, (h + 1) * HI // 2), banks[6 + h][:, 0:HI // 2]
                step(ts(pos_zero[:, at], sum_h, 0.0, ALU.is_equal, float(SKIP), ALU.mult))
                ins = stt(pos_f[:, at], sum_h, -1.0, pos_zero[:, at], ALU.add, ALU.add)
            done(ins, pos_f_ready, 1)
            v.wait_ge(pos_turned, 1)
            v.tensor_copy(pos_int_t[:, 0:4, :].rearrange("p k l -> p (k l)"), banks[4][:, :])
            v.tensor_copy(pos_int_t[:, 4:6, :].rearrange("p k l -> p (k l)"), banks[5][:, 0:2 * P])
            done(v.tensor_copy(pos_int_t[0:HI - 6 * P, 6, :], banks[5][0:HI - 6 * P, 2 * P:3 * P]), pos_int, 1)

            def prepare(u_next, slot, t):
                v.wait_ge(pre_turned, u_next + 1)
                tt(pre[:, slot], mid(w1rep[:], 2), bcast(ew[:, bass.ds(t, 2)], HID0 + 1), ALU.mult).then_inc(pre_ready, 1)

            prepare(0, 0, 0)
            prepare(1, 1, 2)
            v.sem_inc(radial_used, SLOTS)
            v.sem_inc(prod_used, SLOTS)
            for c in range(CHUNKS):
                v.wait_ge(src_rows[c], 16 * GATHER_CHUNK)
                cols = slice(c * GATHER_CHUNK, (c + 1) * GATHER_CHUNK)
                vec_in = A_src[:, cols, 8:32].rearrange("p t (v i) -> p t v i", i=3)
                n3 = unit[:, cols, 0:3].unsqueeze(2).to_broadcast([P, GATHER_CHUNK, 8, 3])
                a4 = vec_a.rearrange("p t (v i) -> p t v i", i=3)
                step(tt(a4, vec_in, n3, ALU.mult))
                v.tensor_copy(ff[:, :, 0:8], A_src[:, cols, 0:8])
                step(total(ff[:, :, 8:16], a4))
                with v.Fori(0, GATHER_CHUNK // 4) as i:
                    for slot in range(SLOTS):
                        u = i * 2 + (c * GATHER_CHUNK // 2 + slot)
                        t_in, t = i * 4 + 2 * slot, i * 4 + (c * GATHER_CHUNK + 2 * slot)
                        prepare(u + 2, slot, t + 4)
                        v.wait_ge(radial_ready, u + (1 + SLOTS))
                        v.wait_ge(prod_used, u + 1)
                        for j in range(2):
                            bank, to = banks[2 + 2 * slot + j], prod[:, 2 * slot + j, :]
                            tt(to[:, 0:256].rearrange("p (a b) -> p a b", b=16),
                               bank[:, 0:256].rearrange("p (a b) -> p a b", b=16),
                               ff[:, bass.ds(t_in + j, 1), :].to_broadcast([P, 16, 16]), ALU.mult)
                            vec = A_src[:, bass.ds(t + j, 1), 8:32].rearrange("p a (v i) -> p (a i) v", i=3)
                            last = tt(to[:, 256:640].rearrange("p (a i v) -> p a i v", i=3, v=8),
                                      bank[:, 256:384].rearrange("p (a v) -> p a v", v=8).unsqueeze(2)
                                      .to_broadcast([P, 16, 3, 8]),
                                      vec.unsqueeze(1).to_broadcast([P, 16, 3, 8]), ALU.mult)
                        last.then_inc(radial_used, 1)
                    for slot in range(SLOTS):
                        v.wait_ge(radial_used, i * 2 + (c * GATHER_CHUNK // 2 + slot + 1 + SLOTS))
                        at, mine = bass.ds(i * 4 + 2 * slot, 2), prod[:, 2 * slot:2 * slot + 2, :]
                        total(path_sums[:, at, 0:16], mine[:, :, 0:256].rearrange("p j (a b) -> p j a b", b=16))
                        last = total(path_sums[:, at, 16:64], mine[:, :, 256:640].rearrange("p j (a b) -> p j a b", b=8))
                        last.then_inc(prod_used, 1)
                v.wait_ge(prod_used, (c + 1) * GATHER_CHUNK // 2 + SLOTS)
                beta = path_sums[:, :, 16:40].rearrange("p t (u i) -> p t u i", i=3)
                gamma = path_sums[:, :, 40:64].rearrange("p t (u i) -> p t u i", i=3)

                def n_at(k):
                    return unit[:, cols, k:k + 3].unsqueeze(2).to_broadcast([P, GATHER_CHUNK, 8, 3])

                vec_out = A_msg[:, cols, 8:32].rearrange("p t (u i) -> p t u i", i=3)
                v.tensor_copy(A_msg[:, cols, 0:8], path_sums[:, :, 0:8])
                v.tensor_copy(g5[:, :, :, 0:3], gamma)
                step(v.tensor_copy(g5[:, :, :, 3:5], gamma[:, :, :, 0:2]))
                step(tt(a4, n_at(1), g5[:, :, :, 2:5], ALU.mult))
                step(tt(vec_out, beta, a4, ALU.add))
                step(tt(a4, n_at(2), g5[:, :, :, 1:4], ALU.mult))
                step(tt(vec_out, vec_out, a4, ALU.subtract))
                step(tt(a4, n_at(0), bcast(path_sums[:, :, 8:16], 3), ALU.mult))
                step(tt(vec_out, vec_out, a4, ALU.add))

            sums(A_sum, A_msg)
            v.wait_ge(dst_rows, 16 * T)
            step(tt(A_dst[:], A_dst[:], A_sum[:], ALU.add))
            step(norm(A_dst))

            deg = stat[:].unsqueeze(2)
            step(v.memset(small[:, 0, :], 1.0))
            step(scan(deg, small[:, 0, :].unsqueeze(2), same, ALU.mult, ALU.add, 0.0))
            root(seam(deg, 1, 0, 1, in_first, ALU.mult, ALU.add, 0.0))
            step(v.tensor_copy(dinv[:], std[:]))
            v.wait_ge(pos_stored, 32)
            done(tt(A_tmp[:], A_dst[:], bcast(dinv[:], FEAT), ALU.mult), table_ready, 1)
            v.memset(A_msg[:], 0.0).then_inc(gather_ok, 1)
            step(ts(A_dst[:], A_dst[:], 1.25, ALU.mult))

            step(total(stat[:], A_src[:]))
            step(ts(stat[:], stat[:], -1.0 / FEAT, ALU.mult))
            count["square"] += 1
            done(tt(A_src[:], A_src[:], bcast(stat[:], FEAT), ALU.add), centered, count["square"])
            v.wait_ge(squared, count["square"])
            root(total(stat[:], A_sum[:]))
            r1 = small[:, 0, :]
            step(v.tensor_copy(r1, std[:]))
            step(tt(stat[:], stat[:], std[:], ALU.mult))
            root(stt(stat[:], stat[:], 1.0 / FEAT, std[:], ALU.mult, ALU.mult))
            step(ts(std[:], std[:], 1.25, ALU.mult))
            step(tt(r1, r1, std[:], ALU.mult))
            step(tt(stat[:], stat[:], std[:], ALU.mult))
            root(tt(stat[:], stat[:], std[:], ALU.mult))
            step(ts(r3[:], std[:], 2.0, ALU.mult))
            step(tt(A_src[:], A_src[:], bcast(r1, FEAT), ALU.mult))
            dinv_sq = std
            step(tt(dinv_sq[:], dinv[:], dinv[:], ALU.mult))

            def nodes(c, half, slot, parts, n_rows):
                n_unit = len(node_units(slot, n_rows))

                def s(k):
                    return n_s[0:parts, k, 0:n_rows]

                o, q = n_o[0:parts, slot, 0:n_rows, :], n_q[0:parts, 0:n_rows, :]
                var, dev, r, tmp = s(0), s(1), s(2), s(3)

                def nroot(k, ins):
                    done(ins, n_var, c * 4 + k)
                    v.wait_ge(n_std, c * 4 + k)
                    nstep(v.reciprocal(tmp, dev))

                n_in = [0]

                def nstep(ins):
                    n_in[0] += 1
                    ins.then_inc(node_seq, 1)
                    v.wait_ge(node_seq, c * NODE_STEPS + n_in[0])

                v.wait_ge(n_bank, c * D_UNITS + (n_unit + SLOTS))
                nroot(1, total(var, q))
                nstep(v.tensor_copy(r, tmp))
                nstep(tt(var, var, tmp, ALU.mult))
                nroot(2, stt(var, var, 1.0 / FEAT, tmp, ALU.mult, ALU.mult))
                nstep(ts(tmp, tmp, 1.25, ALU.mult))
                nstep(tt(r, r, tmp, ALU.mult))
                nstep(tt(var, var, tmp, ALU.mult))
                nroot(3, tt(var, var, tmp, ALU.mult))
                nstep(stt(r, tmp, 2.0, r, ALU.mult, ALU.mult))
                nstep(tt(o, o, bcast(r, FEAT), ALU.mult))
                done(tt(o, o, mid(gb1c[0:parts], n_rows), ALU.add), n_z, c + 1)
                v.wait_ge(n_zsq, c + 1)
                nroot(4, total(var, q))
                assert n_in[0] == NODE_STEPS
                done(tt(o, o, bcast(tmp, FEAT), ALU.mult), n_out, c + 1)

            for k, (first, last_pair, tail) in enumerate(NODE_PAIRS):
                node_chunks(v, nodes, first, last_pair, tail)
                v.wait_ge(rows_in, 16 * T * (k + 1))
                done(scan(A_sum, A_msg, same, ALU.mult, ALU.add, 0.0), gather_ok, k + 3)
                step(seam(A_sum, FEAT, 0, 1, in_first, ALU.mult, ALU.add, 0.0))
                if k < 2:
                    done(tt(A_tmp[:], A_sum[:], bcast(dinv_sq[:], FEAT), ALU.mult), table_ready, k + 2)
                step(tt(A_sum[:], A_sum[:], bcast(dinv[:], FEAT), ALU.mult))
                step(stt(A_dst[:], A_sum[:], 0.25, A_dst[:], ALU.mult, ALU.add))
            v.sem_inc(tmp_free, 1)
            done(norm(A_dst), table_ready, 4)


            spread(A_sum, A_dst, A_msg)
            v.wait_ge(ea_in, 32)
            for slot in range(SLOTS):
                v.wait_ge(n_stored[slot], 16 * (D_CHUNKS // 2 + 1))
            step(v.memset(hidT2[HID0:HID0 + 1], 1.0))
            v.sem_inc(e_vused, SLOTS)

            def quad(a, q):
                return a[:, bass.ds(q * 4, 4), :]

            def bring_dst(q, slot):
                v.wait_ge(e_turned, q + 1)
                v.tensor_copy(cat[:, slot, :, 32:64], quad(A_sum, q))
                v.tensor_copy(cat[:, slot, :, 64:96], quad(A_tmp, q)).then_inc(e_catd, 1)

            def take(q, slot):
                v.wait_ge(e_v, q + (1 + SLOTS))
                v.tensor_copy(quad(A_msg, q), banks[4 + slot][:, 0:P].rearrange("p (t f) -> p t f", f=FEAT)
                              ).then_inc(e_vused, 1)

            pipeline(v, bring_dst, None, None, take)
            v.wait_ge(e_vused, QUADS + SLOTS)
            maxima(A_sum, A_msg)
            step(tt(A_msg[:], A_sum[:], A_dst[:], ALU.max))
            v.wait_ge(table_stored, 16 * 4)
            step(tt(A_dst[:], A_dst[:], A_msg[:], ALU.add))
            done(norm(A_dst), table_ready, 5)
            done(tt(A_src[:], A_src[:], bcast(r3[:], FEAT), ALU.mult), gather_ok, 6)

            spread(A_sum, A_dst, A_msg)
            step(v.memset(cat3[:, :, :, HF:HF + 1], 1.0))
            v.sem_inc(a_used, SLOTS)

            def bring_both(q, slot):
                v.wait_ge(a_turned, q + 1)
                v.wait_ge(quad_rows[1][slot], q * 32 + (64 - 32 * slot))
                v.tensor_copy(cat3[:, slot, :, 0:32], quad(A_src, q))
                v.tensor_copy(cat3[:, slot, :, 32:64], quad(A_sum, q)).then_inc(a_cat, 1)

            def score(q, slot):
                v.wait_ge(a_act, q + (1 + SLOTS))
                v.wait_ge(rf_in[slot], q * 16 + (32 - 16 * slot))
                en_rf = quad(work, q)
                tt(en_rf, banks[2 + slot][:].rearrange("p (t g) -> p t g", t=4)[:, :, 0:HF], rf[:, slot], ALU.mult)
                done(tt(leaky[:, slot], banks[2 + slot][:].rearrange("p (t g) -> p t g", t=4)[:, :, HF:2 * HF],
                        leaky[:, slot], ALU.max), a_leaky, q + 1)
                en_rf = en_rf.rearrange("p t (h f) -> p t h f", h=HEADS)
                total(quad(pair_b, q), en_rf, ALU.max)
                done(tt(leaky[:, slot], leaky[:, slot], mid(attn_rep[:], 4), ALU.mult), a_weighed, q + 1)
                tt(en_rf, en_rf, bcast(quad(pair_b, q), FEAT), ALU.subtract)
                total(quad(pair_a, q), leaky[:, slot].rearrange("p t (h f) -> p t h f", h=HEADS)).then_inc(a_used, 1)

            pipeline(v, bring_both, None, score)
            v.wait_ge(a_used, QUADS + SLOTS)

            maxima(pair_b, pair_a)
            spread(pair_c, pair_b, pair_d)
            done(tt(pair_c, pair_a, pair_c, ALU.subtract), exp_req, 1)
            v.wait_ge(exp_done, 1)
            sums(pair_b, pair_c)
            spread(pair_a, pair_b, pair_d)
            step(ts(pair_a, pair_a, 1e-9, ALU.max))
            step(v.reciprocal(pair_a, pair_a))
            step(tt(pair_c, pair_c, pair_a, ALU.mult))

            def weigh(c):
                at = slice(c * GATHER_CHUNK, (c + 1) * GATHER_CHUNK)
                rows_c = work[:, at, :].rearrange("p t (h f) -> p t h f", h=HEADS)
                tt(rows_c, rows_c, bcast(pair_c[:, at, :], FEAT), ALU.mult).then_inc(w_ready, 1)

            def normalise(c):
                v.wait_ge(w_exp, c + 1)
                at = slice(c * GATHER_CHUNK, (c + 1) * GATHER_CHUNK)
                rows_c = work[:, at, :].rearrange("p t (h f) -> p t h f", h=HEADS)
                step(total(pair_b[:, at, :], rows_c))
                step(v.reciprocal(pair_b[:, at, :], pair_b[:, at, :]))
                step(tt(rows_c, rows_c, bcast(pair_b[:, at, :], FEAT), ALU.mult))
                tt(A_msg[:, at, :], work[:, at, 0:FEAT], work[:, at, FEAT:HF], ALU.add).then_inc(msg_ready, 1)

            in_turn(weigh, normalise)
            v.wait_ge(msg_out, CHUNKS)
            sums(A_sum, A_msg)

            def center(c):
                at = slice(c * GATHER_CHUNK, (c + 1) * GATHER_CHUNK)
                step(tt(A_tmp[:, at, :], A_sum[:, at, :], A_dst[:, at, :], ALU.add))
                step(total(stat[:, at], A_tmp[:, at, :]))
                step(ts(stat[:, at], stat[:, at], -1.0 / FEAT, ALU.mult))
                done(tt(A_tmp[:, at, :], A_tmp[:, at, :], bcast(stat[:, at], FEAT), ALU.add), f_centered, c + 1)

            def scale(c):
                at = slice(c * GATHER_CHUNK, (c + 1) * GATHER_CHUNK)
                v.wait_ge(f_squared, c + 1)
                total(stat[:, at], A_sum[:, at, :]).then_inc(f_var, 1)
                v.wait_ge(f_std, c + 1)
                step(v.reciprocal(std[:, at], std[:, at]))
                tt(A_tmp[:, at, :], A_tmp[:, at, :], bcast(std[:, at], FEAT), ALU.mult).then_inc(final_ready, 1)

            in_turn(center, scale)


_INPUTS = ["x", "src", "dst", "edge_attr3_2x32", "edge_attr_3", "edge_attr_32", "edge_weight",
           "L0_gnn_w1", "L0_gnn_b1", "L0_gnn_w2", "L0_gnn_b2", "L2_gnn_W1", "L2_gnn_b1", "L2_gnn_W2", "L2_gnn_b2",
           "L3_gnn_W1", "L3_gnn_b1", "L3_gnn_W2s", "L3_gnn_b2s", "L3_gnn_W2d", "L3_gnn_b2d", "L3_gnn_attn"]


def kernel(**inputs):
    import numpy as np
    import concourse.bacc as bacc
    from concourse.bass_utils import run_bass_kernel_spmd

    nc = bacc.Bacc("TRN2", target_bir_lowering=False, num_devices=1)
    arrays, args = {}, []
    for name in _INPUTS:
        a = np.ascontiguousarray(inputs[name])
        arrays[f"in_{name}"] = a
        args.append(nc.dram_tensor(f"in_{name}", a.shape, mybir.dt.from_np(a.dtype), kind="ExternalInput").ap())
    out = nc.dram_tensor("out_0", (N_NODES, FEAT), mybir.dt.float32, kind="ExternalOutput").ap()
    gnn_kernel(nc, *args, out)
    return run_bass_kernel_spmd(nc, [arrays], core_ids=[0]).results[0]["out_0"]
```

```python
from contextlib import ExitStack
from math import pi, sqrt

import concourse.bass as bass
from concourse import mybir

N_NODES, FEAT = 100000, 32
N_EDGES = 25000
P = 128
T = -(-N_EDGES // P)
E_PAD = P * T
FULL = N_EDGES // T
REST = N_EDGES - FULL * T
LOG_LO = 7
HI = -(-(N_NODES >> LOG_LO) // 16) * 16
PAD_DST, PAD_NEXT = 131071, 131070
SKIP = 1 << 20
HID0, PATHS = 64, 384
HEADS, HF = 2, 64
EPS = 1e-5
BIG = 1e38
NEG_SLOPE = 0.2
ENDS = 8
FEW = 64
FEWEST = 60
TOP = -(-T // 8) * 8
SLOTS = 2

Y0, C1 = 0.5 / sqrt(pi), sqrt(3 / (4 * pi))
K1, K2 = C1 / sqrt(6), sqrt(3 / (8 * pi))
NORM0, NORM1 = sqrt(4 * pi) / sqrt(16), sqrt(4 * pi) * sqrt(3) / sqrt(32)

GATHER_CHUNK = 28
CHUNKS = T // GATHER_CHUNK
SHORT_AFTER = 5
HIST_UNITS = GATHER_CHUNK // 2
HIST_SLOTS = HIST_UNITS // 2
QUADS = T // 4
MSG = GATHER_CHUNK * FEAT
TABLE_PARTS = [CHUNKS, 1, 1, CHUNKS, CHUNKS]


def parts_until(k):
    return sum(TABLE_PARTS[:k + 1])

D_ROWS = 60
D_CHUNKS = N_NODES // (P * D_ROWS)
D_TAIL = N_NODES - D_CHUNKS * P * D_ROWS
TAIL_P, TAIL_ROWS = D_TAIL // 4, 4
NODE_STEPS = 11
N_WEIGHT_LOADS = 20
UNIT_ROWS = 12
D_UNITS = D_ROWS // UNIT_ROWS


def gnn_kernel(nc, x, src, dst, r_feat, rel, edge_attr, edge_weight, w1, b1, w2, b2,
               m_w1, m_b1, m_w2, m_b2, g_w1, g_b1, g_w2s, g_b2s, g_w2d, g_b2d, attn, out):
    f32, i32, f16 = mybir.dt.float32, mybir.dt.int32, mybir.dt.float16
    ALU, ACT, AX = mybir.AluOpType, mybir.ActivationFunctionType, mybir.AxisListType.X

    with ExitStack() as ctx:
        def sb(name, shape, dt=f32):
            return ctx.enter_context(nc.sbuf_tensor(name, shape, dt))

        def sem(name):
            return ctx.enter_context(nc.semaphore(name))

        def dram(name, shape, dt=f32):
            return nc.dram_tensor(name, shape, dt).ap()

        pos_table = dram("pos_table", (HI * P, 1), i32)
        short_rows = dram("short_rows", (E_PAD, 1), i32)
        edge_sums = dram("edge_sums", (E_PAD, FEAT))
        tables = [dram(f"table_{k}", (E_PAD, FEAT)) for k in range(5)]

        A_dst = sb("A_dst", [P, T, FEAT])
        A_src = sb("A_src", [P, T, FEAT])
        A_msg = sb("A_msg", [P, T, FEAT])
        A_sum = sb("A_sum", [P, T, FEAT])
        A_tmp = sb("A_tmp", [P, T, FEAT])
        work = sb("work", [P, T, HF])
        work_flat = work[:].rearrange("p t f -> p (t f)")

        tmp_flat = A_tmp[:].rearrange("p t f -> p (t f)")

        def carver(of):
            at = [0]

            def carve(parts, *dims, dt=f32):
                n = 1
                for d in dims:
                    n *= d
                words = n if dt in (f32, i32) else n // 2
                view = of[0:parts, at[0]:at[0] + words]
                at[0] += words
                assert at[0] <= of.shape[1]
                if dt is not f32:
                    view = view.bitcast(dt)
                if len(dims) == 2:
                    view = view.rearrange("p (a b) -> p a b", b=dims[1])
                if len(dims) == 3:
                    view = view.rearrange("p (a b c) -> p a b c", b=dims[1], c=dims[2])
                return view
            return carve

        src_i = sb("src_i", [P, T], i32)
        dst_i = sb("dst_i", [P, T], i32)
        nxt_i = sb("nxt_i", [P, T], i32)
        pos_i = sb("pos_i", [P, T], i32)
        out_i = sb("out_i", [P, T], i32)
        ew = sb("ew", [P, T + 4])
        dst_f = sb("dst_f", [P, T])
        is_last = sb("is_last", [P, T])
        not_last = sb("not_last", [P, T])
        same = sb("same", [P, T])
        same_pen = sb("same_pen", [P, T])
        in_first = sb("in_first", [P, T])
        in_first_pen = sb("in_first_pen", [P, T])
        in_final = sb("in_final", [P, T])
        dinv = sb("dinv", [P, T])
        stat = sb("stat", [P, T])
        std = sb("std", [P, T])
        r3 = sb("r3", [P, T])
        small = sb("small", [P, 4, T])
        small2 = sb("small2", [P, 4, T])
        idx_short = nxt_i
        idx_next = sb("idx_next", [P, T], i32)
        out_short = sb("out_short", [P, T], i32)
        same_short, in_first_short, dinv_short = small[:, 1, :], small[:, 2, :], small[:, 3, :]
        n_short = sb("n_short", [1, 1], i32)
        row_base = sb("row_base", [P, 1])
        n_ends = sb("n_ends", [1, 1], i32)

        ident = sb("ident", [P, P])
        ones = sb("ones", [P, 32])
        eps_t = sb("eps_t", [P, 1])
        rows = sb("rows", [32, 8, P])
        diag = sb("diag", [P, P])
        seam_state = sb("seam_state", [32, P])
        seam_shift = sb("seam_shift", [32, P])
        carry = sb("carry", [P, 32])
        end_col = sb("end_col", [P, 32])

        w2fold = sb("w2fold", [HID0 + 1, PATHS])
        w1rep = sb("w1rep", [P, HID0 + 1])
        b1col = sb("b1col", [HID0 + 1, 1])
        mw1 = sb("mw1", [96, HID0])
        mb1 = sb("mb1", [HID0, 1])
        mw2 = sb("mw2", [HID0 + 1, FEAT])
        gw2 = sb("gw2", [HF + 1, 2 * HF])
        gtmp = sb("gtmp", [HF + 1, HF])
        attn_rep = sb("attn_rep", [P, HF])
        gw1 = sb("gw1", [P, P])
        gw3 = sb("gw3", [HF + 1, FEAT])
        gb1 = sb("gb1", [P, FEAT])
        gb1c = sb("gb1c", [P, FEAT])
        nodes_w = sb("nodes_w", [P, 2 * P])
        nodes_t = sb("nodes_t", [P, P])
        zero_hot = sb("zero_hot", [P, P], f16)

        banks = [ctx.enter_context(nc.psum_tensor(f"bank_{b}", [P, 512], f32)) for b in range(8)]

        loaded_dst, loaded_src, loaded_edges = sem("loaded_dst"), sem("loaded_src"), sem("loaded_edges")
        loaded_w, pads_ready = sem("loaded_w"), sem("pads_ready")
        pool_seq, consts_ready, dve_seq = sem("pool_seq"), sem("consts_ready"), sem("dve_seq")
        src_rows = [sem(f"src_rows_{c}") for c in range(CHUNKS)]
        dst_rows = [sem(f"dst_rows_{c}") for c in range(CHUNKS)]
        pos_rows = sem("pos_rows")
        var_ready, std_ready = sem("var_ready"), sem("std_ready")
        centered, squared = sem("centered"), sem("squared")
        ends_ready, ends_turned = sem("ends_ready"), sem("ends_turned")
        carry_ready, carry_turned = sem("carry_ready"), sem("carry_turned")
        onehots_ready, onehots_used = sem("onehots_ready"), sem("onehots_used")
        digits_ready, lo_seq, lo_ready = sem("digits_ready"), sem("lo_seq"), sem("lo_ready")
        count_copied, pos_f_ready = sem("count_copied"), sem("pos_f_ready")
        counted, summed = sem("counted"), sem("summed")
        pos_turned, pos_int, pos_stored = sem("pos_turned"), sem("pos_int"), sem("pos_stored")
        weights_folded, cw_done = sem("weights_folded"), sem("cw_done")
        pre_ready, pre_turned = sem("pre_ready"), sem("pre_turned")
        hid_ready, radial_ready, radial_used = sem("hid_ready"), sem("radial_ready"), sem("radial_used")
        table_ready, table_stored = sem("table_ready"), sem("table_stored")
        gather_ok = sem("gather_ok")
        zeros_stored, count_ready, count_turned = sem("zeros_stored"), sem("count_ready"), sem("count_turned")
        short_ready, short_stored = sem("short_ready"), sem("short_stored")
        few_done, more_done, rest_done = sem("few_done"), sem("more_done"), sem("rest_done")
        short_in = sem("short_in")
        acc_ready = sem("acc_ready")
        sums_in = [sem(f"sums_in_{c}") for c in range(CHUNKS)]
        n_loaded = [sem(f"n_loaded_{s}") for s in range(SLOTS)]
        n_turned, n_xt, n_mm = sem("n_turned"), sem("n_xt"), sem("n_mm")
        n_bank = sem("n_bank")
        n_var, n_std, n_z, n_zsq, n_out = sem("n_var"), sem("n_std"), sem("n_z"), sem("n_zsq"), sem("n_out")
        n_stored = [sem(f"n_stored_{s}") for s in range(SLOTS)]
        ea_in = sem("ea_in")
        e_cat, e_catd, e_turned, e_catT = sem("e_cat"), sem("e_catd"), sem("e_turned"), sem("e_catT")
        e_h, e_hT, e_v, e_vused = sem("e_h"), sem("e_hT"), sem("e_v"), sem("e_vused")
        a_cat, a_turned, a_catT, a_mm = sem("a_cat"), sem("a_turned"), sem("a_catT"), sem("a_mm")
        a_act, a_used = sem("a_act"), sem("a_used")
        quad_rows = [[sem(f"quad_rows_{k}_{s}") for s in range(SLOTS)] for k in (3, 4)]
        rf_in = [sem(f"rf_in_{s}") for s in range(SLOTS)]
        exp_req, exp_done = sem("exp_req"), sem("exp_done")
        res_mm, res_used = sem("res_mm"), sem("res_used")
        w_ready, w_exp = sem("w_ready"), sem("w_exp")
        msg_ready, msg_turned, msg_T = sem("msg_ready"), sem("msg_turned"), sem("msg_T")
        msg_mm, msg_out = sem("msg_mm"), sem("msg_out")
        f_centered, f_squared, f_var, f_std = sem("f_centered"), sem("f_squared"), sem("f_var"), sem("f_std")
        prod_used, node_seq, a_weighed = sem("prod_used"), sem("node_seq"), sem("a_weighed")
        a_leaky = sem("a_leaky")
        final_ready, scattered = sem("final_ready"), sem("scattered")

        cv = carver(A_msg[:].rearrange("p t f -> p (t f)"))
        hi_hot = cv(P, HIST_SLOTS * 2, HI, dt=f16)
        cv = carver(A_sum[:].rearrange("p t f -> p (t f)"))
        lo_hot = cv(P, HIST_SLOTS * 2, P, dt=f16)
        lo_far = cv(P, HIST_SLOTS, P, dt=f16)

        cv = carver(work_flat)
        iota16 = cv(P, HI, dt=f16)
        pre = cv(P, SLOTS, 2, HID0 + 1)
        hidT = cv(HID0 + 1, SLOTS, 2 * P)
        prod = cv(P, 4, 640)
        path_sums = cv(P, GATHER_CHUNK, 64)
        ff = cv(P, GATHER_CHUNK, 16)
        g5 = cv(P, GATHER_CHUNK, 8, 5)
        vec_a = cv(P, GATHER_CHUNK, 24)
        cv = carver(work_flat)
        n_x = cv(P, SLOTS, D_ROWS, FEAT)
        n_o = cv(P, SLOTS, D_ROWS, FEAT)
        n_q = cv(P, SLOTS, D_ROWS, FEAT)
        n_s = cv(P, SLOTS * 4, D_ROWS)
        n_xT = small2[:].rearrange("p a t -> p (a t)")[:, 0:SLOTS * 3 * P].rearrange("p (s w) -> p s w", s=SLOTS)
        cv = carver(A_sum[:].rearrange("p t f -> p (t f)"))
        keys, top, top_i = cv(P, 3, T), cv(P, 3, TOP), cv(P, 3, TOP, dt=i32)
        kept, run, before, run_end, spare = cv(P, T), cv(P, T), cv(P, T), cv(P, T), cv(P, TOP)
        flag, short_row_i = cv(P, TOP), cv(P, T, dt=i32)
        cv = carver(tmp_flat)
        deg, left = cv(P, T), cv(P, T)
        unit = cv(P, T, 5)
        w2raw = cv(HID0 + 1, PATHS)
        node_words = cv(P, 2 * HI)
        node_count, pos_f = node_words[:, 0:HI], node_words[:, HI:2 * HI]
        pos_int_t = node_words[:, 0:7 * P].bitcast(i32).rearrange("p (k l) -> p k l", l=P)
        pos_run, pos_spare = cv(P, HI), cv(P, HI)
        upto, all_ones = cv(P, P), cv(P, P)
        hi_digit, lo_digit, minus_lo = cv(P, T), cv(P, T), cv(P, T)
        cv = carver(work_flat)
        cat = cv(P, SLOTS, 4, 96)
        catT = cv(96, SLOTS, 4 * P)
        hidT2 = cv(HID0 + 1, SLOTS, 4 * P)
        cv = carver(tmp_flat)
        cat3 = cv(P, SLOTS, 4, HF + 1)
        catT3 = cv(HF + 1, SLOTS, 4 * P)
        rf = cv(P, SLOTS, 4, HF)
        leaky = cv(P, SLOTS, 4, HF)
        cv = carver(A_src[:].rearrange("p t f -> p (t f)"))
        msgT = cv(P, SLOTS, GATHER_CHUNK * FEAT)

        edge_no = small2[:, 0, :].bitcast(i32)

        def triple(ap):
            return ap.rearrange("p a t -> p (a t)").rearrange("p (t a) -> p t a", a=3)

        rel_t, rel_sq = triple(small[:, 0:3, :]), triple(small2[:, 1:4, :])

        def pair(ap):
            return ap.rearrange("p a t -> p (a t)").rearrange("p (t h) -> p t h", h=HEADS)

        pair_a, pair_b = pair(small[:, 0:2, :]), pair(small[:, 2:4, :])
        pair_c, pair_d = pair(small2[:, 0:2, :]), pair(small2[:, 2:4, :])

        def flat(ap):
            return ap.rearrange("p a b -> p (a b)")

        def bcast(ap, n):
            return ap.unsqueeze(len(ap.shape)).to_broadcast(list(ap.shape) + [n])

        def mid(ap, n):
            return ap.unsqueeze(1).to_broadcast([ap.shape[0], n, ap.shape[1]])

        main = "(p t) -> p t"
        main3 = "(p t) f -> p t f"

        def pipeline(eng, *steps, after={}):
            lag = len(steps) - 1

            def turn(i, parity):
                for k, step in enumerate(steps):
                    if step is None or isinstance(i, int) and not 0 <= i - k < QUADS:
                        continue
                    step(i - k, (parity - k) % SLOTS)

            i = 0
            while i < QUADS + lag:
                end = min([t for t in after if t >= i] + [QUADS - 1]) + 1
                pairs = (end - i) // 2
                if i > lag and i % 2 == 0 and pairs > 1:
                    with eng.Fori(i // 2, i // 2 + pairs) as pair:
                        turn(pair * 2, 0)
                        turn(pair * 2 + 1, 1)
                    i += 2 * pairs
                else:
                    turn(i, i % 2)
                    i += 1
                for step in after.get(i - 1, ()):
                    step()

        def chunk(a, c):
            return a[:, c * GATHER_CHUNK:(c + 1) * GATHER_CHUNK]

        LAST_ORDER = [*range(1, CHUNKS), 0]

        def in_turn(*steps):
            for i in range(CHUNKS + len(steps) - 1):
                for k, step in enumerate(steps):
                    if 0 <= i - k < CHUNKS:
                        step(i - k)

        def staggered(*steps):
            for i in range(max(lag + times for _, lag, times in steps)):
                for step, lag, times in steps:
                    if 0 <= i - lag < times:
                        step(i - lag)

        NODE_PAIRS = [(0, 2, False), (2, 4, False), (4, 6, False), (6, D_CHUNKS // 2, True)]
        assert D_CHUNKS % 2 == 1 and D_UNITS % 2 == 1

        def node_chunks(eng, body, first, last, tail):
            if first == 0:
                body(0, 0, 0, P, D_ROWS)
                body(1, 0, 1, P, D_ROWS)
                first = 1
            if last > first:
                with eng.Fori(first, last) as i:
                    body(i * 2, i, 0, P, D_ROWS)
                    body(i * 2 + 1, i, 1, P, D_ROWS)
            if tail:
                body(D_CHUNKS - 1, D_CHUNKS // 2, 0, P, D_ROWS)
                body(D_CHUNKS, D_CHUNKS // 2, 1, TAIL_P, TAIL_ROWS)

        def node_rows(ap, c, parts):
            if parts == P:
                return ap[bass.ds(c * (P * D_ROWS), P * D_ROWS), :].rearrange("(p r) f -> p r f", p=P)
            return ap[D_CHUNKS * P * D_ROWS:N_NODES, :].rearrange("(p r) f -> p r f", p=parts)

        def node_units(slot, n_rows):
            if n_rows == TAIL_ROWS:
                return [(0, slot, TAIL_ROWS)]
            return [(j, (slot + j) % SLOTS, UNIT_ROWS) for j in range(D_UNITS)]

        block = ctx.enter_context(nc.Block())

        @block.sync
        def _(sp):
            sp.wait_ge(pads_ready, 1)
            for tile, ap, off, done in ((src_i, src, 0, loaded_src), (dst_i, dst, 0, loaded_dst),
                                        (nxt_i, dst, 1, loaded_dst)):
                n = REST - off
                sp.dma_start(tile[0:FULL, :], ap[off:off + FULL * T].rearrange(main, t=T)).then_inc(done, 16)
                sp.dma_start(tile[FULL:FULL + 1, 0:n],
                             ap[off + FULL * T:off + FULL * T + n].rearrange("(p t) -> p t", p=1)).then_inc(done, 16)
            sp.dma_start(ew[0:FULL, 0:T], edge_weight[0:FULL * T].rearrange(main, t=T)).then_inc(loaded_edges, 16)
            sp.dma_start(ew[FULL:FULL + 1, 0:REST],
                         edge_weight[FULL * T:N_EDGES].rearrange("(p t) -> p t", p=1)).then_inc(loaded_edges, 16)
            sp.dma_start(rel_t[0:FULL], rel[0:FULL * T, :].rearrange(main3, t=T)).then_inc(loaded_edges, 16)
            sp.dma_start(rel_t[FULL:FULL + 1, 0:REST],
                         rel[FULL * T:N_EDGES, :].rearrange("(p t) f -> p t f", p=1)).then_inc(loaded_edges, 16)
            sp.wait_ge(gather_ok, 1)
            for zeroed in (edge_sums, tables[1], tables[2]):
                sp.dma_start(zeroed.rearrange(main3, t=T), A_dst[:]).then_inc(zeros_stored, 16)
            sp.wait_ge(pads_ready, 2)
            row, col = "(a b) -> a b", "(a b) -> a b"
            for to, of in (
                (w2raw[0:HID0, :], w2), (w2raw[HID0:HID0 + 1, :], b2.rearrange(row, a=1)),
                (w1rep[:, 0:HID0], w1[0, :].partition_broadcast(P)), (b1col[0:HID0, :], b1.rearrange(col, b=1)),
                (mw1[:], m_w1), (mb1[:], m_b1.rearrange(col, b=1)),
                (mw2[0:HID0, :], m_w2), (mw2[HID0:HID0 + 1, :], m_b2.rearrange(row, a=1)),
                (gw2[0:32, 0:HF], g_w2s), (gw2[0:32, HF:2 * HF], g_w2s), (gw2[32:64, HF:2 * HF], g_w2d),
                (gw2[HF:HF + 1, 0:HF], g_b2s.rearrange(row, a=1)),
                (gw2[HF:HF + 1, HF:2 * HF], g_b2s.rearrange(row, a=1)),
                (gtmp[HF:HF + 1, :], g_b2d.rearrange(row, a=1)),
                (attn_rep[:], attn[0].rearrange("h f -> (h f)").partition_broadcast(P)),
                (gb1[:], g_b1.partition_broadcast(P)),
                *((gw1[32 * k:32 * k + 32, 32 * k:32 * k + 32], g_w1) for k in range(4)),
            ):
                sp.dma_start(to, of).then_inc(loaded_w, 16)

            sp.wait_ge(pos_int, 1)
            table = pos_table.rearrange("(h l) a -> h (l a)", l=P)
            whole = HI // P
            sp.dma_start(table[0:whole * P, :].rearrange("(k p) l -> p k l", p=P),
                         pos_int_t[:, 0:whole, :]).then_inc(pos_stored, 16)
            sp.dma_start(table[whole * P:HI, :], pos_int_t[0:HI - whole * P, whole, :]).then_inc(pos_stored, 16)

            def exchange(k, of, order=range(CHUNKS)):
                for i, c in enumerate(order):
                    sp.wait_ge(table_ready, parts_until(k) - CHUNKS + i + 1)
                    sp.dma_start(chunk(tables[k].rearrange(main3, t=T), c), chunk(of, c)).then_inc(table_stored, 16)

            def load_nodes(c, half, slot, parts, n_rows):
                sp.wait_ge(n_turned, c * D_UNITS + D_UNITS)
                sp.dma_start(n_x[0:parts, slot, 0:n_rows, :], node_rows(x, c, parts)).then_inc(n_loaded[slot], 16)

            sp.wait_ge(short_ready, 1)
            sp.dma_start(short_rows.rearrange("(p t) a -> p (t a)", t=T), short_row_i).then_inc(short_stored, 16)
            n = sp.value_load(n_short[0:1, 0:1], min_val=0, max_val=T)

            sp.wait_ge(gather_ok, 2)
            node_chunks(sp, load_nodes, 0, 1, False)
            exchange(0, A_tmp)
            ahead = [1] + [last + 1 for _, last, _ in NODE_PAIRS[:2]] + [D_CHUNKS // 2]
            node_chunks(sp, load_nodes, ahead[0], ahead[1], False)
            for k in (1, 2):
                sp.wait_ge(table_ready, parts_until(k))
                table = tables[k].rearrange(main3, t=T)
                with sp.If(n > FEW):
                    sp.dma_start(table, A_sum[:]).then_inc(table_stored, 16)
                with sp.Else():
                    sp.dma_start(table[:, 0:FEW, :], A_sum[:, 0:FEW, :]).then_inc(table_stored, 16)
                node_chunks(sp, load_nodes, ahead[k], ahead[k + 1], k == 2)
            sp.wait_ge(short_in, 5)
            for c in range(CHUNKS):
                sp.dma_start(chunk(A_msg, c), chunk(edge_sums.rearrange(main3, t=T), c)).then_inc(sums_in[c], 16)
            sp.dma_start(A_tmp[0:FULL], edge_attr[0:FULL * T, :].rearrange(main3, t=T)).then_inc(ea_in, 16)
            sp.dma_start(A_tmp[FULL:FULL + 1, 0:REST, :],
                         edge_attr[FULL * T:N_EDGES, :].rearrange("(p t) f -> p t f", p=1)).then_inc(ea_in, 16)
            exchange(3, A_dst)
            exchange(4, A_dst, LAST_ORDER)

            edges = r_feat.rearrange("e h f -> e (h f)")

            def load_rf(q, slot, rest_row):
                sp.wait_ge(a_used, q + 1)
                sp.dma_start(rf[0:FULL, slot], edges[0:FULL * T, :].rearrange("(p t) f -> p t f", t=T)
                             [:, bass.ds(q * 4, 4), :]).then_inc(rf_in[slot], 16)
                sp.dma_start(rf[FULL:P, slot], edges[bass.ds(rest_row, 4), :].rearrange("(p t) f -> p t f", p=1)
                             ).then_inc(rf_in[slot], 16)

            true_quads = REST // 4
            assert REST % 4 == 0 and true_quads % 2 == 1 and QUADS % 2 == 1
            with sp.Fori(0, true_quads // 2) as i:
                for slot in range(SLOTS):
                    load_rf(i * 2 + slot, slot, i * 8 + (FULL * T + 4 * slot))
            load_rf(true_quads - 1, 0, N_EDGES - 4)
            load_rf(true_quads, 1, 0)
            with sp.Fori((true_quads + 1) // 2, QUADS // 2) as i:
                for slot in range(SLOTS):
                    load_rf(i * 2 + slot, slot, 0)
            load_rf(QUADS - 1, 0, 0)
            sp.wait_ge(scattered, 16 * T)

        @block.gpsimd
        def _(pool):
            pool.memset(src_i[:], SKIP)
            pool.memset(dst_i[:], PAD_DST)
            pool.memset(nxt_i[:], PAD_NEXT)
            pool.memset(ew[:], 0.0)
            pool.memset(small[:], 1.0).then_inc(pads_ready, 1)
            pool.memset(w1rep[:], 0.0)
            pool.memset(b1col[:], 1.0)
            pool.memset(gw2[:], 0.0)
            pool.memset(gw1[:], 0.0)
            pool.memset(A_src[:, REST:T, :], 0.0).then_inc(pads_ready, 1)
            pool.memset(pos_i[:], SKIP)
            pool.memset(ones[:], 1.0)
            pool.memset(eps_t[:], EPS)
            pool.memset(zero_hot[:], 0.0)
            pool.memset(all_ones, 1.0)
            pool.memset(upto, 1.0)
            pool.memset(ident[:], 0.0).then_inc(pool_seq, 1)
            pool.wait_ge(pool_seq, 1)
            pool.affine_select(out=ident[:], in_=ident[:], compare_op=ALU.not_equal, fill=1.0, base=0,
                               pattern=[[-1, P]], channel_multiplier=1)
            pool.affine_select(out=upto, in_=upto, compare_op=ALU.is_ge, fill=0.0, base=0,
                               pattern=[[1, P]], channel_multiplier=-1)
            pool.iota(left, pattern=[[-1, T]], base=T, channel_multiplier=0, allow_small_or_imprecise_dtypes=True)
            pool.iota(edge_no, pattern=[[1, T]], base=1, channel_multiplier=T)
            pool.iota(iota16, pattern=[[1, HI]], base=0, channel_multiplier=0,
                      allow_small_or_imprecise_dtypes=True).then_inc(consts_ready, 1)

            def gather(column, of, idx, limit, done, columns=range(T)):
                for t in columns:
                    pool.indirect_dma_start(
                        out=column(t), out_offset=None, in_=of,
                        in_offset=bass.IndirectOffsetOnAxis(ap=idx[:, t:t + 1], axis=0),
                        bounds_check=limit, oob_is_err=False).then_inc(done(t), 16)

            pool.wait_ge(loaded_src, 32)
            pool.wait_ge(pads_ready, 2)
            gather(lambda t: A_src[:, t, :], x, src_i, N_NODES - 1, lambda t: src_rows[t // GATHER_CHUNK])
            pool.wait_ge(pos_stored, 32)
            gather(lambda t: pos_i[:, t:t + 1], pos_table, src_i, N_NODES - 1, lambda t: pos_rows)
            pool.wait_ge(loaded_dst, 64)
            pool.wait_ge(zeros_stored, 48)
            gather(lambda t: A_dst[:, t, :], x, dst_i, N_NODES - 1, lambda t: dst_rows[t // GATHER_CHUNK])

            pool.wait_ge(short_ready, 1)
            n = pool.value_load(n_short[0:1, 0:1], min_val=0, max_val=T)
            turns = [0]

            def short_columns(move):
                turns[0] += 1
                for t in range(FEWEST):
                    move(t).then_inc(few_done, 16)
                with pool.If(n > FEWEST):
                    for t in range(FEWEST, FEW):
                        move(t).then_inc(more_done, 16)
                    pool.wait_ge(more_done, 16 * (FEW - FEWEST) * turns[0])
                with pool.If(n > FEW):
                    for t in range(FEW, T):
                        move(t).then_inc(rest_done, 16)
                    pool.wait_ge(rest_done, 16 * (T - FEW) * turns[0])
                pool.wait_ge(few_done, 16 * FEWEST * turns[0])
                pool.sem_inc(short_in, 1)

            def take_short(column, of, idx):
                return lambda t: pool.indirect_dma_start(
                    out=column(t), out_offset=None, in_=of,
                    in_offset=bass.IndirectOffsetOnAxis(ap=idx[:, t:t + 1], axis=0),
                    bounds_check=E_PAD - 1, oob_is_err=False)

            for k in range(3):
                pool.wait_ge(table_stored, 16 * parts_until(k))
                pool.wait_ge(gather_ok, k + 2)
                short_columns(take_short(lambda t: A_msg[:, t, :], tables[k], idx_next if k else idx_short))
                if k == 0:
                    pool.wait_ge(short_stored, 16)
                    short_columns(take_short(lambda t: idx_next[:, t:t + 1], short_rows, idx_short))
            pool.wait_ge(acc_ready, 1)
            short_columns(lambda t: pool.indirect_dma_start(
                out=edge_sums, out_offset=bass.IndirectOffsetOnAxis(ap=out_short[:, t:t + 1], axis=0),
                in_=A_tmp[:, t, :], in_offset=None, bounds_check=E_PAD - 1, oob_is_err=False))
            for k in (3, 4):
                pool.wait_ge(table_stored, 16 * parts_until(k))
                pool.wait_ge(gather_ok, k + 2)
                for q in range(QUADS):
                    here = quad_rows[k - 3][q % SLOTS]
                    if q >= SLOTS:
                        pool.wait_ge(here, 64 * (q // SLOTS))
                    gather(lambda t: A_src[:, t, :], tables[k], pos_i, E_PAD - 1, lambda t: here,
                           range(4 * q, 4 * q + 4))
            for slot in range(SLOTS):
                pool.wait_ge(n_stored[slot], 16 * (D_CHUNKS // 2 + 1))
            for i, c in enumerate(LAST_ORDER):
                pool.wait_ge(final_ready, i + 1)
                for t in range(c * GATHER_CHUNK, (c + 1) * GATHER_CHUNK):
                    pool.indirect_dma_start(
                        out=out, out_offset=bass.IndirectOffsetOnAxis(ap=out_i[:, t:t + 1], axis=0),
                        in_=A_tmp[:, t, :], in_offset=None, bounds_check=N_NODES - 1,
                        oob_is_err=False).then_inc(scattered, 16)

        @block.scalar
        def _(act):
            done = {"root": 0, "square": 0, "norm": 0}

            def next_root(scale, bias=True):
                done["root"] += 1
                act.wait_ge(var_ready, done["root"])
                nc.scalar.activation(std[:], stat[:], ACT.Sqrt, scale=scale,
                                     bias=eps_t[:] if bias else 0.0).then_inc(std_ready, 1)

            def norm_steps(of, squares=A_sum, order=range(CHUNKS)):
                base = done["norm"] * CHUNKS
                done["norm"] += 1

                def square(i):
                    act.wait_ge(f_centered, base + i + 1)
                    nc.scalar.activation(chunk(squares, order[i]), chunk(of, order[i]), ACT.Square).then_inc(f_squared, 1)

                def take_root(i):
                    act.wait_ge(f_var, base + i + 1)
                    nc.scalar.activation(chunk(std, order[i]), chunk(stat, order[i]), ACT.Sqrt, scale=1.0 / FEAT,
                                         bias=eps_t[:]).then_inc(f_std, 1)

                return square, take_root

            def norm(of):
                in_turn(*norm_steps(of))

            def next_square(of):
                done["square"] += 1
                act.wait_ge(centered, done["square"])
                nc.scalar.activation(A_sum[:], of[:], ACT.Square).then_inc(squared, 1)

            act.wait_ge(consts_ready, 1)
            next_root(1.0, bias=False)
            next_root(1.0, bias=False)

            act.wait_ge(digits_ready, 1)
            with act.Fori(0, T // GATHER_CHUNK) as i:
                for k in range(HIST_UNITS):
                    slot = k % HIST_SLOTS
                    act.wait_ge(onehots_used, i * HIST_UNITS + (k + 1))
                    t = bass.ds(i * GATHER_CHUNK + (2 * k + 1), 1)
                    far = lo_far[:, slot, :]
                    nc.scalar.activation(far, iota16[:, 0:P], ACT.Abs, bias=minus_lo[:, t]).then_inc(lo_seq, 1)
                    act.wait_ge(lo_seq, i * HIST_UNITS + (k + 1))
                    nc.scalar.activation(lo_hot[:, 2 * slot + 1, :], far, ACT.Relu, scale=-1.0,
                                         bias=ones[:, 0:1]).then_inc(lo_ready, 1)

            act.wait_ge(loaded_w, 16 * N_WEIGHT_LOADS)
            act.sem_inc(hid_ready, SLOTS)
            with act.Fori(0, T // 4) as i:
                for slot in range(SLOTS):
                    u = i * 2 + slot
                    act.wait_ge(pre_turned, u + (1 + SLOTS))
                    act.wait_ge(radial_ready, u + 1)
                    nc.scalar.activation(hidT[:, slot, :], banks[slot][0:HID0 + 1, 0:2 * P], ACT.Relu,
                                         bias=b1col[:]).then_inc(hid_ready, 1)

            norm(A_dst)
            next_root(1.0, bias=False)

            act.sem_inc(n_xt, SLOTS)
            act.sem_inc(n_bank, SLOTS)

            def unit_sizes(c, j):
                return c % SLOTS, P if c < D_CHUNKS else TAIL_P, c * D_UNITS + j

            def bring_rows(c, j, s, nr):
                slot, parts, u = unit_sizes(c, j)
                width = (nr // 4) * parts
                act.wait_ge(n_turned, u + (1 + SLOTS * D_UNITS))
                act.wait_ge(n_mm, u + 1)
                nc.scalar.copy(n_xT[:, s, 0:width], banks[s][:, 0:width]).then_inc(n_xt, 1)

            def take_products(c, j, s, nr):
                slot, parts, u = unit_sizes(c, j)
                n, r = nr * FEAT, j * UNIT_ROWS
                act.wait_ge(n_mm, u + (1 + SLOTS))
                nc.scalar.activation(n_q[0:parts, slot, r:r + nr, :].rearrange("p r f -> p (r f)"),
                                     banks[2 + s][0:parts, 0:n], ACT.Square)
                if j == 0 and c >= SLOTS:
                    act.wait_ge(n_stored[slot], c // SLOTS * 16)
                nc.scalar.copy(n_o[0:parts, slot, r:r + nr, :].rearrange("p r f -> p (r f)"),
                               banks[4 + s][0:parts, 0:n]).then_inc(n_bank, 1)

            def node_norms(c):
                slot = c % SLOTS
                parts, n_rows = (P, D_ROWS) if c < D_CHUNKS else (TAIL_P, TAIL_ROWS)
                var, dev = n_s[0:parts, 4 * slot, 0:n_rows], n_s[0:parts, 4 * slot + 1, 0:n_rows]

                def node_root(k, scale):
                    act.wait_ge(n_var, c * 4 + k)
                    nc.scalar.activation(dev, var, ACT.Sqrt, scale=scale, bias=eps_t[0:parts]).then_inc(n_std, 1)

                def node_square():
                    act.wait_ge(n_z, c + 1)
                    nc.scalar.activation(n_q[0:parts, slot, 0:n_rows, :], n_o[0:parts, slot, 0:n_rows, :],
                                         ACT.Square).then_inc(n_zsq, 1)

                def node_store():
                    node_root(4, 1.0 / FEAT)
                    act.wait_ge(n_out, c + 1)
                    act.dma_start(node_rows(out, c, parts), n_o[0:parts, slot, 0:n_rows, :]).then_inc(n_stored[slot], 16)

                return [lambda: node_root(1, 1.0 / FEAT), lambda: node_root(2, 1.5625),
                        lambda: node_root(3, 4.0), node_square, node_store]

            def nodes(first, last_pair, tail):
                chunks = list(range(2 * first, 2 * last_pair)) + ([D_CHUNKS - 1, D_CHUNKS] if tail else [])
                units = [(c, *unit) for c in chunks
                         for unit in node_units(c % SLOTS, D_ROWS if c < D_CHUNKS else TAIL_ROWS)]
                norms = []
                for i in range(len(units) + 1):
                    if i < len(units):
                        bring_rows(*units[i])
                    if i:
                        take_products(*units[i - 1])
                    if norms:
                        norms.pop(0)()
                    if i and (i == len(units) or units[i][0] != units[i - 1][0]):
                        norms += node_norms(units[i - 1][0])
                for part in norms:
                    part()

            for window in NODE_PAIRS:
                nodes(*window)
            next_square(A_src)
            next_root(1.0 / FEAT)
            next_root(1.5625)
            next_root(4.0)
            norm(A_dst)

            for slot in range(SLOTS):
                act.wait_ge(n_stored[slot], 16 * (D_CHUNKS // 2 + 1))
            act.sem_inc(e_catT, SLOTS)
            act.sem_inc(e_hT, SLOTS)

            def bring_src(q, slot):
                act.wait_ge(quad_rows[0][slot], q * 32 + (64 - 32 * slot))
                act.wait_ge(e_turned, q + 1)
                nc.scalar.copy(cat[:, slot, :, 0:32], A_src[:, bass.ds(q * 4, 4), :]).then_inc(e_cat, 1)

            def copy_turned(q, slot):
                act.wait_ge(e_turned, q + (1 + SLOTS))
                act.wait_ge(e_h, q + 1)
                nc.scalar.copy(catT[:, slot, :], banks[slot][0:96, :]).then_inc(e_catT, 1)

            def hidden(q, slot):
                act.wait_ge(e_h, q + (1 + SLOTS))
                act.wait_ge(e_v, q + 1)
                nc.scalar.activation(hidT2[0:HID0, slot, :], banks[2 + slot][0:HID0, :], ACT.Relu,
                                     bias=mb1[:]).then_inc(e_hT, 1)

            square, take_root = norm_steps(A_dst, A_msg, LAST_ORDER)
            n_ends_reg = act.value_load(n_ends[0:1, 0:1], min_val=0, max_val=T)
            with act.If(n_ends_reg > ENDS):
                pipeline(act, bring_src, copy_turned, hidden)
                in_turn(square, take_root)
            with act.Else():
                after = {}
                for c in range(1, CHUNKS - 1):
                    after[7 * c + 10] = [lambda i=c - 1: square(i)]
                    after[7 * c + 12] = [lambda i=c - 1: take_root(i)]
                pipeline(act, bring_src, copy_turned, hidden, after=after)
                for part in (square, take_root):
                    part(CHUNKS - 2)
                    part(CHUNKS - 1)

            act.sem_inc(a_catT, SLOTS)
            act.sem_inc(a_act, SLOTS)
            act.sem_inc(res_used, SLOTS)
            act.wait_ge(table_stored, 16 * parts_until(4))

            def copy_turned3(q, slot):
                act.wait_ge(a_turned, q + (1 + SLOTS))
                act.wait_ge(a_mm, q + 1)
                nc.scalar.copy(catT3[:, slot, :], banks[slot][0:HF + 1, :]).then_inc(a_catT, 1)

            def slope(q, slot):
                act.wait_ge(a_mm, q + (1 + SLOTS))
                act.wait_ge(a_used, q + 1)
                nc.scalar.activation(leaky[:, slot], banks[2 + slot][:].rearrange("p (t g) -> p t g", t=4)
                                     [:, :, HF:2 * HF], ACT.Copy, scale=NEG_SLOPE).then_inc(a_act, 1)
                act.wait_ge(res_mm, q + (1 + SLOTS))
                nc.scalar.copy(A_dst[:, bass.ds(q * 4, 4), :], banks[4 + slot][:, 0:P].rearrange("p (t f) -> p t f", f=FEAT)
                               ).then_inc(res_used, 1)

            pipeline(act, None, copy_turned3, slope)
            act.wait_ge(exp_req, 1)
            nc.scalar.activation(small2[:, 0:2, :], small2[:, 0:2, :], ACT.Exp).then_inc(exp_done, 1)

            def exp_chunk(c):
                act.wait_ge(w_ready, c + 1)
                nc.scalar.activation(chunk(work, c), chunk(work, c), ACT.Exp).then_inc(w_exp, 1)

            def copy_messages(c):
                act.wait_ge(msg_turned, c + 1)
                if c >= SLOTS:
                    act.wait_ge(msg_mm, c - 1)
                b = 2 * (c % SLOTS)
                nc.scalar.copy(msgT[:, c % SLOTS, 0:512], banks[b][:, :])
                nc.scalar.copy(msgT[:, c % SLOTS, 512:MSG], banks[b + 1][:, 0:MSG - 512]).then_inc(msg_T, 1)

            def take_product(c):
                act.wait_ge(msg_mm, c + 1)
                b, to = 4 + 2 * (c % SLOTS), chunk(A_msg, c).rearrange("p t f -> p (t f)")
                nc.scalar.copy(to[:, 0:512], banks[b][:, :])
                nc.scalar.copy(to[:, 512:MSG], banks[b + 1][:, 0:MSG - 512]).then_inc(msg_out, 1)

            square, take_root = norm_steps(A_tmp, A_msg, LAST_ORDER)
            with act.If(n_ends_reg > ENDS):
                in_turn(exp_chunk, copy_messages, take_product)
                in_turn(square, take_root)
            with act.Else():
                staggered((exp_chunk, 0, CHUNKS), (copy_messages, 1, CHUNKS), (take_product, 1, CHUNKS),
                          (take_root, 4, CHUNKS - 1), (square, 3, CHUNKS - 1))
                square(CHUNKS - 1)
                take_root(CHUNKS - 1)

        @block.tensor
        def _(pe):
            def turn(out_ap, in_ap, n):
                return nc.tensor.transpose(out_ap, in_ap, ident[0:n, 0:n])

            seams = {"n": 0}

            def seam(width):
                seams["n"] += 1
                pe.wait_ge(ends_ready, 3 + seams["n"])
                turn(banks[6][0:width, 0:P], end_col[:, 0:width], P).then_inc(ends_turned, 1)
                pe.wait_ge(carry_ready, seams["n"])
                turn(banks[7][:, 0:width], seam_shift[0:width, :], width).then_inc(carry_turned, 1)

            pe.wait_ge(consts_ready, 1)
            for k in range(2):
                pe.wait_ge(ends_ready, k + 1)
                nc.tensor.matmul(banks[6 + k][0:32, 0:P], ones[:], diag[:], start=True, stop=True).then_inc(ends_turned, 1)

            pe.wait_ge(ends_ready, 3)
            turn(banks[6][0:1, 0:P], end_col[:, 0:1], P).then_inc(ends_turned, 1)
            seam(1)
            seam(1)

            for k in range(2):
                pe.wait_ge(weights_folded, k + 1)
                nc.tensor.matmul(banks[4 + k][:, 0:P], nodes_t[:], nodes_w[:, 0:P], start=True, stop=True).then_inc(cw_done, 1)

            half = HI // 2
            pe.wait_ge(digits_ready, 1)
            for h in range(2):
                nc.tensor.matmul(banks[6 + h][:, 0:half], zero_hot[:], iota16[:, 0:half], start=True, stop=False)
            pe.sem_inc(onehots_used, HIST_SLOTS)
            with pe.Fori(0, T // GATHER_CHUNK) as i:
                for k in range(HIST_UNITS):
                    slot = k % HIST_SLOTS
                    pe.wait_ge(onehots_ready, i * HIST_UNITS + (k + 1))
                    pe.wait_ge(lo_ready, i * HIST_UNITS + (k + 1))
                    for j in range(2):
                        for h in range(2):
                            last = nc.tensor.matmul(banks[6 + h][:, 0:half], lo_hot[:, 2 * slot + j, :],
                                                    hi_hot[:, 2 * slot + j, h * half:(h + 1) * half],
                                                    start=False, stop=False)
                    last.then_inc(onehots_used, 1)
            for h in range(2):
                last = nc.tensor.matmul(banks[6 + h][:, 0:half], zero_hot[:], iota16[:, 0:half], start=False, stop=True)
            last.then_inc(counted, 1)
            pe.wait_ge(count_copied, 1)
            for h in range(2):
                of = node_count[:, h * half:(h + 1) * half]
                nc.tensor.matmul(banks[2 + h][:, 0:half], upto, of, start=True, stop=True)
                last = nc.tensor.matmul(banks[4 + h][:, 0:half], all_ones, of, start=True, stop=True)
            last.then_inc(summed, 1)
            pe.wait_ge(pos_f_ready, 1)
            for k in range(7):
                n = min(P, HI - k * P)
                last = turn(banks[4 + k // 4][0:n, (k % 4) * P:(k % 4 + 1) * P], pos_f[:, k * P:k * P + n], P)
            last.then_inc(pos_turned, 1)

            pe.sem_inc(pre_turned, SLOTS)
            pe.sem_inc(radial_ready, SLOTS)
            pe.wait_ge(pos_int, 1)

            def turn_pre(u, slot):
                pe.wait_ge(pre_ready, u + 1)
                pe.wait_ge(hid_ready, u + 1)
                for j in range(2):
                    last = turn(banks[slot][0:HID0 + 1, j * P:(j + 1) * P], pre[:, slot, j, :], P)
                last.then_inc(pre_turned, 1)

            turn_pre(0, 0)
            turn_pre(1, 1)

            def radial_pair(i):
                for slot in range(SLOTS):
                    u = i * 2 + slot
                    pe.wait_ge(hid_ready, u + (1 + SLOTS))
                    pe.wait_ge(radial_used, u + 1)
                    for j in range(2):
                        last = nc.tensor.matmul(banks[2 + 2 * slot + j][:, 0:PATHS], hidT[:, slot, j * P:(j + 1) * P],
                                                w2fold[:], start=True, stop=True)
                    last.then_inc(radial_ready, 1)
                for slot in range(SLOTS):
                    turn_pre(i * 2 + (2 + slot), slot)

            with pe.Fori(0, SHORT_AFTER * GATHER_CHUNK // 4) as i:
                radial_pair(i)
            pe.wait_ge(count_ready, 1)
            turn(banks[6][0:1, 0:P], spare[:, 0:1], P).then_inc(count_turned, 1)
            with pe.Fori(SHORT_AFTER * GATHER_CHUNK // 4, QUADS) as i:
                radial_pair(i)
            seam(32)

            pe.sem_inc(n_mm, SLOTS)
            pe.sem_inc(n_turned, SLOTS * D_UNITS)

            def nodes(c, half, slot, parts, n_rows):
                pe.wait_ge(n_loaded[slot], half * 16 + 16)
                units = node_units(slot, n_rows)

                def turn_rows(j, s, nr):
                    pe.wait_ge(n_xt, c * D_UNITS + (j + 1))
                    for k in range(nr // 4):
                        r = j * UNIT_ROWS + 4 * k
                        last = turn(banks[s][:, k * parts:(k + 1) * parts],
                                    n_x[0:parts, slot, r:r + 4, :].rearrange("p r f -> p (r f)"), parts)
                    last.then_inc(n_turned, 1)

                turn_rows(*units[0])
                for j, s, nr in units:
                    if j + 1 < len(units):
                        turn_rows(*units[j + 1])
                    u = c * D_UNITS + j
                    pe.wait_ge(n_xt, u + (1 + SLOTS))
                    pe.wait_ge(n_bank, u + 1)
                    for k in range(nr // 4):
                        for w in range(2):
                            last = nc.tensor.matmul(banks[2 + 2 * w + s][0:parts, k * P:(k + 1) * P],
                                                    n_xT[:, s, k * parts:(k + 1) * parts],
                                                    nodes_w[:, w * P:(w + 1) * P], start=True, stop=True)
                    last.then_inc(n_mm, 1)

            for first, last_pair, tail in NODE_PAIRS:
                node_chunks(pe, nodes, first, last_pair, tail)
                if not tail:
                    seam(32)
            seam(32)

            pe.sem_inc(e_turned, SLOTS)
            pe.sem_inc(e_h, SLOTS)
            pe.sem_inc(e_v, SLOTS)

            def turn_cat(q, slot):
                pe.wait_ge(e_cat, q + 1)
                pe.wait_ge(e_catd, q + 1)
                pe.wait_ge(e_catT, q + 1)
                for j in range(4):
                    last = turn(banks[slot][0:96, j * P:(j + 1) * P], cat[:, slot, j, :], P)
                last.then_inc(e_turned, 1)

            def first_product(q, slot):
                pe.wait_ge(e_catT, q + (1 + SLOTS))
                pe.wait_ge(e_hT, q + 1)
                nc.tensor.matmul(banks[2 + slot][0:HID0, :], mw1[:], catT[:, slot, :],
                                 start=True, stop=True).then_inc(e_h, 1)

            def second_product(q, slot):
                pe.wait_ge(e_hT, q + (1 + SLOTS))
                pe.wait_ge(e_vused, q * 4 + 4)
                for j in range(4):
                    last = nc.tensor.matmul(banks[4 + slot][:, j * FEAT:(j + 1) * FEAT],
                                            hidT2[:, slot, j * P:(j + 1) * P], mw2[:], start=True, stop=True)
                last.then_inc(e_v, 1)

            pipeline(pe, turn_cat, first_product, second_product)
            seam(32)
            seam(32)

            pe.sem_inc(a_turned, SLOTS)
            pe.sem_inc(a_mm, SLOTS)
            pe.sem_inc(res_mm, SLOTS)

            def turn_cat3(q, slot):
                pe.wait_ge(a_cat, q + 1)
                pe.wait_ge(a_catT, q + 1)
                for j in range(4):
                    last = turn(banks[slot][0:HF + 1, j * P:(j + 1) * P], cat3[:, slot, j, :], P)
                last.then_inc(a_turned, 1)

            def project(q, slot):
                pe.wait_ge(a_catT, q + (1 + SLOTS))
                pe.wait_ge(a_act, q + 1)
                pe.wait_ge(a_used, q + 1)
                for j in range(4):
                    last = nc.tensor.matmul(banks[2 + slot][:, j * P:(j + 1) * P],
                                            catT3[:, slot, j * P:(j + 1) * P], gw2[:], start=True, stop=True)
                last.then_inc(a_mm, 1)
                pe.wait_ge(res_used, q + 1)
                for j in range(4):
                    last = nc.tensor.matmul(banks[4 + slot][:, j * FEAT:(j + 1) * FEAT],
                                            catT3[:, slot, j * P:(j + 1) * P], gw3[:], start=True, stop=True)
                last.then_inc(res_mm, 1)

            pipeline(pe, turn_cat3, project)
            for _ in range(4):
                seam(2)

            def quads_of(c, first_bank):
                for k in range(GATHER_CHUNK // 4):
                    yield k, banks[first_bank + k // 4][:, (k % 4) * P:(k % 4 + 1) * P]

            def turn_messages(c):
                pe.wait_ge(msg_ready, c + 1)
                for k, to in quads_of(c, 2 * (c % SLOTS)):
                    t = c * GATHER_CHUNK + 4 * k
                    last = turn(to, A_msg[:, t:t + 4, :].rearrange("p t f -> p (t f)"), P)
                last.then_inc(msg_turned, 1)

            def message_product(c):
                pe.wait_ge(msg_T, c + 1)
                if c >= SLOTS:
                    pe.wait_ge(msg_out, c - 1)
                for k, to in quads_of(c, 4 + 2 * (c % SLOTS)):
                    last = nc.tensor.matmul(to, msgT[:, c % SLOTS, k * P:(k + 1) * P], gw1[:], start=True, stop=True)
                last.then_inc(msg_mm, 1)

            for c in range(CHUNKS):
                turn_messages(c)
                message_product(c)
            seam(32)

        @block.vector
        def _(v):
            ends_reg = []
            count = {"norm": 0, "seq": 0, "root": 0, "square": 0, "ends": 0, "turned": 0, "carry": 0}

            def step(ins):
                count["seq"] += 1
                ins.then_inc(dve_seq, 1)
                v.wait_ge(dve_seq, count["seq"])

            def done(ins, s, n):
                ins.then_inc(s, 1)
                v.wait_ge(s, n)

            def tt(o, a, b, op):
                return v.tensor_tensor(out=o, in0=a, in1=b, op=op)

            def ts(o, a, s1, op0, s2=None, op1=None):
                if op1 is None:
                    return v.tensor_scalar(o, a, s1, None, op0)
                return v.tensor_scalar(o, a, s1, s2, op0, op1)

            def stt(o, a, s, b, op0, op1):
                return v.scalar_tensor_tensor(out=o, in0=a, scalar=s, in1=b, op0=op0, op1=op1)

            def total(o, a, op=ALU.add):
                return v.tensor_reduce(out=o, in_=a, axis=AX, op=op)

            def root(ins):
                count["root"] += 1
                done(ins, var_ready, count["root"])
                v.wait_ge(std_ready, count["root"])
                step(v.reciprocal(std[:], std[:]))

            def norm_steps(a, make, finish, squares=A_sum, order=range(CHUNKS)):
                base = count["norm"] * CHUNKS
                count["norm"] += 1

                def center(i):
                    c = order[i]
                    step(make(c))
                    step(total(chunk(stat, c), chunk(a, c)))
                    step(ts(chunk(stat, c), chunk(stat, c), -1.0 / FEAT, ALU.mult))
                    tt(chunk(a, c), chunk(a, c), bcast(chunk(stat, c), FEAT), ALU.add).then_inc(f_centered, 1)

                def variance(i):
                    c = order[i]
                    v.wait_ge(f_squared, base + i + 1)
                    total(chunk(stat, c), chunk(squares, c)).then_inc(f_var, 1)

                def scale(i):
                    c = order[i]
                    v.wait_ge(f_std, base + i + 1)
                    step(v.reciprocal(chunk(std, c), chunk(std, c)))
                    finish(c, tt(chunk(a, c), chunk(a, c), bcast(chunk(std, c), FEAT), ALU.mult))

                return center, variance, scale

            def norm(a, make, finish):
                in_turn(*norm_steps(a, make, finish))

            def seam(to, width, state_row, carry_row, mask, op0, op1, first, back=False, columns=None):
                e = 0 if back else to.shape[1] - 1
                count["ends"] += 1
                done(v.tensor_copy(end_col[:, 0:width], to[:, e, :]), ends_ready, count["ends"])
                v.wait_ge(ends_turned, count["ends"])
                w = slice(0, width)
                flip = slice(None, None, -1) if back else slice(None)
                step(v.tensor_tensor_scan(out=seam_state[w, flip], data0=rows[w, state_row, flip],
                                          data1=banks[6][w, 0:P][:, flip], initial=first, op0=op0, op1=op1))
                edge = P - 1 if back else 0
                step(v.memset(seam_shift[w, edge:edge + 1], first))
                count["carry"] += 1
                if back:
                    ins = tt(seam_shift[w, 0:P - 1], seam_state[w, 1:P], rows[w, carry_row, 0:P - 1], op0)
                else:
                    ins = tt(seam_shift[w, 1:P], seam_state[w, 0:P - 1], rows[w, carry_row, 1:P], op0)
                done(ins, carry_ready, count["carry"])
                v.wait_ge(carry_turned, count["carry"])
                step(v.tensor_copy(carry[:, w], banks[7][:, w]))

                def add_carry(at):
                    for f in range(width):
                        last = stt(to[:, at, f], mask[:, at], carry[:, f:f + 1], to[:, at, f], op0, op1)
                    step(last)

                if columns:
                    return add_carry(columns)
                columns = to.shape[1]
                before_it = dict(count)
                with v.If(ends_reg[0] > ENDS):
                    add_carry(slice(0, columns))
                count.update(before_it)
                with v.Else():
                    add_carry(slice(columns - ENDS, columns) if back else slice(0, ENDS))

            def scan(to, of, mask, op0, op1, first, back=False):
                flip = slice(None, None, -1) if back else slice(None)
                for f in range(of.shape[2]):
                    last = v.tensor_tensor_scan(out=to[:, flip, f], data0=mask[:, 0:of.shape[1]][:, flip], data1=of[:, flip, f],
                                                initial=first, op0=op0, op1=op1)
                return last

            def sums(to, of):
                step(scan(to, of, same, ALU.mult, ALU.add, 0.0))
                seam(to, of.shape[2], 0, 1, in_first, ALU.mult, ALU.add, 0.0)

            def maxima(to, of):
                step(scan(to, of, same_pen, ALU.add, ALU.max, -BIG))
                seam(to, of.shape[2], 2, 3, in_first_pen, ALU.add, ALU.max, -BIG)

            def spread(to, of, tmp):
                step(tt(tmp[:], of[:], bcast(is_last[:], of.shape[2]), ALU.mult))
                step(scan(to, tmp, not_last, ALU.mult, ALU.add, 0.0, back=True))
                seam(to, of.shape[2], 4, 5, in_final, ALU.mult, ALU.add, 0.0, back=True)

            v.memset(A_dst[:], 0.0).then_inc(gather_ok, 1)
            v.wait_ge(pads_ready, 2)
            v.wait_ge(consts_ready, 1)
            v.wait_ge(loaded_dst, 64)
            step(v.tensor_copy(dst_f[:], dst_i[:]))
            step(v.tensor_copy(stat[:], nxt_i[:]))
            step(tt(is_last[:], dst_f[:], stat[:], ALU.not_equal))
            step(ts(not_last[:], is_last[:], -1.0, ALU.mult, 1.0, ALU.add))
            step(v.memset(same[:, 0:1], 0.0))
            step(tt(same[:, 1:T], dst_f[:, 1:T], dst_f[:, 0:T - 1], ALU.is_equal))
            step(ts(same_pen[:], same[:], -1.0, ALU.add, BIG, ALU.mult))
            step(ts(in_first[:], dst_f[:], dst_f[:, 0:1], ALU.is_equal))
            step(ts(in_first_pen[:], in_first[:], -1.0, ALU.add, BIG, ALU.mult))
            step(ts(stat[:], dst_f[:], float(N_NODES), ALU.is_lt))
            step(ts(in_final[:], dst_f[:], dst_f[:, T - 1:T], ALU.is_equal))
            step(tt(in_final[:], in_final[:], stat[:], ALU.mult))
            step(ts(stat[:], dst_f[:], float(-SKIP), ALU.add))
            step(tt(stat[:], stat[:], is_last[:], ALU.mult))
            step(ts(out_i[:], stat[:], float(SKIP), ALU.add))

            for k, e in enumerate((T - 1, 0)):
                count["ends"] += 1
                done(ts(diag[:], ident[:], dst_f[:, e:e + 1], ALU.mult), ends_ready, count["ends"])
                v.wait_ge(ends_turned, count["ends"])
                step(v.tensor_copy(rows[:, 6 + k, :], banks[6 + k][0:32, 0:P]))
            last_row, first_row = rows[:, 6, :], rows[:, 7, :]
            step(v.memset(rows[:, 0:6, :], 0.0))
            step(tt(rows[:, 0, 1:P], last_row[:, 0:P - 1], last_row[:, 1:P], ALU.is_equal))
            step(tt(rows[:, 1, 1:P], last_row[:, 0:P - 1], first_row[:, 1:P], ALU.is_equal))
            step(ts(rows[:, 2:4, :], rows[:, 0:2, :], -1.0, ALU.add, BIG, ALU.mult))
            step(tt(rows[:, 5, 0:P - 1], last_row[:, 0:P - 1], first_row[:, 1:P], ALU.is_equal))
            step(tt(rows[:, 4, :], last_row, first_row, ALU.is_equal))
            step(tt(rows[:, 4, :], rows[:, 4, :], rows[:, 5, :], ALU.mult))

            total(end_col[:, 2:3], in_first[:])
            step(total(end_col[:, 3:4], in_final[:]))
            count["ends"] += 1
            done(tt(end_col[:, 0:1], end_col[:, 2:3], end_col[:, 3:4], ALU.max), ends_ready, count["ends"])
            v.wait_ge(ends_turned, count["ends"])
            step(total(end_col[0:1, 1:2], banks[6][0:1, 0:P], ALU.max))
            step(v.tensor_copy(n_ends[:], end_col[0:1, 1:2]))
            ends_reg.append(v.value_load(n_ends[0:1, 0:1], min_val=0, max_val=T))

            degree, everywhere, one = (a[:].unsqueeze(2) for a in (r3, stat, dinv))
            step(v.memset(dinv[:], 1.0))
            sums(degree, one)
            spread(everywhere, degree, one)
            root(v.tensor_copy(deg, stat[:]))
            step(v.tensor_copy(dinv[:], std[:]))

            v.wait_ge(loaded_edges, 64)
            step(tt(rel_sq, rel_t, rel_t, ALU.mult))
            root(total(stat[:], rel_sq))
            for to, of in ((0, 1), (1, 2), (2, 0), (3, 1), (4, 2)):
                ins = tt(unit[:, :, to], rel_t[:, :, of], std[:], ALU.mult)
            step(ins)

            v.wait_ge(loaded_w, 16 * N_WEIGHT_LOADS)
            three = w2raw[:, 192:PATHS].rearrange("p (m k) -> p m k", k=3)
            fold = w2fold[:, 0:256].rearrange("p (j u t v) -> p j u t v", j=2, u=8, t=2)

            def uv(ap):
                return ap.rearrange("p (u v) -> p u v", u=8)

            ts(fold[:, 0, :, 0, :], uv(w2raw[:, 0:64]), NORM0 * Y0, ALU.mult)
            ts(fold[:, 0, :, 1, :], uv(w2raw[:, 64:128]), NORM0 * C1 / sqrt(3), ALU.mult)
            ts(fold[:, 1, :, 0, :], uv(w2raw[:, 128:192]), NORM1 * C1 / sqrt(3), ALU.mult)
            ts(fold[:, 1, :, 1, :], uv(three[:, :, 2]), NORM1 * K2, ALU.mult)
            ts(w2fold[:, 320:384], three[:, :, 1], NORM1 * K1, ALU.mult)
            step(ts(w2fold[:, 256:320], three[:, :, 2], -NORM1 * K2 / 3, ALU.mult))
            step(stt(w2fold[:, 256:320], three[:, :, 0], NORM1 * Y0 / sqrt(3), w2fold[:, 256:320], ALU.mult, ALU.add))
            step(tt(gw2[HF:HF + 1, HF:2 * HF], gw2[HF:HF + 1, HF:2 * HF], gtmp[HF:HF + 1, :], ALU.add))
            d = slice(32, 64)
            step(v.memset(gw3[:], 0.0))
            tt(gw3[d, :], gw1[d, d], ident[d, d], ALU.add)
            v.tensor_copy(gw3[HF:HF + 1, :], gb1[HF:HF + 1, :])
            step(v.memset(nodes_t[:], 0.0))
            for k in range(4):
                q = slice(32 * k, 32 * k + 32)
                ins = v.memset(nodes_t[q, q], 1.0 / FEAT)
            step(ins)
            step(tt(nodes_w[:, 0:P], ident[:], nodes_t[:], ALU.subtract))
            done(tt(nodes_t[:], ident[:], gw1[:], ALU.add), weights_folded, 1)
            v.wait_ge(cw_done, 1)
            done(v.tensor_copy(nodes_t[:], banks[4][:, 0:P]), weights_folded, 2)
            v.wait_ge(cw_done, 2)
            step(v.tensor_copy(nodes_w[:, P:2 * P], banks[5][:, 0:P]))
            step(total(end_col[:, 0:1], gb1[:]))
            step(ts(end_col[:, 0:1], end_col[:, 0:1], -1.0 / FEAT, ALU.mult))
            step(ts(gb1c[:], gb1[:], end_col[:, 0:1], ALU.add))

            step(ts(row_base[:], edge_no[:, 0:1], -1.0, ALU.add))
            step(ts(nxt_i[:], dst_i[:], LOG_LO, ALU.arith_shift_right))
            step(v.tensor_copy(hi_digit, nxt_i[:]))
            step(ts(nxt_i[:], dst_i[:], P - 1, ALU.bitwise_and))
            v.tensor_copy(lo_digit, nxt_i[:])
            done(ts(minus_lo, nxt_i[:], -1.0, ALU.mult), digits_ready, 1)

            with v.Fori(0, T // GATHER_CHUNK) as i:
                for k in range(HIST_UNITS):
                    slot = k % HIST_SLOTS
                    v.wait_ge(onehots_used, i * HIST_UNITS + (k + 1))
                    t = [bass.ds(i * GATHER_CHUNK + (2 * k + j), 1) for j in range(2)]
                    ts(lo_hot[:, 2 * slot, :], iota16[:, 0:P], lo_digit[:, t[0]], ALU.is_equal)
                    ts(hi_hot[:, 2 * slot, :], iota16, hi_digit[:, t[0]], ALU.is_equal)
                    ts(hi_hot[:, 2 * slot + 1, :], iota16, hi_digit[:, t[1]], ALU.is_equal).then_inc(onehots_ready, 1)

            halves = [slice(h * HI // 2, (h + 1) * HI // 2) for h in range(2)]
            v.wait_ge(counted, 1)
            v.memset(pos_spare, 1.0)
            v.tensor_copy(node_count[:, halves[0]], banks[6][:, 0:HI // 2])
            done(v.tensor_copy(node_count[:, halves[1]], banks[7][:, 0:HI // 2]), count_copied, 1)
            v.wait_ge(summed, 1)
            for h, at in enumerate(halves):
                before_h = pos_run[:, at.start - 1:at.start] if h else 0.0
                step(v.tensor_tensor_scan(out=pos_run[:, at], data0=pos_spare[:, at], data1=banks[4 + h][:, 0:HI // 2],
                                          initial=before_h, op0=ALU.mult, op1=ALU.add))
            step(ts(pos_spare, node_count, 0.0, ALU.is_equal, float(SKIP), ALU.mult))
            for h, at in enumerate(halves):
                step(tt(pos_run[:, at], pos_run[:, at], banks[4 + h][:, 0:HI // 2], ALU.subtract))
                step(tt(pos_run[:, at], pos_run[:, at], banks[2 + h][:, 0:HI // 2], ALU.add))
            done(stt(pos_f, pos_run, -1.0, pos_spare, ALU.add, ALU.add), pos_f_ready, 1)
            v.wait_ge(pos_turned, 1)
            v.tensor_copy(pos_int_t[:, 0:4, :].rearrange("p k l -> p (k l)"), banks[4][:, :])
            v.tensor_copy(pos_int_t[:, 4:6, :].rearrange("p k l -> p (k l)"), banks[5][:, 0:2 * P])
            done(v.tensor_copy(pos_int_t[0:HI - 6 * P, 6, :], banks[5][0:HI - 6 * P, 2 * P:3 * P]), pos_int, 1)

            def prepare(u_next, slot, t):
                v.wait_ge(pre_turned, u_next + 1)
                tt(pre[:, slot], mid(w1rep[:], 2), bcast(ew[:, bass.ds(t, 2)], HID0 + 1), ALU.mult).then_inc(pre_ready, 1)

            def scan1(to, of, mask, back=False):
                flip = slice(None, None, -1) if back else slice(None)
                return v.tensor_tensor_scan(out=to[:, flip], data0=mask[:, flip], data1=of[:, flip], initial=0.0,
                                            op0=ALU.mult, op1=ALU.add)

            def make_short():
                v.wait_ge(pos_rows, 16 * T)
                step(v.tensor_copy(spare[:, 0:T], pos_i[:]))
                step(ts(kept, spare[:, 0:T], SKIP / 2, ALU.is_lt))
                v.memset(kept[:, 0:1], 1.0)
                step(v.memset(kept[:, T - 1:T], 1.0))
                key = [keys[:, k, :] for k in range(3)]
                ts(key[0], left, 32768.0, ALU.mult, 32767.0, ALU.add)
                step(ts(spare[:, 0:T], spare[:, 0:T], 32767.0, ALU.min))
                step(tt(key[0], key[0], spare[:, 0:T], ALU.subtract))
                step(scan1(run, kept, same))
                step(ts(flag[:, 0:T], run, 1.0, ALU.is_equal))
                step(ts(key[1], deg, 2.0, ALU.mult))
                step(tt(key[1], key[1], flag[:, 0:T], ALU.add))
                step(stt(key[1], left, 65536.0, key[1], ALU.mult, ALU.add))
                step(v.memset(before[:, T - 1:T], 0.0))
                step(v.tensor_copy(before[:, 0:T - 1], same[:, 1:T]))
                step(ts(flag[:, 0:T], before, -1.0, ALU.mult, 1.0, ALU.add))
                step(ts(spare[:, 0:T], left, -1.0, ALU.mult, float(T), ALU.add))
                step(tt(flag[:, 0:T], flag[:, 0:T], spare[:, 0:T], ALU.mult))
                step(scan1(run_end, flag[:, 0:T], before, back=True))
                step(stt(key[2], left, 256.0, run_end, ALU.mult, ALU.add))
                step(tt(keys, keys, mid(kept, 3), ALU.mult))
                step(v.memset(before, 1.0))
                step(scan1(spare[:, 0:T], kept, before))
                step(ts(spare[:, 0:T], spare[:, 0:T], row_base[:], ALU.add, float(-1 - SKIP), ALU.add))
                step(ts(flag[:, 0:T], run, 0.0, ALU.is_gt))
                step(tt(spare[:, 0:T], spare[:, 0:T], flag[:, 0:T], ALU.mult))
                step(ts(short_row_i, spare[:, 0:T], float(SKIP), ALU.add))
                done(total(spare[:, 0:1], kept), count_ready, 1)
                v.wait_ge(count_turned, 1)
                step(total(spare[0:1, 8:9], banks[6][0:1, 0:P], ALU.max))
                step(v.tensor_copy(n_short[:], spare[0:1, 8:9]))
                n = v.value_load(n_short[0:1, 0:1], min_val=0, max_val=T)
                step(v.memset(top, 0.0))

                def take_top(r):
                    at = slice(8 * r, 8 * r + 8)
                    for k in range(3):
                        ins = v.max(out=top[:, k, at], in_=key[k])
                    step(ins)
                    for k in range(3):
                        ins = v.match_replace(out=key[k], in_to_replace=top[:, k, at], in_values=key[k], imm_value=0.0)
                    step(ins)

                for r in range(FEW // 8):
                    take_top(r)
                at = count["seq"]
                with v.If(n > FEW):
                    for r in range(FEW // 8, TOP // 8):
                        take_top(r)
                with v.Else():
                    v.sem_inc(dve_seq, count["seq"] - at)
                step(v.tensor_copy(top_i, top))
                own = slice(0, T)
                step(ts(keys[:, 0, :].bitcast(i32), top_i[:, 0, own], 32767, ALU.bitwise_and))
                ts(idx_short[:], keys[:, 0, :].bitcast(i32), -1.0, ALU.mult, 32767.0, ALU.add)
                step(ts(spare.bitcast(i32), top_i[:, 1, :], 1, ALU.bitwise_and))
                step(v.tensor_copy(flag, spare.bitcast(i32)))
                ts(same_short[:], flag[:, own], -1.0, ALU.mult, 1.0, ALU.add)
                step(scan1(run, flag[:, own], before))
                ts(in_first_short[:], run, 1.0, ALU.is_equal)
                step(ts(keys[:, 0, :].bitcast(i32), top_i[:, 1, own], 1, ALU.arith_shift_right))
                step(ts(keys[:, 0, :].bitcast(i32), keys[:, 0, :].bitcast(i32), 32767, ALU.bitwise_and))
                step(ts(dinv_short[:], keys[:, 0, :].bitcast(i32), 1.0, ALU.max))
                step(ts(kept, top[:, 2, own], 0.0, ALU.is_equal))
                step(v.memset(run_end, 1.0))
                step(tt(run_end[:, 0:T - 1], flag[:, 1:T], kept[:, 1:T], ALU.max))
                step(ts(kept, kept, -1.0, ALU.mult, 1.0, ALU.add))
                step(tt(run_end, run_end, kept, ALU.mult))
                step(ts(keys[:, 0, :].bitcast(i32), top_i[:, 2, own], 255, ALU.bitwise_and))
                step(ts(run, keys[:, 0, :].bitcast(i32), row_base[:], ALU.add, float(-SKIP), ALU.add))
                step(tt(run, run, run_end, ALU.mult))
                step(ts(out_short[:], run, float(SKIP), ALU.add))
                done(v.memset(idx_next[:], SKIP), short_ready, 1)

            prepare(0, 0, 0)
            prepare(1, 1, 2)
            v.sem_inc(radial_used, SLOTS)
            v.sem_inc(prod_used, SLOTS)
            for c in range(CHUNKS):
                v.wait_ge(src_rows[c], 16 * GATHER_CHUNK)
                cols = slice(c * GATHER_CHUNK, (c + 1) * GATHER_CHUNK)
                vec_in = A_src[:, cols, 8:32].rearrange("p t (v i) -> p t v i", i=3)
                n3 = unit[:, cols, 0:3].unsqueeze(2).to_broadcast([P, GATHER_CHUNK, 8, 3])
                a4 = vec_a.rearrange("p t (v i) -> p t v i", i=3)
                step(tt(a4, vec_in, n3, ALU.mult))
                v.tensor_copy(ff[:, :, 0:8], A_src[:, cols, 0:8])
                step(total(ff[:, :, 8:16], a4))
                with v.Fori(0, GATHER_CHUNK // 4) as i:
                    for slot in range(SLOTS):
                        u = i * 2 + (c * GATHER_CHUNK // 2 + slot)
                        t_in, t = i * 4 + 2 * slot, i * 4 + (c * GATHER_CHUNK + 2 * slot)
                        prepare(u + 2, slot, t + 4)
                        v.wait_ge(radial_ready, u + (1 + SLOTS))
                        v.wait_ge(prod_used, u + 1)
                        for j in range(2):
                            bank, to = banks[2 + 2 * slot + j], prod[:, 2 * slot + j, :]
                            tt(to[:, 0:256].rearrange("p (a b) -> p a b", b=16),
                               bank[:, 0:256].rearrange("p (a b) -> p a b", b=16),
                               ff[:, bass.ds(t_in + j, 1), :].to_broadcast([P, 16, 16]), ALU.mult)
                            vec = A_src[:, bass.ds(t + j, 1), 8:32].rearrange("p a (v i) -> p (a i) v", i=3)
                            last = tt(to[:, 256:640].rearrange("p (a i v) -> p a i v", i=3, v=8),
                                      bank[:, 256:384].rearrange("p (a v) -> p a v", v=8).unsqueeze(2)
                                      .to_broadcast([P, 16, 3, 8]),
                                      vec.unsqueeze(1).to_broadcast([P, 16, 3, 8]), ALU.mult)
                        last.then_inc(radial_used, 1)
                    for slot in range(SLOTS):
                        v.wait_ge(radial_used, i * 2 + (c * GATHER_CHUNK // 2 + slot + 1 + SLOTS))
                        at, mine = bass.ds(i * 4 + 2 * slot, 2), prod[:, 2 * slot:2 * slot + 2, :]
                        total(path_sums[:, at, 0:16], mine[:, :, 0:256].rearrange("p j (a b) -> p j a b", b=16))
                        last = total(path_sums[:, at, 16:64], mine[:, :, 256:640].rearrange("p j (a b) -> p j a b", b=8))
                        last.then_inc(prod_used, 1)
                v.wait_ge(prod_used, (c + 1) * GATHER_CHUNK // 2 + SLOTS)
                beta = path_sums[:, :, 16:40].rearrange("p t (u i) -> p t u i", i=3)
                gamma = path_sums[:, :, 40:64].rearrange("p t (u i) -> p t u i", i=3)

                def n_at(k):
                    return unit[:, cols, k:k + 3].unsqueeze(2).to_broadcast([P, GATHER_CHUNK, 8, 3])

                vec_out = A_msg[:, cols, 8:32].rearrange("p t (u i) -> p t u i", i=3)
                v.tensor_copy(A_msg[:, cols, 0:8], path_sums[:, :, 0:8])
                v.tensor_copy(g5[:, :, :, 0:3], gamma)
                step(v.tensor_copy(g5[:, :, :, 3:5], gamma[:, :, :, 0:2]))
                step(tt(a4, n_at(1), g5[:, :, :, 2:5], ALU.mult))
                step(tt(vec_out, beta, a4, ALU.add))
                step(tt(a4, n_at(2), g5[:, :, :, 1:4], ALU.mult))
                step(tt(vec_out, vec_out, a4, ALU.subtract))
                step(tt(a4, n_at(0), bcast(path_sums[:, :, 8:16], 3), ALU.mult))
                step(tt(vec_out, vec_out, a4, ALU.add))
                if c == SHORT_AFTER - 1:
                    make_short()

            v.wait_ge(short_stored, 16)
            sums(A_sum, A_msg)
            v.memset(A_msg[:], 0.0).then_inc(gather_ok, 1)
            v.wait_ge(pos_stored, 32)

            def first_table(c, ins):
                step(ins)
                tt(chunk(A_tmp, c), chunk(A_dst, c), bcast(chunk(dinv, c), FEAT), ALU.mult).then_inc(table_ready, 1)

            def add_layer0(c):
                v.wait_ge(dst_rows[c], 16 * GATHER_CHUNK)
                return tt(chunk(A_dst, c), chunk(A_dst, c), chunk(A_sum, c), ALU.add)

            norm(A_dst, add_layer0, first_table)

            v.wait_ge(table_ready, parts_until(0))
            step(ts(A_dst[:], A_dst[:], 1.25, ALU.mult))

            root(ts(stat[:], dinv_short[:], 1.0, ALU.mult))
            step(v.tensor_copy(dinv_short[:], std[:]))

            def nodes(c, half, slot, parts, n_rows):
                n_unit = len(node_units(slot, n_rows))

                def s(k):
                    return n_s[0:parts, 4 * slot + k, 0:n_rows]

                o, q = n_o[0:parts, slot, 0:n_rows, :], n_q[0:parts, slot, 0:n_rows, :]
                var, dev, r, tmp = s(0), s(1), s(2), s(3)

                def nroot(k, ins):
                    done(ins, n_var, c * 4 + k)
                    v.wait_ge(n_std, c * 4 + k)
                    nstep(v.reciprocal(tmp, dev))

                n_in = [0]

                def nstep(ins):
                    n_in[0] += 1
                    ins.then_inc(node_seq, 1)
                    v.wait_ge(node_seq, c * NODE_STEPS + n_in[0])

                v.wait_ge(n_bank, c * D_UNITS + (n_unit + SLOTS))
                nroot(1, total(var, q))
                nstep(v.tensor_copy(r, tmp))
                nstep(tt(var, var, tmp, ALU.mult))
                nroot(2, stt(var, var, 1.0 / FEAT, tmp, ALU.mult, ALU.mult))
                nstep(ts(tmp, tmp, 1.25, ALU.mult))
                nstep(tt(r, r, tmp, ALU.mult))
                nstep(tt(var, var, tmp, ALU.mult))
                nroot(3, tt(var, var, tmp, ALU.mult))
                nstep(stt(r, tmp, 2.0, r, ALU.mult, ALU.mult))
                nstep(tt(o, o, bcast(r, FEAT), ALU.mult))
                done(tt(o, o, mid(gb1c[0:parts], n_rows), ALU.add), n_z, c + 1)
                v.wait_ge(n_zsq, c + 1)
                nroot(4, total(var, q))
                assert n_in[0] == NODE_STEPS
                done(tt(o, o, bcast(tmp, FEAT), ALU.mult), n_out, c + 1)

            n = v.value_load(n_short[0:1, 0:1], min_val=0, max_val=T)

            def propagate(k, width):
                a_sum, a_msg, acc = A_sum[:, 0:width, :], A_msg[:, 0:width, :], A_tmp[:, 0:width, :]
                by = bcast(dinv_short[:, 0:width], FEAT)
                step(scan(a_sum, a_msg, same_short, ALU.mult, ALU.add, 0.0))
                if k < 2:
                    v.memset(a_msg, 0.0).then_inc(gather_ok, 1)
                seam(a_sum, FEAT, 0, 1, in_first_short, ALU.mult, ALU.add, 0.0)
                step(tt(a_sum, a_sum, by, ALU.mult))
                ins = tt(acc, acc, a_sum, ALU.add) if k else v.tensor_copy(acc, a_sum)
                if k < 2:
                    step(ins)
                    done(tt(a_sum, a_sum, by, ALU.mult), table_ready, parts_until(k + 1))
                else:
                    done(ins, acc_ready, 1)

            for k in range(3):
                node_chunks(v, nodes, *NODE_PAIRS[k])
                v.wait_ge(short_in, (1, 3, 4)[k])
                before_it = dict(count)
                with v.If(n > FEW):
                    propagate(k, T)
                count.update(before_it)
                with v.Else():
                    propagate(k, FEW)
            node_chunks(v, nodes, *NODE_PAIRS[3])

            step(total(stat[:], A_src[:]))
            step(ts(stat[:], stat[:], -1.0 / FEAT, ALU.mult))
            count["square"] += 1
            done(tt(A_src[:], A_src[:], bcast(stat[:], FEAT), ALU.add), centered, count["square"])
            v.wait_ge(squared, count["square"])
            root(total(stat[:], A_sum[:]))
            r1 = small[:, 0, :]
            step(v.tensor_copy(r1, std[:]))
            step(tt(stat[:], stat[:], std[:], ALU.mult))
            root(stt(stat[:], stat[:], 1.0 / FEAT, std[:], ALU.mult, ALU.mult))
            step(ts(std[:], std[:], 1.25, ALU.mult))
            step(tt(r1, r1, std[:], ALU.mult))
            step(tt(stat[:], stat[:], std[:], ALU.mult))
            root(tt(stat[:], stat[:], std[:], ALU.mult))
            step(ts(r3[:], std[:], 2.0, ALU.mult))
            done(tt(A_src[:], A_src[:], bcast(r1, FEAT), ALU.mult), gather_ok, 5)
            def add_layer1(c):
                v.wait_ge(sums_in[c], 16)
                return stt(chunk(A_dst, c), chunk(A_msg, c), 0.25, chunk(A_dst, c), ALU.mult, ALU.add)

            norm(A_dst, add_layer1, lambda c, ins: ins.then_inc(table_ready, 1))
            v.wait_ge(table_ready, parts_until(3))

            spread(A_sum, A_dst, A_msg)
            v.wait_ge(ea_in, 32)
            for slot in range(SLOTS):
                v.wait_ge(n_stored[slot], 16 * (D_CHUNKS // 2 + 1))
            step(v.memset(hidT2[HID0:HID0 + 1], 1.0))
            v.sem_inc(e_vused, 4 * SLOTS)

            def quad(a, q):
                return a[:, bass.ds(q * 4, 4), :]

            def bring_dst(q, slot):
                v.wait_ge(e_turned, q + 1)
                v.tensor_copy(cat[:, slot, :, 32:64], quad(A_sum, q))
                v.tensor_copy(cat[:, slot, :, 64:96], quad(A_tmp, q)).then_inc(e_catd, 1)

            def take(q, slot):
                rows_q = A_src[:, bass.ds(q * 4, 4), :]
                tt(rows_q, rows_q, bcast(r3[:, bass.ds(q * 4, 4)], FEAT), ALU.mult)
                v.wait_ge(e_v, q + (1 + SLOTS))
                for j in range(4):
                    v_j = banks[4 + slot][:, j * FEAT:(j + 1) * FEAT]
                    if j == 0 and isinstance(q, int) and q == 0:
                        ins = v.tensor_copy(A_sum[:, 0, :], v_j)
                    else:
                        at, prev = (bass.ds(q * 4 + k, 1) for k in (j, j - 1))
                        ins = stt(A_sum[:, at, :].rearrange("p a f -> p (a f)"),
                                  A_sum[:, prev, :].rearrange("p a f -> p (a f)"), same_pen[:, at], v_j,
                                  ALU.add, ALU.max)
                    done(ins, e_vused, q * 4 + (j + 1 + 4 * SLOTS))

            v.wait_ge(table_stored, 16 * parts_until(3))

            def add_layer2(c):
                step(tt(chunk(A_msg, c), chunk(A_sum, c), chunk(A_dst, c), ALU.max))
                return tt(chunk(A_dst, c), chunk(A_dst, c), chunk(A_msg, c), ALU.add)

            center, variance, scale = norm_steps(A_dst, add_layer2, lambda c, ins: ins.then_inc(table_ready, 1),
                                                 A_msg, LAST_ORDER)
            maxima_seam = (A_sum, FEAT, 2, 3, in_first_pen, ALU.add, ALU.max, -BIG)
            before_it = dict(count)
            seq_after = count["seq"] + 64
            with v.If(ends_reg[0] > ENDS):
                pipeline(v, bring_dst, None, None, take)
                seam(*maxima_seam, columns=slice(0, T))
                in_turn(center, variance, scale)
                v.sem_inc(dve_seq, seq_after - count["seq"])
            count.update(before_it)
            with v.Else():
                after = {}
                for c in range(1, CHUNKS - 1):
                    after[7 * c + 9] = [lambda i=c - 1: center(i)]
                    after[7 * c + 11] = [lambda i=c - 1: variance(i)]
                    after[7 * c + 12] = [lambda i=c - 1: scale(i)]
                pipeline(v, bring_dst, None, None, take, after=after)
                center(CHUNKS - 2)
                seam(*maxima_seam, columns=slice(0, ENDS))
                center(CHUNKS - 1)
                for i in (CHUNKS - 2, CHUNKS - 1):
                    variance(i)
                    scale(i)
                v.sem_inc(dve_seq, seq_after - count["seq"])
            count["seq"] = seq_after
            v.sem_inc(gather_ok, 1)
            v.wait_ge(table_ready, parts_until(4))

            spread(A_sum, A_dst, A_msg)
            step(v.memset(cat3[:, :, :, HF:HF + 1], 1.0))
            v.sem_inc(a_used, SLOTS)

            def bring_both(q, slot):
                v.wait_ge(a_turned, q + 1)
                v.wait_ge(quad_rows[1][slot], q * 32 + (64 - 32 * slot))
                v.tensor_copy(cat3[:, slot, :, 0:32], quad(A_src, q))
                v.tensor_copy(cat3[:, slot, :, 32:64], quad(A_sum, q)).then_inc(a_cat, 1)

            def score(q, slot):
                v.wait_ge(a_act, q + (1 + SLOTS))
                v.wait_ge(rf_in[slot], q * 16 + (32 - 16 * slot))
                en_rf = quad(work, q)
                tt(en_rf, banks[2 + slot][:].rearrange("p (t g) -> p t g", t=4)[:, :, 0:HF], rf[:, slot], ALU.mult)
                done(tt(leaky[:, slot], banks[2 + slot][:].rearrange("p (t g) -> p t g", t=4)[:, :, HF:2 * HF],
                        leaky[:, slot], ALU.max), a_leaky, q + 1)
                en_rf = en_rf.rearrange("p t (h f) -> p t h f", h=HEADS)
                total(quad(pair_b, q), en_rf, ALU.max)
                done(tt(leaky[:, slot], leaky[:, slot], mid(attn_rep[:], 4), ALU.mult), a_weighed, q + 1)
                tt(en_rf, en_rf, bcast(quad(pair_b, q), FEAT), ALU.subtract)
                total(quad(pair_a, q), leaky[:, slot].rearrange("p t (h f) -> p t h f", h=HEADS)).then_inc(a_used, 1)

            pipeline(v, bring_both, None, score)
            v.wait_ge(a_used, QUADS + SLOTS)

            maxima(pair_b, pair_a)
            spread(pair_c, pair_b, pair_d)
            done(tt(pair_c, pair_a, pair_c, ALU.subtract), exp_req, 1)
            v.wait_ge(exp_done, 1)
            sums(pair_b, pair_c)
            spread(pair_a, pair_b, pair_d)
            step(ts(pair_a, pair_a, 1e-9, ALU.max))
            step(v.reciprocal(pair_a, pair_a))
            step(tt(pair_c, pair_c, pair_a, ALU.mult))

            def weigh(c):
                at = slice(c * GATHER_CHUNK, (c + 1) * GATHER_CHUNK)
                rows_c = work[:, at, :].rearrange("p t (h f) -> p t h f", h=HEADS)
                tt(rows_c, rows_c, bcast(pair_c[:, at, :], FEAT), ALU.mult).then_inc(w_ready, 1)

            def normalise(c):
                v.wait_ge(w_exp, c + 1)
                at = slice(c * GATHER_CHUNK, (c + 1) * GATHER_CHUNK)
                rows_c = work[:, at, :].rearrange("p t (h f) -> p t h f", h=HEADS)
                step(total(pair_b[:, at, :], rows_c))
                step(v.reciprocal(pair_b[:, at, :], pair_b[:, at, :]))
                step(tt(rows_c, rows_c, bcast(pair_b[:, at, :], FEAT), ALU.mult))
                tt(A_msg[:, at, :], work[:, at, 0:FEAT], work[:, at, FEAT:HF], ALU.add).then_inc(msg_ready, 1)

            def scan_chunk(c):
                v.wait_ge(msg_out, c + 1)
                at = slice(c * GATHER_CHUNK, (c + 1) * GATHER_CHUNK)
                for f in range(FEAT):
                    so_far = A_sum[:, at.start - 1, f:f + 1] if c else 0.0
                    last = v.tensor_tensor_scan(out=A_sum[:, at, f], data0=same[:, at], data1=A_msg[:, at, f],
                                                initial=so_far, op0=ALU.mult, op1=ALU.add)
                step(last)

            center, variance, scale = norm_steps(
                A_tmp, lambda c: tt(chunk(A_tmp, c), chunk(A_sum, c), chunk(A_dst, c), ALU.add),
                lambda c, ins: ins.then_inc(final_ready, 1), A_msg, LAST_ORDER)
            message_seam = (A_sum, FEAT, 0, 1, in_first, ALU.mult, ALU.add, 0.0)
            before_it = dict(count)
            with v.If(ends_reg[0] > ENDS):
                in_turn(weigh, normalise)
                in_turn(scan_chunk)
                seam(*message_seam, columns=slice(0, T))
                in_turn(center, variance, scale)
            count.update(before_it)
            with v.Else():
                staggered((weigh, 0, CHUNKS), (normalise, 1, CHUNKS), (variance, 4, CHUNKS - 1),
                          (scan_chunk, 2, CHUNKS), (scale, 4, CHUNKS - 1), (center, 3, CHUNKS - 1))
                seam(*message_seam, columns=slice(0, ENDS))
                for part in (center, variance, scale):
                    part(CHUNKS - 1)


_INPUTS = ["x", "src", "dst", "edge_attr3_2x32", "edge_attr_3", "edge_attr_32", "edge_weight",
           "L0_gnn_w1", "L0_gnn_b1", "L0_gnn_w2", "L0_gnn_b2", "L2_gnn_W1", "L2_gnn_b1", "L2_gnn_W2", "L2_gnn_b2",
           "L3_gnn_W1", "L3_gnn_b1", "L3_gnn_W2s", "L3_gnn_b2s", "L3_gnn_W2d", "L3_gnn_b2d", "L3_gnn_attn"]


def kernel(**inputs):
    import numpy as np
    import concourse.bacc as bacc
    from concourse.bass_utils import run_bass_kernel_spmd

    nc = bacc.Bacc("TRN2", target_bir_lowering=False, num_devices=1)
    arrays, args = {}, []
    for name in _INPUTS:
        a = np.ascontiguousarray(inputs[name])
        arrays[f"in_{name}"] = a
        args.append(nc.dram_tensor(f"in_{name}", a.shape, mybir.dt.from_np(a.dtype), kind="ExternalInput").ap())
    out = nc.dram_tensor("out_0", (N_NODES, FEAT), mybir.dt.float32, kind="ExternalOutput").ap()
    gnn_kernel(nc, *args, out)
    return run_bass_kernel_spmd(nc, [arrays], core_ids=[0]).results[0]["out_0"]
```
